# Optimizing a Trainium2 kernel written in Bass

```python
import numpy as np
import jax
import jax.numpy as jnp

def _softmax(x, axis=-1):
    return jax.nn.softmax(x, axis=axis)

def _gelu(x):
    return jax.nn.gelu(x, approximate=True)

def _silu(x):
    return jax.nn.silu(x)

def _sigmoid(x):
    return jax.nn.sigmoid(x)

def _layernorm(x, axis=-1, eps=1e-05):
    m = jnp.mean(x, axis=axis, keepdims=True)
    v = jnp.var(x, axis=axis, keepdims=True)
    return (x - m) / jnp.sqrt(v + eps)

def _scatter_add(tgt, idx, src, axis=0):
    return tgt.at[idx].add(src)

def _segment_sum(src, seg, n):
    return jax.ops.segment_sum(src, seg, n)
kernel_name = 'mk_prb_d1_jaxref_r4_5d60d1'

def setup_inputs(seed: int=0):
    np.random.seed(seed)
    _w = jnp.asarray

    def _L0_attn_setup():
        import jax, jax.numpy as jnp
        import numpy as np
        B, T, D_MODEL = (4, 1024, 512)
        D_LATENT = 128
        D_COMP = 64
        THETA = 10000.0
        LN_EPS = 1e-05

        def _rope_tables(seq_len: int, dim: int):
            inv_freq = 1.0 / THETA ** (jnp.arange(0, dim, 2, dtype=jnp.float32) / dim)
            freqs = jnp.arange(seq_len, dtype=jnp.float32)[:, None] * inv_freq[None, :]
            cos = jnp.concatenate([jnp.cos(freqs), jnp.cos(freqs)], axis=-1)
            sin = jnp.concatenate([jnp.sin(freqs), jnp.sin(freqs)], axis=-1)
            return (cos, sin)

        def _rotate_half(x):
            x1, x2 = jnp.split(x, 2, axis=-1)
            return jnp.concatenate([-x2, x1], axis=-1)
        key = jax.random.key(seed)
        ks = jax.random.split(key, 8)
        s = 0.02
        return {'x': jax.random.normal(ks[0], (B, T, D_MODEL), dtype=jnp.float32), 'W_to_kv': jax.random.normal(ks[1], (D_LATENT, D_MODEL), dtype=jnp.float32) * s, 'W_compress': jax.random.normal(ks[2], (D_COMP, D_LATENT), dtype=jnp.float32) * s, 'ln_gamma': jnp.ones((D_COMP,), dtype=jnp.float32), 'ln_beta': jnp.zeros((D_COMP,), dtype=jnp.float32), 'W_q_comp': jax.random.normal(ks[3], (D_COMP, D_COMP), dtype=jnp.float32) * s, 'W_kv_comp': jax.random.normal(ks[4], (2 * D_COMP, D_COMP), dtype=jnp.float32) * s, 'W_comp2lat': jax.random.normal(ks[5], (D_LATENT, D_COMP), dtype=jnp.float32) * s, 'W_out_res': jnp.zeros((D_MODEL, D_LATENT), dtype=jnp.float32), 'b_out_res': jnp.zeros((D_MODEL,), dtype=jnp.float32)}
    _L0_attn_in = _L0_attn_setup()

    def _L0_ffn_setup():
        import jax, jax.numpy as jnp
        import numpy as np
        B, S, D = (2, 512, 512)
        E, TOP_K = (16, 2)
        F_EXP, F_SH = (256, 512)

        def _reference_tuple_inner(hidden_states, router_w, gate_w, up_w, down_w, shared_gate_w, shared_up_w, shared_down_w):
            b, s, d = hidden_states.shape
            flat = hidden_states.reshape(-1, d)
            T = flat.shape[0]
            router_logits = flat @ router_w.T
            probs = jax.nn.softmax(router_logits, axis=-1)
            topk_w, topk_idx = jax.lax.top_k(probs, TOP_K)
            topk_w = topk_w / jnp.sum(topk_w, axis=-1, keepdims=True)
            shared = jax.nn.silu(flat @ shared_gate_w) * (flat @ shared_up_w) @ shared_down_w
            flat_idx = topk_idx.reshape(-1)
            flat_w = topk_w.reshape(-1)
            token_ids = jnp.repeat(jnp.arange(T), TOP_K)
            order = jnp.argsort(flat_idx)
            sorted_tok = token_ids[order]
            sorted_w = flat_w[order]
            group_sizes = jnp.bincount(flat_idx, length=E).astype(jnp.int32)
            xs = flat[sorted_tok]
            g = jax.lax.ragged_dot(xs, gate_w, group_sizes)
            u = jax.lax.ragged_dot(xs, up_w, group_sizes)
            h = jax.nn.silu(g) * u
            dn = jax.lax.ragged_dot(h, down_w, group_sizes)
            routed = jnp.zeros_like(flat).at[sorted_tok].add(sorted_w[:, None] * dn)
            output = (shared + routed).reshape(b, s, d)
            return (output, router_logits)
        key = jax.random.key(seed)
        ks = jax.random.split(key, 8)
        scale = 0.02
        return {'hidden_states': jax.random.normal(ks[0], (B, S, D), jnp.float32), 'router_w': jax.random.normal(ks[1], (E, D), jnp.float32) * scale, 'gate_w': jax.random.normal(ks[2], (E, D, F_EXP), jnp.float32) * scale, 'up_w': jax.random.normal(ks[3], (E, D, F_EXP), jnp.float32) * scale, 'down_w': jax.random.normal(ks[4], (E, F_EXP, D), jnp.float32) * scale, 'shared_gate_w': jax.random.normal(ks[5], (D, F_SH), jnp.float32) * scale, 'shared_up_w': jax.random.normal(ks[6], (D, F_SH), jnp.float32) * scale, 'shared_down_w': jax.random.normal(ks[7], (F_SH, D), jnp.float32) * scale}
    _L0_ffn_in = _L0_ffn_setup()
    _d = {'L0_attn_x': _L0_attn_in['x'], 'L0_attn_W_to_kv': _L0_attn_in['W_to_kv'], 'L0_attn_W_compress': _L0_attn_in['W_compress'], 'L0_attn_ln_gamma': _L0_attn_in['ln_gamma'], 'L0_attn_ln_beta': _L0_attn_in['ln_beta'], 'L0_attn_W_q_comp': _L0_attn_in['W_q_comp'], 'L0_attn_W_kv_comp': _L0_attn_in['W_kv_comp'], 'L0_attn_W_comp2lat': _L0_attn_in['W_comp2lat'], 'L0_attn_W_out_res': _L0_attn_in['W_out_res'], 'L0_attn_b_out_res': _L0_attn_in['b_out_res'], 'L0_ffn_router_w': _L0_ffn_in['router_w'], 'L0_ffn_gate_w': _L0_ffn_in['gate_w'], 'L0_ffn_up_w': _L0_ffn_in['up_w'], 'L0_ffn_down_w': _L0_ffn_in['down_w'], 'L0_ffn_shared_gate_w': _L0_ffn_in['shared_gate_w'], 'L0_ffn_shared_up_w': _L0_ffn_in['shared_up_w'], 'L0_ffn_shared_down_w': _L0_ffn_in['shared_down_w']}
    _x0 = _d['L0_attn_x']
    _d['L0_attn_x'] = jax.random.normal(jax.random.fold_in(jax.random.key(seed), 1), (2, 4096, 512), dtype=_x0.dtype)
    del _x0
    return _d

def reference(L0_attn_x, L0_attn_W_to_kv, L0_attn_W_compress, L0_attn_ln_gamma, L0_attn_ln_beta, L0_attn_W_q_comp, L0_attn_W_kv_comp, L0_attn_W_comp2lat, L0_attn_W_out_res, L0_attn_b_out_res, L0_ffn_router_w, L0_ffn_gate_w, L0_ffn_up_w, L0_ffn_down_w, L0_ffn_shared_gate_w, L0_ffn_shared_up_w, L0_ffn_shared_down_w):

    def _L0_attn_ref(x, W_to_kv, W_compress, ln_gamma, ln_beta, W_q_comp, W_kv_comp, W_comp2lat, W_out_res, b_out_res):
        import jax, jax.numpy as jnp
        import numpy as np
        B, T, D_MODEL = (4, 1024, 512)
        D_LATENT = 128
        D_COMP = 64
        THETA = 10000.0
        LN_EPS = 1e-05

        def _rope_tables(seq_len: int, dim: int):
            inv_freq = 1.0 / THETA ** (jnp.arange(0, dim, 2, dtype=jnp.float32) / dim)
            freqs = jnp.arange(seq_len, dtype=jnp.float32)[:, None] * inv_freq[None, :]
            cos = jnp.concatenate([jnp.cos(freqs), jnp.cos(freqs)], axis=-1)
            sin = jnp.concatenate([jnp.sin(freqs), jnp.sin(freqs)], axis=-1)
            return (cos, sin)

        def _rotate_half(x):
            x1, x2 = jnp.split(x, 2, axis=-1)
            return jnp.concatenate([-x2, x1], axis=-1)
        Bx, Tx, _ = x.shape
        dc = W_compress.shape[0]
        kv_latent = x @ W_to_kv.T
        c = kv_latent @ W_compress.T
        mu = jnp.mean(c, axis=-1, keepdims=True)
        var = jnp.mean((c - mu) ** 2, axis=-1, keepdims=True)
        ch = (c - mu) * jax.lax.rsqrt(var + LN_EPS) * ln_gamma + ln_beta
        q = ch @ W_q_comp.T
        kv = ch @ W_kv_comp.T
        k, v = jnp.split(kv, 2, axis=-1)
        cos, sin = _rope_tables(Tx, dc)
        q = q * cos + _rotate_half(q) * sin
        k = k * cos + _rotate_half(k) * sin
        scale = 1.0 / jnp.sqrt(jnp.float32(dc))
        scores = jnp.einsum('btd,bsd->bts', q, k) * scale
        causal = jnp.tril(jnp.ones((Tx, Tx), dtype=bool))
        scores = jnp.where(causal[None], scores, jnp.float32(-1e+30))
        attn = jax.nn.softmax(scores, axis=-1)
        o = jnp.einsum('bts,bsd->btd', attn, v)
        z = o @ W_comp2lat.T
        out = z @ W_to_kv + z @ W_out_res.T + b_out_res
        return out

    def _L0_ffn_ref(hidden_states, router_w, gate_w, up_w, down_w, shared_gate_w, shared_up_w, shared_down_w):
        import jax, jax.numpy as jnp
        import numpy as np
        B, S, D = (2, 512, 512)
        E, TOP_K = (16, 2)
        F_EXP, F_SH = (256, 512)

        def _reference_tuple_inner(hidden_states, router_w, gate_w, up_w, down_w, shared_gate_w, shared_up_w, shared_down_w):
            b, s, d = hidden_states.shape
            flat = hidden_states.reshape(-1, d)
            T = flat.shape[0]
            router_logits = flat @ router_w.T
            probs = jax.nn.softmax(router_logits, axis=-1)
            topk_w, topk_idx = jax.lax.top_k(probs, TOP_K)
            topk_w = topk_w / jnp.sum(topk_w, axis=-1, keepdims=True)
            shared = jax.nn.silu(flat @ shared_gate_w) * (flat @ shared_up_w) @ shared_down_w
            flat_idx = topk_idx.reshape(-1)
            flat_w = topk_w.reshape(-1)
            token_ids = jnp.repeat(jnp.arange(T), TOP_K)
            order = jnp.argsort(flat_idx)
            sorted_tok = token_ids[order]
            sorted_w = flat_w[order]
            group_sizes = jnp.bincount(flat_idx, length=E).astype(jnp.int32)
            xs = flat[sorted_tok]
            g = jax.lax.ragged_dot(xs, gate_w, group_sizes)
            u = jax.lax.ragged_dot(xs, up_w, group_sizes)
            h = jax.nn.silu(g) * u
            dn = jax.lax.ragged_dot(h, down_w, group_sizes)
            routed = jnp.zeros_like(flat).at[sorted_tok].add(sorted_w[:, None] * dn)
            output = (shared + routed).reshape(b, s, d)
            return (output, router_logits)
        return _reference_tuple_inner(hidden_states, router_w, gate_w, up_w, down_w, shared_gate_w, shared_up_w, shared_down_w)[0]
    x = L0_attn_x
    xn = _layernorm(x, axis=-1)
    x = x + _L0_attn_ref(xn, L0_attn_W_to_kv, L0_attn_W_compress, L0_attn_ln_gamma, L0_attn_ln_beta, L0_attn_W_q_comp, L0_attn_W_kv_comp, L0_attn_W_comp2lat, L0_attn_W_out_res, L0_attn_b_out_res) + _L0_ffn_ref(xn, L0_ffn_router_w, L0_ffn_gate_w, L0_ffn_up_w, L0_ffn_down_w, L0_ffn_shared_gate_w, L0_ffn_shared_up_w, L0_ffn_shared_down_w)
    return x

_drawn_inputs = setup_inputs


def setup_inputs(seed=0):
    import zlib

    import numpy as np

    out = dict(_drawn_inputs(seed))
    spreads = {'L0_attn_ln_gamma': (1.0, 0.6),
     'L0_attn_ln_beta': (0.0, 0.8),
     'L0_attn_W_out_res': (0.0, 0.8),
     'L0_attn_b_out_res': (0.0, 2.0)}
    factors = {'L0_attn_W_to_kv': 8.0,
     'L0_attn_W_compress': 8.0,
     'L0_attn_W_q_comp': 8.0,
     'L0_attn_W_kv_comp': 8.0,
     'L0_attn_W_comp2lat': 8.0,
     'L0_ffn_router_w': 8.0,
     'L0_ffn_gate_w': 8.0,
     'L0_ffn_up_w': 8.0,
     'L0_ffn_down_w': 8.0,
     'L0_ffn_shared_gate_w': 8.0,
     'L0_ffn_shared_up_w': 8.0,
     'L0_ffn_shared_down_w': 8.0}
    for name, (base, spread) in spreads.items():
        noise = np.random.default_rng([zlib.crc32(name.encode()), seed]).standard_normal(out[name].shape)
        drawn = base * np.exp(spread * noise) if base else spread * noise
        out[name] = jnp.asarray(drawn.astype(out[name].dtype))
    for name, factor in factors.items():
        out[name] = (out[name] * factor).astype(out[name].dtype)
    return out
```

```python
from contextlib import ExitStack

import numpy as np
import concourse.bass as bass
from concourse import mybir

F32 = mybir.dt.float32
F32R = mybir.dt.float32r
BF16 = mybir.dt.bfloat16
I32 = mybir.dt.int32
ALU = mybir.AluOpType
ACT = mybir.ActivationFunctionType
AX = mybir.AxisListType

P = 128
B, T, D = 2, 4096, 512
N = B * T
E, FE, FS = 16, 256, 512
C = 64
LAT = 128
GT = 4
GROUP = GT * P
NG = N // GROUP
KD = D // P
FC = FS // P
RT = 256
NRT = 2 * N // RT + E
REGION = 2 * N
LIST = E * REGION + RT
LN_EPS = 1e-5
QB = T // GROUP
BIG = 3.0e38
NEG = -1.0e30
CA = C + 1


def after(eng, sem, value):
    if isinstance(value, int) and value <= 0:
        return
    eng.wait_ge(sem, value)


def hold(eng, gate):
    eng.sem_inc(gate, 1)


def build(nc, x, w_kv, w_compT, gamma, beta, w_qk, w_qk_swap, w_vT, w_c2l, w_outT, b_out, routerT,
          gate_w, up_w, down_w, sh_gate, sh_up, sh_down, rope, ident_in, tri_in, route_in, tile_in, upto_in, token_in, out):
    q_d = nc.dram_tensor("q_scratch", (C, N), F32, kind="Internal").ap()
    k_d = nc.dram_tensor("k_scratch", (C, N), F32, kind="Internal").ap()
    v_d = nc.dram_tensor("v_scratch", (NG, P, GT * CA), F32, kind="Internal").ap()
    base_d = nc.dram_tensor("base_scratch", (N, D), F32, kind="Internal").ap()
    xn_d = nc.dram_tensor("xn_scratch", (N, D), F32, kind="Internal").ap()
    list_d = nc.dram_tensor("token_list", (LIST, 1), I32, kind="Internal").ap()
    rows_out = nc.dram_tensor("rows_out", (NRT * RT, D), F32, kind="Internal").ap()

    with ExitStack() as ctx:
        keep = lambda name, shape, dt: ctx.enter_context(nc.sbuf_tensor(name, shape, dt))
        ident = keep("ident", [P, P], F32)
        slots_all = keep("slots_all", [P, NG * GT, 2], I32)
        gap_all = keep("gap_all", [P, NG * GT], F32)
        table = keep("table", [1, 2, NRT], I32)
        prepare(nc, x, w_kv, w_compT, gamma, beta, w_qk, w_qk_swap, w_vT, b_out, routerT, sh_gate, sh_up,
                sh_down, rope, ident_in, tri_in, route_in, tile_in, upto_in, token_in, q_d, k_d, v_d, base_d, xn_d, list_d,
                ident, slots_all, gap_all, table)
        routed(nc, gate_w, up_w, down_w, xn_d, list_d, rows_out, ident, table)
        attend(nc, w_kv, w_c2l, w_outT, tri_in, q_d, k_d, v_d, base_d, rows_out, out, ident, slots_all, gap_all)


def prepare(nc, x, w_kv, w_compT, gamma, beta, w_qk, w_qk_swap, w_vT, b_out, routerT, sh_gate, sh_up,
            sh_down, rope, ident_in, tri_in, route_in, tile_in, upto_in, token_in, q_d, k_d, v_d, base_d, xn_d, list_d,
            ident, slots_all, gap_all, table):
    ctx = ExitStack()
    with ctx:
        sb = lambda name, shape, dt=F32: ctx.enter_context(nc.sbuf_tensor(name, shape, dt))
        ps = lambda name: ctx.enter_context(nc.psum_tensor(name, [P, 512], F32))
        sem = lambda name: ctx.enter_context(nc.semaphore(name))

        wg = sb("wg", [P, KD, FS]); wu = sb("wu", [P, KD, FS]); wd = sb("wd", [P, FC, D])
        wcr = sb("wcr", [P, KD, C + E])
        wkv = sb("wkv", [P, D]); wcT = sb("wcT", [P, C])
        wqk = sb("wqk", [C, 2 * C]); wqks = sb("wqks", [C, 2 * C]); wv = sb("wv", [C, C])
        gam = sb("gam", [C, 1]); bet = sb("bet", [C, 1]); bias = sb("bias", [P, D])
        tri = sb("tri", [P, 2, P]); before = sb("before", [P, P], BF16); ones = sb("ones", [P, P], BF16)
        rt = sb("rt", [P, 5, E])
        tt = sb("tt", [1, NRT * E + NRT])
        upto = sb("upto", [P, E, E])
        halfs = sb("halfs", [P, GT])
        zeros = sb("zeros", [P, LIST // P], I32)
        token = sb("token", [P, NG * GT], I32)
        tok = [sb(f"tok_{i}", [P, GT], I32) for i in range(2)]
        x4 = [sb(f"x4_{i}", [P, GT, D]) for i in range(2)]
        xn4 = [sb(f"xn4_{i}", [P, GT, D]) for i in range(2)]
        xb4 = [sb(f"xb4_{i}", [P, GT, D]) for i in range(2)]
        xT = [sb(f"xT_{i}", [P, KD, GROUP]) for i in range(2)]
        cs = [sb(f"cs_{i}", [P, 2, GROUP]) for i in range(2)]
        h = sb("h", [P, FC, GROUP])
        sg = [sb(f"sg_{i}", [P, GROUP]) for i in range(2)]
        stx = sb("stx", [P, GT, 6]); mvx = sb("mvx", [P, GT, 2]); rsx = sb("rsx", [P, GT])
        stc = sb("stc", [P, GT, 6]); mvc = sb("mvc", [P, GT, 2]); rsc = sb("rsc", [P, GT])
        lc = sb("lc", [P, GT, C + E]); cn = sb("cn", [P, GT, C])
        top = sb("top", [P, 2, GT]); pick = sb("pick", [P, 2, GT])
        eq = sb("eq", [P, GT, E]); oh = sb("oh", [P, 2, GT, E]); rest = sb("rest", [P, GT, E])
        mask = sb("mask", [P, GT, E], BF16)
        pb = sb("pb", [P, GT, E]); pk = sb("pk", [P, 2, GT, E]); slotf = sb("slotf", [P, GT, 2])
        slot = [sb(f"slot_{i}", [P, GT, 2], I32) for i in range(2)]
        carry = sb("carry", [P, E])
        chT = sb("chT", [C, GROUP]); t1 = sb("t1", [P, GROUP]); t2 = sb("t2", [P, GROUP])
        qks = [sb(f"qks_{i}", [P, GROUP]) for i in range(2)]
        vs = [sb(f"vs_{i}", [P, GT, CA]) for i in range(2)]
        cnt = sb("cnt", [P, 6, E]); cnti = sb("cnti", [P, 2, E], I32)
        NS = NG * GT * 2
        se = sb("se", [P, NS]); sp_ = sb("sp_", [P, NS]); sei = sb("sei", [P, NS], I32)
        big = sb("big", [1, NRT, E]); big2 = sb("big2", [1, NRT, E]); small = sb("small", [1, 4, NRT])

        tb = [ps("tb0"), ps("tb1")]
        lb, nb = ps("lb"), ps("nb")
        gb = [ps(f"gb{i}") for i in range(4)]

        consts, x_in = sem("consts"), [sem("x_in0"), sem("x_in1")]
        setup, wc_done, wc_ev = sem("setup"), sem("wc_done"), sem("wc_ev")
        chain, pool_chain = sem("chain"), sem("pool_chain")
        mvx_done, rsx_done, xn_done, xb_done = sem("mvx_done"), sem("rsx_done"), sem("xn_done"), sem("xb_done")
        mvc_done, rsc_done, cn_done = sem("mvc_done"), sem("rsc_done"), sem("cn_done")
        t_done, t_ev, l_done, mask_done = sem("t_done"), sem("t_ev"), sem("l_done"), sem("mask_done")
        cT_done, ch_done, pos_done, pos_ev = sem("cT_done"), sem("ch_done"), sem("pos_done"), sem("pos_ev")
        qkv_done, qk_done, v_done, slot_done = sem("qkv_done"), sem("qk_done"), sem("v_done"), sem("slot_done")
        f_done, sg_done, h_done = sem("f_done"), sem("sg_done"), sem("h_done")
        d_done, d_ev = sem("d_done"), sem("d_ev")
        scattered = [sem("scattered0"), sem("scattered1")]
        st_qkv = [sem("st_qkv0"), sem("st_qkv1")]
        st_base = [sem("st_base0"), sem("st_base1")]
        rope_done = sem("rope_done")
        sp_gate = sem("sp_gate")
        dve_gate, pe_gate, pool_gate = sem("dve_gate"), sem("pe_gate"), sem("pool_gate")
        st_xn = [sem("st_xn0"), sem("st_xn1")]
        cleared = sem("cleared")

        loads = [(ident[:, :], ident_in), (wkv[:, :], w_kv), (wcT[:, :], w_compT),
                 (wcr[:, :, C:C + E], routerT.rearrange("(k p) e -> p k e", p=P)),
                 (tri[:, :, :], tri_in.rearrange("a p c -> p a c")), (rt[:, :, :], route_in),
                 (wqk[:, :], w_qk), (wqks[:, :], w_qk_swap), (wv[:, :], w_vT), (gam[:, :], gamma), (bet[:, :], beta),
                 (bias[:, :], b_out.partition_broadcast(P)),
                 (wg[:, :, :], sh_gate.rearrange("(k p) f -> p k f", p=P)),
                 (wu[:, :, :], sh_up.rearrange("(k p) f -> p k f", p=P)),
                 (wd[:, :, :], sh_down.rearrange("(k p) f -> p k f", p=P)),
                 (tt[:, :], tile_in), (upto[:, :, :], upto_in), (token[:, :], token_in)]
        CONSTS = 16 * len(loads)
        x_g = x.rearrange("(g j p) d -> g p j d", j=GT, p=P)
        base_g = base_d.rearrange("(g j p) d -> g p j d", j=GT, p=P)
        xn_g = xn_d.rearrange("(g j p) d -> g p j d", j=GT, p=P)
        rope_g = rope

        def pick_g(ap, n):
            return ap[n] if isinstance(n, int) else ap[bass.ds(n, 1)].rearrange("o p j d -> p (o j) d")

        def run(eng, first, step):
            first()
            step(None, 0, 0)
            step(0, 1, 1)
            step(1, 2, 0)
            with eng.Fori(1, NG // 2 - 1) as i:
                step(2 * i, 2 * i + 1, 1)
                step(2 * i + 1, 2 * i + 2, 0)
            step(NG - 2, NG - 1, 1)
            step(NG - 1, None, 0)

        block = ctx.enter_context(nc.Block())

        def times(n, q):
            return 8 * (n - q)

        @block.sync
        def _(sp):
            def load(n, q):
                after(sp, xn_done, n - 1)
                after(sp, xb_done, n - 1)
                after(sp, qk_done, n - 1)
                hold(sp, sp_gate)
                sp.dma_start(x4[q][:, :, :], pick_g(x_g, n)).then_inc(x_in[q], 16)
                sp.dma_start(cs[q][:, :, :], pick_g(rope_g, n)).then_inc(x_in[q], 16)

            def first():
                load(0, 0)
                for dst, src in loads:
                    sp.dma_start(dst, src).then_inc(consts, 16)
                sp.wait_ge(setup, 1)
                sp.dma_start(list_d.rearrange("(p a) o -> p (a o)", p=P), zeros[:, :]).then_inc(cleared, 16)
                store_xn(0, 0)

            def store_xn(n, q):
                sp.wait_ge(xn_done, n + 1)
                hold(sp, sp_gate)
                sp.dma_start(pick_g(xn_g, n), xn4[q][:, :, :]).then_inc(st_xn[q], 16)

            def step(s, n, q):
                if n is not None:
                    if not (isinstance(n, int) and n == NG - 1):
                        load(n + 1, 1 - q)
                    store_qkv(n, q)
                    if not (isinstance(n, int) and n == NG - 1):
                        store_xn(n + 1, 1 - q)
                if s is not None:
                    sp.wait_ge(d_ev, 4 * s + 4)
                    hold(sp, sp_gate)
                    sp.dma_start(pick_g(base_g, s), xb4[1 - q][:, :, :]).then_inc(st_base[1 - q], 16)

            def store_qkv(n, q):
                sp.wait_ge(qk_done, n + 1)
                sp.wait_ge(v_done, n + 1)
                hold(sp, sp_gate)
                cols = slice(n * GROUP, (n + 1) * GROUP) if isinstance(n, int) else bass.ds(n * GROUP, GROUP)
                sp.dma_start(q_d[:, cols], qks[q][0:C, :]).then_inc(st_qkv[q], 16)
                sp.dma_start(k_d[:, cols], qks[q][C:2 * C, :]).then_inc(st_qkv[q], 16)
                vdst = v_d[n] if isinstance(n, int) else v_d[bass.ds(n, 1)].rearrange("o p c -> (o p) c")
                sp.dma_start(vdst, vs[q][:, :, :].rearrange("p j c -> p (j c)")).then_inc(st_qkv[q], 16)

            run(sp, first, step)
            for q in range(2):
                sp.wait_ge(st_qkv[q], 48 * NG // 2)
                sp.wait_ge(st_base[q], 16 * NG // 2)
                sp.wait_ge(st_xn[q], 16 * NG // 2)

        @block.tensor
        def _(pe):
            def shared_gu(s, q, f):
                t = 4 * s + f
                if f >= 2:
                    pe.wait_ge(h_done, t - 1)
                else:
                    after(pe, d_ev, 4 * s - 2 + 2 * f)
                if f == 0:
                    pe.wait_ge(t_ev, 4 * s + 4)
                g, u = gb[2 * (f % 2)], gb[2 * (f % 2) + 1]
                for dst, w in ((g, wg), (u, wu)):
                    for k in range(KD):
                        mm = pe.matmul(dst[:, :], w[:, k, f * P:(f + 1) * P], xT[q][:, k, :],
                                       start=(k == 0), stop=(k == KD - 1))
                mm.then_inc(f_done, 1)

            def shared_down(s, j):
                if j == 0:
                    pe.wait_ge(h_done, 4 * s + 4)
                for k in range(FC):
                    mm = pe.matmul(gb[j][:, :], h[:, k, j * P:(j + 1) * P], wd[:, k, :],
                                   start=(k == 0), stop=(k == FC - 1))
                mm.then_inc(d_done, 1)

            def turn(n, q):
                pe.wait_ge(xn_done, n + 1)
                after(pe, qk_done, n)
                for j in range(GT):
                    after(pe, t_ev, 4 * n + j - 1)
                    for k in range(KD):
                        mm = pe.transpose(tb[j % 2][:, k * P:(k + 1) * P], xn4[q][:, j, k * P:(k + 1) * P], ident[:, :])
                    mm.then_inc(t_done, 1)

            def logits(n, q):
                pe.wait_ge(t_ev, 4 * n + 4)
                after(pe, v_done, n)
                for j in range(GT):
                    for k in range(KD):
                        mm = pe.matmul(lb[:, j * (C + E):(j + 1) * (C + E)], xT[q][:, k, j * P:(j + 1) * P],
                                       wcr[:, k, :], start=(k == 0), stop=(k == KD - 1))
                mm.then_inc(l_done, 1)

            def turn_c(n):
                pe.wait_ge(cn_done, n + 1)
                hold(pe, pe_gate)
                for j in range(GT):
                    mm = pe.transpose(nb[0:C, j * P:(j + 1) * P], cn[:, j, :], ident[:, :])
                mm.then_inc(cT_done, 1)

            def positions(n):
                pe.wait_ge(mask_done, n + 1)
                for j in range(GT):
                    for i in range(j + 1):
                        pe.matmul(lb[:, j * E:(j + 1) * E], (before if i == j else ones)[:, :], mask[:, i, :],
                                  start=(i == 0), stop=(i == j))
                for i in range(GT):
                    mm = pe.matmul(lb[:, GT * E:(GT + 1) * E], ones[:, :], mask[:, i, :], start=(i == 0), stop=(i == GT - 1))
                mm.then_inc(pos_done, 1)

            def qkv(n):
                pe.wait_ge(ch_done, n + 1)
                pe.matmul(nb[:, :], wqk[:, :], chT[:, :], start=True, stop=True)
                pe.matmul(tb[0][:, :], wqks[:, :], chT[:, :], start=True, stop=True)
                pe.wait_ge(pos_ev, n + 1)
                for j in range(GT):
                    mm = pe.matmul(lb[:, j * C:(j + 1) * C], chT[:, j * P:(j + 1) * P], wv[:, :], start=True, stop=True)
                mm.then_inc(qkv_done, 1)

            def first():
                pe.wait_ge(consts, CONSTS)
                for k in range(KD):
                    mm = pe.matmul(nb[:, k * C:(k + 1) * C], wkv[:, k * P:(k + 1) * P], wcT[:, :], start=True, stop=True)
                mm.then_inc(wc_done, 1)
                pe.wait_ge(wc_ev, 1)
                pe.wait_ge(setup, 1)

            def step(s, n, q):
                if s is not None:
                    shared_gu(s, 1 - q, 0)
                if n is not None:
                    turn(n, q)
                if s is not None:
                    shared_gu(s, 1 - q, 1)
                if n is not None:
                    logits(n, q)
                if s is not None:
                    shared_gu(s, 1 - q, 2)
                if n is not None:
                    turn_c(n)
                    positions(n)
                if s is not None:
                    shared_gu(s, 1 - q, 3)
                if n is not None:
                    qkv(n)
                if s is not None:
                    for j in range(GT):
                        shared_down(s, j)

            run(pe, first, step)

        @block.scalar
        def _(act):
            def silu(s, f):
                t = 4 * s + f
                act.wait_ge(f_done, t + 1)
                after(act, h_done, t - 1)
                act.activation(sg[f % 2][:, :], gb[2 * (f % 2)][:, :], ACT.Silu).then_inc(sg_done, 1)

            def step(s, n, q):
                if s is not None:
                    silu(s, 0)
                if n is not None:
                    for j in range(GT):
                        act.wait_ge(t_done, 4 * n + j + 1)
                        act.copy(xT[q][:, :, j * P:(j + 1) * P],
                                 tb[j % 2][:, :].rearrange("p (k t) -> p k t", k=KD)).then_inc(t_ev, 1)
                if s is not None:
                    for f in range(1, FC):
                        silu(s, f)

            run(act, lambda: None, step)

        @block.vector
        def _(dve):
            LINKS = 18

            def linked(n, k):
                dve.wait_ge(chain, n * LINKS + k)

            def norm(n, q):
                dve.wait_ge(x_in[q], times(n, q) * 2 + 32)
                for j in range(GT):
                    i = dve.bn_stats(stx[:, j, :], x4[q][:, j, :])
                i.then_inc(chain, 1)
                linked(n, 1)
                hold(dve, dve_gate)
                for j in range(GT):
                    i = dve.bn_aggr(mvx[:, j, :], stx[:, j, :])
                i.then_inc(mvx_done, 1)
                after(dve, st_xn[q], times(n, q))
                dve.wait_ge(rsx_done, n + 1)
                for j in range(GT):
                    i = dve.tensor_scalar(xn4[q][:, j, :], x4[q][:, j, :], mvx[:, j, 0:1], rsx[:, j:j + 1],
                                          ALU.subtract, ALU.mult)
                i.then_inc(xn_done, 1)

            def compressed(n):
                dve.wait_ge(l_done, n + 1)
                dve.tensor_copy(lc[:, :, :], lb[:, 0:GT * (C + E)].rearrange("p (j c) -> p j c", j=GT)).then_inc(chain, 1)
                linked(n, 2)
                for j in range(GT):
                    i = dve.bn_stats(stc[:, j, :], lc[:, j, 0:C])
                i.then_inc(chain, 1)
                linked(n, 3)
                hold(dve, dve_gate)
                for j in range(GT):
                    i = dve.bn_aggr(mvc[:, j, :], stc[:, j, :])
                i.then_inc(mvc_done, 1)

            def choose(n):
                rev = rt[:, 0:GT, :]
                lg = lc[:, :, C:C + E]
                wide = lambda ap: ap.unsqueeze(2).broadcast_to([P, GT, E])
                for c in range(2):
                    src = lg if c == 0 else rest[:, :, :]
                    o = 3 + 6 * c
                    dve.tensor_reduce(top[:, c, :], src, AX.X, ALU.max).then_inc(chain, 1)
                    linked(n, o + 1)
                    dve.tensor_tensor(eq[:, :, :], src, wide(top[:, c, :]), ALU.is_equal).then_inc(chain, 1)
                    linked(n, o + 2)
                    dve.tensor_tensor(pb[:, :, :], eq[:, :, :], rev, ALU.mult).then_inc(chain, 1)
                    linked(n, o + 3)
                    dve.tensor_reduce(pick[:, c, :], pb[:, :, :], AX.X, ALU.max).then_inc(chain, 1)
                    linked(n, o + 4)
                    dve.tensor_tensor(oh[:, c, :, :], rev, wide(pick[:, c, :]), ALU.is_equal).then_inc(chain, 1)
                    linked(n, o + 5)
                    if c == 0:
                        dve.scalar_tensor_tensor(out=rest[:, :, :], in0=oh[:, 0, :, :], scalar=-BIG, in1=lg,
                                                 op0=ALU.mult, op1=ALU.add).then_inc(chain, 1)
                        linked(n, 9)

            def mask_and_gap(n):
                after(dve, pos_done, n)
                dve.tensor_tensor(mask[:, :, :], oh[:, 0, :, :], oh[:, 1, :, :], ALU.add).then_inc(mask_done, 1)
                at = slice(n * GT, (n + 1) * GT) if isinstance(n, int) else bass.ds(n * GT, GT)
                dve.tensor_tensor(gap_all[:, at], top[:, 1, :], top[:, 0, :], ALU.subtract).then_inc(chain, 1)

            def normed(n):
                dve.wait_ge(rsc_done, n + 1)
                for j in range(GT):
                    i = dve.tensor_scalar(cn[:, j, :], lc[:, j, 0:C], mvc[:, j, 0:1], rsc[:, j:j + 1],
                                          ALU.subtract, ALU.mult)
                i.then_inc(cn_done, 1)

            def scaled(n):
                dve.wait_ge(cT_done, n + 1)
                dve.tensor_scalar(chT[:, :], nb[0:C, :], gam[:, 0:1], bet[:, 0:1], ALU.mult, ALU.add).then_inc(ch_done, 1)

            def slots(n, q):
                dve.wait_ge(pos_done, n + 1)
                dve.tensor_tensor(pb[:, :, :], lb[:, 0:GT * E].rearrange("p (j e) -> p j e", e=E),
                                  carry[:, :].unsqueeze(1).broadcast_to([P, GT, E]), ALU.add).then_inc(chain, 1)
                linked(n, 16)
                dve.tensor_tensor(carry[:, :], lb[:, GT * E:(GT + 1) * E], carry[:, :], ALU.add).then_inc(pos_ev, 1)
                for c in range(2):
                    i = dve.tensor_tensor(pk[:, c, :, :], oh[:, c, :, :], pb[:, :, :], ALU.mult)
                i.then_inc(chain, 1)
                linked(n, 17)
                for c in range(2):
                    i = dve.tensor_reduce(slotf[:, :, c], pk[:, c, :, :], AX.X, ALU.add)
                i.then_inc(chain, 1)
                linked(n, 18)
                after(dve, scattered[q], times(n, q) * 8)
                at = slice(n * GT, (n + 1) * GT) if isinstance(n, int) else bass.ds(n * GT, GT)
                dve.tensor_copy(tok[q][:, :], token[:, at])
                dve.tensor_copy(slot[q][:, :, :], slotf[:, :, :]).then_inc(slot_done, 1)
                dve.tensor_copy(slots_all[:, at, :], slotf[:, :, :])

            def roped(n, q):
                dve.wait_ge(qkv_done, n + 1)
                dve.tensor_tensor(t1[:, :], nb[:, :], cs[q][:, 0, :], ALU.mult)
                dve.tensor_tensor(t2[:, :], tb[0][:, :], cs[q][:, 1, :], ALU.mult).then_inc(rope_done, 1)
                after(dve, st_qkv[q], times(n, q) * 3)
                dve.tensor_copy(vs[q][:, :, 0:C], lb[:, 0:GT * C].rearrange("p (j c) -> p j c", j=GT)).then_inc(v_done, 1)
                dve.wait_ge(rope_done, n + 1)
                dve.tensor_tensor(qks[q][:, :], t1[:, :], t2[:, :], ALU.add).then_inc(qk_done, 1)

            def hidden(s, f):
                t = 4 * s + f
                dve.wait_ge(sg_done, t + 1)
                if f == 0:
                    after(dve, d_done, 4 * s)
                dve.tensor_tensor(h[:, f, :], gb[2 * (f % 2) + 1][:, :], sg[f % 2][:, :], ALU.mult).then_inc(h_done, 1)

            def added(s, q, j):
                if j == 0:
                    dve.wait_ge(xb_done, s + 1)
                dve.wait_ge(d_done, 4 * s + j + 1)
                dve.tensor_tensor(xb4[q][:, j, :], gb[j][:, :], xb4[q][:, j, :], ALU.add).then_inc(d_ev, 1)

            def first():
                dve.wait_ge(consts, CONSTS)
                dve.tensor_copy(before[:, :], tri[:, 0, :])
                dve.tensor_copy(carry[:, :], rt[:, GT, :])
                dve.memset(ones[:, :], 1.0)
                dve.memset(zeros[:, :], 0)
                dve.memset(halfs[:, :], -0.5)
                dve.memset(vs[0][:, :, C:CA], 1.0)
                dve.memset(vs[1][:, :, C:CA], 1.0).then_inc(setup, 1)
                dve.wait_ge(wc_done, 1)
                dve.tensor_copy(wcr[:, :, 0:C], nb[:, 0:KD * C].rearrange("p (k c) -> p k c", k=KD)).then_inc(wc_ev, 1)
                norm(0, 0)

            def step(s, n, q):
                if s is not None:
                    hidden(s, 0)
                    hidden(s, 1)
                if n is not None:
                    compressed(n)
                    choose(n)
                    mask_and_gap(n)
                    normed(n)
                if s is not None:
                    hidden(s, 2)
                if n is not None:
                    scaled(n)
                if s is not None:
                    hidden(s, 3)
                if n is not None:
                    slots(n, q)
                    roped(n, q)
                if s is not None:
                    added(s, 1 - q, 0)
                    added(s, 1 - q, 1)
                if n is not None and not (isinstance(n, int) and n == NG - 1):
                    norm(n + 1, 1 - q)
                if s is not None:
                    added(s, 1 - q, 2)
                    added(s, 1 - q, 3)

            run(dve, first, step)

            links = [NG * LINKS]

            def link(i):
                links[0] += 1
                i.then_inc(chain, 1)
                dve.wait_ge(chain, links[0])

            tile_e = tt[:, 0:NRT * E].rearrange("p (t e) -> p t e", e=E)
            tile_1 = tt[:, NRT * E:]
            dve.wait_ge(pos_ev, NG)
            link(dve.tensor_tensor(cnt[:, 0, :], carry[:, :], rt[:, GT, :], ALU.subtract))
            link(dve.tensor_scalar(cnt[:, 1, :], cnt[:, 0, :], float(RT - 1), None, ALU.add))
            link(dve.tensor_copy(cnti[:, 0, :], cnt[:, 1, :]))
            link(dve.tensor_scalar(cnti[:, 1, :], cnti[:, 0, :], RT.bit_length() - 1, None, ALU.logical_shift_right))
            link(dve.tensor_copy(cnt[:, 2, :], cnti[:, 1, :]))
            tiles_b = lambda p, n: cnt[0:p, 2, :].unsqueeze(1).broadcast_to([p, n, E])
            tri_b = x4[1][:, :, :].rearrange("p a b -> p (a b)")[:, 0:E * E].rearrange("p (a b) -> p a b", b=E)
            link(dve.tensor_tensor(tri_b, upto[:, :, :], tiles_b(P, E), ALU.mult))
            link(dve.tensor_reduce(cnt[:, 3, :], tri_b, AX.X, ALU.add))
            link(dve.tensor_tensor(cnt[:, 4, :], cnt[:, 3, :], cnt[:, 2, :], ALU.subtract))
            link(dve.tensor_scalar(cnt[:, 5, :], cnt[:, 4, :], float(RT), None, ALU.mult))

            slots = slots_all[:, :, :].rearrange("p t c -> p (t c)")
            link(dve.tensor_scalar(sei[:, :], slots, REGION.bit_length() - 1, None, ALU.logical_shift_right))
            link(dve.tensor_copy(se[:, :], sei[:, :]))
            link(dve.scalar_tensor_tensor(out=sp_[:, :], in0=se[:, :], scalar=-float(REGION), in1=slots,
                                          op0=ALU.mult, op1=ALU.add))
            hot = x4[0][:, :, :].rearrange("p a b -> p (a b)").rearrange("p (s e) -> p s e", e=E)
            rev_b = rt[:, 0, :].unsqueeze(1).broadcast_to([P, NS, E])
            link(dve.tensor_scalar(se[:, :], se[:, :], -1.0, float(E), ALU.mult, ALU.add))
            link(dve.tensor_tensor(hot, se[:, :].unsqueeze(2).broadcast_to([P, NS, E]), rev_b, ALU.is_equal))
            link(dve.tensor_tensor(hot, hot, cnt[:, 5, :].unsqueeze(1).broadcast_to([P, NS, E]), ALU.mult))
            link(dve.tensor_reduce(se[:, :], hot, AX.X, ALU.add))
            link(dve.tensor_tensor(slots, se[:, :], sp_[:, :], ALU.add))

            link(dve.tensor_tensor(big[:, :, :], tile_e, cnt[0:1, 3, :].unsqueeze(1).broadcast_to([1, NRT, E]), ALU.is_ge))
            link(dve.tensor_reduce(small[:, 0, :], big[:, :, :], AX.X, ALU.add))
            link(dve.tensor_tensor(big2[:, :, :], big[:, :, :], tiles_b(1, NRT), ALU.mult))
            link(dve.tensor_reduce(small[:, 1, :], big2[:, :, :], AX.X, ALU.add))
            link(dve.tensor_tensor(small[:, 2, :], tile_1, small[:, 1, :], ALU.subtract))
            link(dve.tensor_scalar(small[:, 2, :], small[:, 2, :], float(RT), None, ALU.mult))
            link(dve.scalar_tensor_tensor(out=small[:, 3, :], in0=small[:, 0, :], scalar=float(REGION),
                                          in1=small[:, 2, :], op0=ALU.mult, op1=ALU.add))
            link(dve.tensor_scalar(small[:, 1, :], small[:, 3, :], float(E * REGION), None, ALU.min))
            link(dve.tensor_copy(table[:, 0, :], small[:, 1, :]))
            link(dve.tensor_scalar(small[:, 0, :], small[:, 0, :], float(E - 1), None, ALU.min))
            link(dve.tensor_copy(table[:, 1, :], small[:, 0, :]))

        @block.gpsimd
        def _(pool):
            def root(n, per, mv, rs, waited, done):
                pool.wait_ge(waited, n + 1)
                hold(pool, pool_gate)
                pool.tensor_scalar(rs[:, :], mv[:, :, 1], LN_EPS, None, ALU.add).then_inc(pool_chain, 1)
                pool.wait_ge(pool_chain, 2 * n + 1 + per)
                pool.tensor_tensor(rs[:, :], rs[:, :], halfs[:, :], ALU.pow).then_inc(done, 1)

            def norm(n, q):
                root(n, 0, mvx, rsx, mvx_done, rsx_done)
                after(pool, st_base[q], times(n, q))
                for j in range(GT):
                    i = pool.tensor_tensor(xb4[q][:, j, :], x4[q][:, j, :], bias[:, :], ALU.add)
                i.then_inc(xb_done, 1)

            def first():
                pool.wait_ge(setup, 1)
                norm(0, 0)

            def step(s, n, q):
                if n is None:
                    return
                root(n, 1, mvc, rsc, mvc_done, rsc_done)
                pool.wait_ge(slot_done, n + 1)
                pool.wait_ge(cleared, 16)
                hold(pool, pool_gate)
                for j in range(GT):
                    for c in range(2):
                        pool.indirect_dma_start(list_d[:, :], bass.IndirectOffsetOnAxis(ap=slot[q][:, j, c:c + 1], axis=0),
                                                tok[q][:, j:j + 1], None).then_inc(scattered[q], 16)
                if not (isinstance(n, int) and n == NG - 1):
                    norm(n + 1, 1 - q)

            run(pool, first, step)
            for q in range(2):
                pool.wait_ge(scattered[q], 128 * NG // 2)


def routed(nc, gate_w, up_w, down_w, xn_d, list_d, rows_out, ident, table):
    with ExitStack() as ctx:
        sb = lambda name, shape, dt=F32: ctx.enter_context(nc.sbuf_tensor(name, shape, dt))
        ps = lambda name: ctx.enter_context(nc.psum_tensor(name, [P, 512], F32))
        sem = lambda name: ctx.enter_context(nc.semaphore(name))
        pair = lambda name: [sem(name + "0"), sem(name + "1")]
        FK, RS = FE // P, RT // P

        ids = [sb(f"ids_{i}", [P, RS], I32) for i in range(2)]
        rows = [sb(f"rows_{i}", [P, RS, D]) for i in range(2)]
        wg = [sb(f"ewg_{i}", [P, KD, FE]) for i in range(2)]
        wu = [sb(f"ewu_{i}", [P, KD, FE]) for i in range(2)]
        wd = [sb(f"ewd_{i}", [P, FK, D]) for i in range(2)]
        rT = [sb(f"rT_{i}", [P, KD, RT]) for i in range(2)]
        h = [sb(f"eh_{i}", [P, FK, RT]) for i in range(2)]
        sg = [sb(f"esg_{i}", [P, RT]) for i in range(2)]
        res = [sb(f"res_{i}", [P, RS, D]) for i in range(2)]
        tb = [ps(f"etb{i}") for i in range(RS)]
        gu = [ps(f"egu{i}") for i in range(FK)]
        db = [ps(f"edb{i}") for i in range(RS)]

        ids_ld = pair("ids_ld")
        rows_ld, gu_ld, wd_ld, stored = pair("rows_ld"), pair("gu_ld"), pair("wd_ld"), pair("rstored")
        t_done, t_ev0, t_ev1 = sem("et_done"), sem("et_ev0"), sem("et_ev1")
        f_done, sg_done, h_done = sem("ef_done"), sem("esg_done"), sem("eh_done")
        d_done, d_ev0, d_ev1 = sem("ed_done"), sem("ed_ev0"), sem("ed_ev1")
        pool_gate, sp_gate = sem("epool_gate"), sem("esp_gate")

        def run(eng, step, extra=0):
            step(0, 0)
            step(1, 1)
            with eng.Fori(1, NRT // 2 - 1) as i:
                step(2 * i, 0)
                step(2 * i + 1, 1)
            step(NRT - 2, 0)
            step(NRT - 1, 1)

        uses = lambda t, q: 8 * (t - q)

        block = ctx.enter_context(nc.Block())

        @block.sync
        def _(sp):
            def step(t, q):
                at = slice(t, t + 1) if isinstance(t, int) else bass.ds(t, 1)
                row = sp.value_load(table[0:1, 0, at], min_val=0, max_val=E * REGION)
                e = sp.value_load(table[0:1, 1, at], min_val=0, max_val=E - 1)
                after(sp, rows_ld[q], 2 * uses(t, q))
                hold(sp, sp_gate)
                sp.dma_start(ids[q][:, :], list_d[bass.ds(row, RT), :].rearrange("(p s) o -> p (s o)", s=RS)).then_inc(ids_ld[q], 16)
                after(sp, f_done, 2 * t - 2)
                hold(sp, sp_gate)
                sp.dma_start(wg[q][:, :, :], gate_w[bass.ds(e, 1)].rearrange("o (k p) f -> p (o k) f", p=P)).then_inc(gu_ld[q], 16)
                sp.dma_start(wu[q][:, :, :], up_w[bass.ds(e, 1)].rearrange("o (k p) f -> p (o k) f", p=P)).then_inc(gu_ld[q], 16)
                after(sp, d_done, 2 * t - 2)
                hold(sp, sp_gate)
                sp.dma_start(wd[q][:, :, :], down_w[bass.ds(e, 1)].rearrange("o (k p) f -> p (o k) f", p=P)).then_inc(wd_ld[q], 16)

            run(sp, step)

        @block.tensor
        def _(pe):
            def turn(t, q):
                pe.wait_ge(rows_ld[q], 2 * uses(t, q) + 32)
                after(pe, t_ev0, t)
                after(pe, t_ev1, t)
                for s in range(RS):
                    for k in range(KD):
                        mm = pe.transpose(tb[s][:, k * P:(k + 1) * P], rows[q][:, s, k * P:(k + 1) * P], ident[:, :])
                    mm.then_inc(t_done, 1)

            def gate_up(t, q, f):
                if f == 0:
                    pe.wait_ge(t_ev0, t + 1)
                    pe.wait_ge(t_ev1, t + 1)
                    pe.wait_ge(gu_ld[q], 2 * uses(t, q) + 32)
                after(pe, h_done, 2 * t + f - 1)
                for o, w in ((0, wg[q]), (RT, wu[q])):
                    for k in range(KD):
                        mm = pe.matmul(gu[f][:, o:o + RT], w[:, k, f * P:(f + 1) * P], rT[q][:, k, :],
                                       start=(k == 0), stop=(k == KD - 1))
                mm.then_inc(f_done, 1)

            def down(t, q):
                pe.wait_ge(h_done, 2 * t + 2)
                pe.wait_ge(wd_ld[q], uses(t, q) + 16)
                after(pe, d_ev0, t)
                after(pe, d_ev1, t)
                for s in range(RS):
                    for k in range(FK):
                        mm = pe.matmul(db[s][:, :], h[q][:, k, s * P:(s + 1) * P], wd[q][:, k, :],
                                       start=(k == 0), stop=(k == FK - 1))
                    mm.then_inc(d_done, 1)

            def step(t, q):
                gate_up(t, q, 0)
                if not (isinstance(t, int) and t == 0):
                    down(t - 1, 1 - q)
                gate_up(t, q, 1)
                if not (isinstance(t, int) and t == NRT - 1):
                    turn(t + 1, 1 - q)

            turn(0, 0)
            run(pe, step)
            down(NRT - 1, 1)

        @block.scalar
        def _(act):
            def turned(t, q):
                act.wait_ge(t_done, 2 * t + 1)
                act.copy(rT[q][:, :, 0:P], tb[0][:, :].rearrange("p (k t) -> p k t", k=KD)).then_inc(t_ev0, 1)

            def silu(t, q, f):
                act.wait_ge(f_done, 2 * t + f + 1)
                after(act, h_done, 2 * t + f - 1)
                act.activation(sg[f][:, :], gu[f][:, 0:RT], ACT.Silu).then_inc(sg_done, 1)

            def downed(t, q):
                act.wait_ge(d_done, 2 * t + 1)
                after(act, stored[q], uses(t, q))
                act.copy(res[q][:, 0, :], db[0][:, :]).then_inc(d_ev0, 1)

            def step(t, q):
                silu(t, q, 0)
                if not (isinstance(t, int) and t == 0):
                    downed(t - 1, 1 - q)
                silu(t, q, 1)
                if not (isinstance(t, int) and t == NRT - 1):
                    turned(t + 1, 1 - q)

            turned(0, 0)
            run(act, step)
            downed(NRT - 1, 1)

        @block.vector
        def _(dve):
            def turned(t, q):
                dve.wait_ge(t_done, 2 * t + 2)
                dve.tensor_copy(rT[q][:, :, P:2 * P], tb[1][:, :].rearrange("p (k t) -> p k t", k=KD)).then_inc(t_ev1, 1)

            def hidden(t, q, f):
                dve.wait_ge(sg_done, 2 * t + f + 1)
                dve.tensor_tensor(h[q][:, f, :], gu[f][:, RT:2 * RT], sg[f][:, :], ALU.mult).then_inc(h_done, 1)

            def downed(t, q):
                dve.wait_ge(d_done, 2 * t + 2)
                after(dve, stored[q], uses(t, q))
                dve.tensor_copy(res[q][:, 1, :], db[1][:, :]).then_inc(d_ev1, 1)

            def step(t, q):
                hidden(t, q, 0)
                if not (isinstance(t, int) and t == 0):
                    downed(t - 1, 1 - q)
                hidden(t, q, 1)
                if not (isinstance(t, int) and t == NRT - 1):
                    turned(t + 1, 1 - q)

            turned(0, 0)
            run(dve, step)
            downed(NRT - 1, 1)

        @block.gpsimd
        def _(pool):
            def gather(t, q):
                after(pool, t_done, 2 * t - 2)
                pool.wait_ge(ids_ld[q], uses(t, q) + 16)
                hold(pool, pool_gate)
                for s in range(RS):
                    pool.indirect_dma_start(rows[q][:, s, :], None, xn_d[:, :],
                                            bass.IndirectOffsetOnAxis(ap=ids[q][:, s:s + 1], axis=0)).then_inc(rows_ld[q], 16)

            def step(t, q):
                if not (isinstance(t, int) and t >= NRT - 2):
                    gather(t + 2, q)
                pool.wait_ge(d_ev0, t + 1)
                pool.wait_ge(d_ev1, t + 1)
                hold(pool, pool_gate)
                dst = rows_out[t * RT:(t + 1) * RT, :] if isinstance(t, int) else rows_out[bass.ds(t * RT, RT), :]
                pool.dma_start(dst.rearrange("(p s) d -> p s d", s=RS), res[q][:, :, :]).then_inc(stored[q], 16)

            gather(0, 0)
            gather(1, 1)
            run(pool, step)
            for q in range(2):
                pool.wait_ge(stored[q], 16 * NRT // 2)


def attend(nc, w_kv, w_c2l, w_outT, tri_in, q_d, k_d, v_d, base_d, rows_out, out, ident, slots_all, gap_all):
    with ExitStack() as ctx:
        sb = lambda name, shape, dt=F32: ctx.enter_context(nc.sbuf_tensor(name, shape, dt))
        ps = lambda name: ctx.enter_context(nc.psum_tensor(name, [P, 512], F32))
        sem = lambda name: ctx.enter_context(nc.semaphore(name))
        pair = lambda name: [sem(name + "0"), sem(name + "1")]
        KB = T // P
        NP, NSC = 4, 3
        SCALE = C ** -0.5

        qa = sb("qa", [CA, T]); ka = sb("ka", [CA, T]); va = sb("va", [P, KB, CA])
        qr = sb("qr", [C, T], F32R); kr = sb("kr", [C, T], F32R)
        mo = sb("mo", [C, D]); wz = sb("wz", [LAT, D]); wo = sb("wo", [LAT, D]); wc = sb("wc", [LAT, C])
        tri = sb("tri3", [P, 2, P]); future = sb("future", [P, P], BF16); identb = sb("identb", [P, P], BF16)
        w_all = sb("w_all", [P, 2, NG * GT]); den = sb("den", [P, NG * GT])
        mx = sb("mx", [P, GT, QB]); mcol = sb("mcol", [P, GT, CA]); last = sb("last", [CA, 1])
        pr = [sb(f"pr_{i}", [P, GROUP]) for i in range(NP)]
        oT = sb("oT", [CA, GROUP]); lr = sb("lr", [P, GT])
        base = [sb(f"base_{i}", [P, GT, D]) for i in range(2)]
        got = [sb(f"got_{i}", [P, 2, GT, D]) for i in range(2)]

        mb = [ps("mb0"), ps("mb1")]
        sc = [ps(f"sc{i}") for i in range(NSC)]
        ob, pj, nb = ps("ob"), ps("pj"), ps("anb")

        const_in, qkv_in, a_ready, r_done = sem("const_in"), sem("qkv_in"), sem("a_ready"), sem("r_done")
        sum_w, mo_done, mo_ev, w_exp, chain = sem("sum_w"), sem("mo_done"), sem("mo_ev"), sem("w_exp"), sem("a_chain")
        m_done, m_red, mc_done, mt_done, mrow = sem("m_done"), sem("m_red"), sem("mc_done"), sem("mt_done"), sem("mrow")
        s_done, e_done, sel_done, pv_done = sem("s_done"), sem("e_done"), sem("sel_done"), sem("pv_done")
        o_ev, l_done, l_ev, p_done, p_ev = sem("o_ev"), sem("al_done"), sem("l_ev"), sem("p_done"), sem("p_ev")
        blk_done, base_in, got_in, out_st = sem("blk_done"), pair("base_in"), pair("got_in"), pair("out_st")

        base_g = base_d.rearrange("(g j p) d -> g p j d", j=GT, p=P)
        out_g = out.rearrange("b t d -> (b t) d").rearrange("(g j p) d -> g p j d", j=GT, p=P)
        CONSTS = 16 * 4

        units = [GT * (n % QB + 1) for n in range(NG)]
        first_unit = [sum(units[:n]) for n in range(NG + 1)]

        def steps(n):
            ahead = units[n + 1] if n + 1 < NG and (n + 1) % QB else 0
            for kb in range(units[n]):
                lo = kb
                hi = kb + 1 if kb + 1 < units[n] else ahead
                yield kb, range(min(lo, ahead), min(hi, ahead)) if ahead else range(0)

        block = ctx.enter_context(nc.Block())

        @block.sync
        def _(sp):
            for dst, src in ((wz[:, :], w_kv), (wo[:, :], w_outT), (wc[:, :], w_c2l),
                             (tri[:, :, :], tri_in.rearrange("a p c -> p a c"))):
                sp.dma_start(dst, src).then_inc(const_in, 16)

            def load_base(n):
                after(sp, out_st[n % 2], 16 * (n // 2))
                sp.dma_start(base[n % 2][:, :, :], base_g[n]).then_inc(base_in[n % 2], 16)

            for n in range(NG):
                if n % QB == 0:
                    b = n // QB
                    after(sp, pv_done, first_unit[n])
                    sp.dma_start(qa[0:C, :], q_d[:, b * T:(b + 1) * T]).then_inc(qkv_in, 16)
                    sp.dma_start(ka[0:C, :], k_d[:, b * T:(b + 1) * T]).then_inc(qkv_in, 16)
                    sp.dma_start(va[:, :, :].rearrange("p (g j) c -> p g (j c)", j=GT),
                                 v_d[b * QB:(b + 1) * QB].rearrange("g p c -> p g c")).then_inc(qkv_in, 16)
                load_base(n)
                if n:
                    sp.wait_ge(blk_done, n)
                    sp.dma_start(out_g[n - 1], base[(n - 1) % 2][:, :, :]).then_inc(out_st[(n - 1) % 2], 16)
            sp.wait_ge(blk_done, NG)
            sp.dma_start(out_g[NG - 1], base[(NG - 1) % 2][:, :, :]).then_inc(out_st[(NG - 1) % 2], 16)
            for q in range(2):
                sp.wait_ge(out_st[q], 16 * NG // 2)

        @block.tensor
        def _(pe):
            def max_scores(n, v):
                m, (j, c) = n % QB, divmod(v, n % QB + 1)
                g = first_unit[n] + v
                if v == 0:
                    pe.wait_ge(r_done, 2 * (n // QB) + 2)
                after(pe, m_red, g - 1)
                w = GROUP if c < m else P * (j + 1)
                col = m * GROUP + j * P
                mm = pe.matmul(mb[g % 2][:, 0:w], qr[:, col:col + P], kr[:, c * GROUP:c * GROUP + w],
                               start=True, stop=(c < m))
                if c == m:
                    mm = pe.matmul(mb[g % 2][:, w - P:w], identb[:, :], future[:, :], start=False, stop=True)
                mm.then_inc(m_done, 1)

            def turn_max(n):
                pe.wait_ge(mc_done, n + 1)
                after(pe, l_ev, n - 1)
                for j in range(GT):
                    mm = pe.matmul(nb[0:CA, j * P:(j + 1) * P], mcol[:, j, :], ident[:, :], start=True, stop=True)
                mm.then_inc(mt_done, 1)

            def scores(n, kb):
                u, m = first_unit[n] + kb, n % QB
                off = max(0, kb - GT * m) * P
                if kb == 0:
                    pe.wait_ge(mrow, n + 1)
                after(pe, e_done, u - NSC + 1)
                pe.matmul(sc[u % NSC][:, off:GROUP], ka[:, kb * P:(kb + 1) * P],
                          qa[:, m * GROUP + off:(m + 1) * GROUP], start=True, stop=True).then_inc(s_done, 1)

            def outputs(n, kb):
                u, m = first_unit[n] + kb, n % QB
                d = kb - GT * m
                off = max(0, d) * P
                pe.wait_ge(e_done, u + 1)
                if d >= 0:
                    pe.wait_ge(sel_done, GT * n + d + 1)
                if kb == 0:
                    after(pe, o_ev, n)
                pe.matmul(ob[0:CA, off:GROUP], va[:, kb, :], pr[u % NP][:, off:GROUP],
                          start=(kb == 0), stop=(kb == units[n] - 1)).then_inc(pv_done, 1)

            def project(n, j):
                if j == 0:
                    pe.wait_ge(o_ev, n + 1)
                    pe.wait_ge(mrow, min(n + 2, NG))
                    for i in range(GT):
                        mm = pe.matmul(nb[:, i:i + 1], oT[:, i * P:(i + 1) * P], last[:, :], start=True, stop=True)
                    mm.then_inc(l_done, 1)
                after(pe, p_ev, GT * n + j)
                pe.matmul(pj[:, :], oT[0:C, j * P:(j + 1) * P], mo[:, :], start=True, stop=True).then_inc(p_done, 1)

            pe.wait_ge(sum_w, 1)
            pe.matmul(pj[0:C, :], wc[:, :], wz[:, :], start=True, stop=True).then_inc(mo_done, 1)
            pe.wait_ge(mo_ev, 1)
            pe.wait_ge(a_ready, 1)
            for n in range(NG):
                if n % QB == 0:
                    for v in range(units[n]):
                        max_scores(n, v)
                    turn_max(n)
                for kb, ahead in steps(n):
                    scores(n, kb)
                    for v in ahead:
                        max_scores(n + 1, v)
                    if kb >= 2:
                        outputs(n, kb - 2)
                    if n and kb < GT:
                        project(n - 1, kb)
                outputs(n, units[n] - 2)
                outputs(n, units[n] - 1)
                if (n + 1) % QB:
                    turn_max(n + 1)
            for j in range(GT):
                project(NG - 1, j)

        @block.scalar
        def _(act):
            act.activation(w_all[:, 1, :], gap_all[:, :], ACT.Exp).then_inc(w_exp, 1)
            act.wait_ge(mo_done, 1)
            act.copy(mo[:, :], pj[0:C, :]).then_inc(mo_ev, 1)
            for n in range(NG):
                m = n % QB
                if m == 0:
                    act.wait_ge(qkv_in, 48 * (n // QB) + 48)
                    act.copy(kr[:, :], ka[0:C, :]).then_inc(r_done, 1)
                for kb in range(units[n]):
                    u = first_unit[n] + kb
                    off = max(0, kb - GT * m) * P
                    act.wait_ge(s_done, u + 1)
                    after(act, pv_done, u - NP + 1)
                    act.activation(pr[u % NP][:, off:GROUP], sc[u % NSC][:, off:GROUP], ACT.Exp,
                                   scale=SCALE).then_inc(e_done, 1)
                act.wait_ge(pv_done, first_unit[n + 1])
                after(act, p_done, GT * n)
                act.copy(oT[:, :], ob[0:CA, :]).then_inc(o_ev, 1)

        @block.vector
        def _(dve):
            links = [0]

            def link(i):
                links[0] += 1
                i.then_inc(chain, 1)
                dve.wait_ge(chain, links[0])

            def reduce_max(n, v):
                m, (j, c) = n % QB, divmod(v, n % QB + 1)
                g = first_unit[n] + v
                w = GROUP if c < m else P * (j + 1)
                dve.wait_ge(m_done, g + 1)
                dve.tensor_reduce(mx[:, j, c:c + 1], mb[g % 2][:, 0:w], AX.X, ALU.max).then_inc(m_red, 1)

            def negated_max(n):
                m = n % QB
                dve.wait_ge(m_red, first_unit[n + 1])
                after(dve, mt_done, n)
                dve.tensor_reduce(mcol[:, :, C], mx[:, :, 0:m + 1], AX.X, ALU.max, negate=True).then_inc(mc_done, 1)
                dve.wait_ge(mt_done, n + 1)
                dve.tensor_copy(qa[C:CA, m * GROUP:(m + 1) * GROUP], nb[C:CA, :]).then_inc(mrow, 1)

            def combine(n, j):
                q, t = n % 2, GT * n + j
                if j == 0:
                    dve.wait_ge(l_done, n + 1)
                    link(dve.reciprocal(lr[:, :], nb[:, 0:GT]))
                    dve.wait_ge(base_in[q], 16 * (n // 2) + 16)
                    dve.wait_ge(got_in[q], 128 * (n // 2) + 128)
                    dve.sem_inc(l_ev, 1)
                dve.wait_ge(p_done, t + 1)
                row = base[q][:, j, :]
                dve.scalar_tensor_tensor(out=row, in0=pj[:, :], scalar=lr[:, j:j + 1], in1=row,
                                         op0=ALU.mult, op1=ALU.add).then_inc(p_ev, 1)
                dve.wait_ge(p_ev, t + 1)
                link(dve.scalar_tensor_tensor(out=row, in0=got[q][:, 0, j, :], scalar=w_all[:, 0, t:t + 1], in1=row,
                                              op0=ALU.mult, op1=ALU.add))
                i = dve.scalar_tensor_tensor(out=row, in0=got[q][:, 1, j, :], scalar=w_all[:, 1, t:t + 1], in1=row,
                                             op0=ALU.mult, op1=ALU.add)
                if j == GT - 1:
                    i.then_inc(blk_done, 1)

            dve.wait_ge(const_in, CONSTS)
            dve.tensor_tensor(wz[:, :], wz[:, :], wo[:, :], ALU.add).then_inc(sum_w, 1)
            dve.tensor_copy(future[:, :], tri[:, 1, :])
            dve.tensor_copy(identb[:, :], ident[:, :])
            dve.memset(mcol[:, :, :], 0.0)
            dve.memset(last[0:C, :], 0.0)
            dve.memset(last[C:CA, :], 1.0)
            dve.memset(ka[C:CA, :], 1.0).then_inc(a_ready, 1)
            dve.wait_ge(w_exp, 1)
            link(dve.tensor_scalar(den[:, :], w_all[:, 1, :], 1.0, None, ALU.add))
            link(dve.reciprocal(w_all[:, 0, :], den[:, :]))
            link(dve.tensor_tensor(w_all[:, 1, :], w_all[:, 1, :], w_all[:, 0, :], ALU.mult))
            for n in range(NG):
                if n % QB == 0:
                    dve.wait_ge(qkv_in, 48 * (n // QB) + 48)
                    dve.tensor_copy(qr[:, :], qa[0:C, :]).then_inc(r_done, 1)
                    for v in range(units[n]):
                        reduce_max(n, v)
                    negated_max(n)
                for kb, ahead in steps(n):
                    for v in ahead:
                        reduce_max(n + 1, v)
                    if n and kb < GT:
                        combine(n - 1, kb)
                if (n + 1) % QB:
                    negated_max(n + 1)
            for j in range(GT):
                combine(NG - 1, j)

        @block.gpsimd
        def _(pool):
            def gather(n):
                q = n % 2
                after(pool, blk_done, n - 1)
                for j in range(GT):
                    for c in range(2):
                        pool.indirect_dma_start(got[q][:, c, j, :], None, rows_out[:, :],
                                                bass.IndirectOffsetOnAxis(ap=slots_all[:, GT * n + j, c:c + 1], axis=0)
                                                ).then_inc(got_in[q], 16)

            gather(0)
            for n in range(NG):
                for d in range(GT):
                    u = first_unit[n] + GT * (n % QB) + d
                    part = pr[u % NP][:, d * P:(d + 1) * P]
                    pool.wait_ge(e_done, u + 1)
                    pool.affine_select(out=part, in_=part, pattern=[[1, P]], compare_op=ALU.is_ge, fill=0.0,
                                       base=0, channel_multiplier=-1).then_inc(sel_done, 1)
                if n + 1 < NG:
                    gather(n + 1)


def rope_tables():
    f = np.float32
    inv = f(1.0) / np.power(f(10000.0), np.arange(0, C, 2, dtype=f) / f(C)).astype(f)
    angle = np.arange(T, dtype=f)[:, None] * inv[None, :]
    cos, sin = np.cos(angle).astype(f), np.sin(angle).astype(f)
    cos = np.concatenate([cos, cos], axis=1).T
    sin = np.concatenate([-sin, sin], axis=1).T
    one = np.stack([np.concatenate([cos, cos]), np.concatenate([sin, sin])], axis=1)
    seq = one.reshape(2 * C, 2, QB, GROUP).transpose(2, 0, 1, 3)
    return np.ascontiguousarray(np.concatenate([seq] * B))


def shape_tables():
    f = np.float32
    i = np.arange(P)
    tri = np.stack([(i[:, None] < i[None, :]).astype(f), np.where(i[None, :] > i[:, None], f(NEG), f(0)).astype(f)])
    rev = np.tile((E - np.arange(E)).astype(f), (P, GT, 1))
    start = np.tile((np.arange(E) * REGION).astype(f), (P, 1, 1))
    tiles = np.repeat(np.arange(NRT), E).astype(f)
    upto = (np.arange(E)[None, :] <= np.arange(E)[:, None]).astype(f)
    upto = np.tile(upto, (P, 1, 1))
    row = np.concatenate([tiles, np.arange(NRT).astype(f)])[None, :]
    token = np.arange(N, dtype=np.int32).reshape(NG * GT, P).T
    return np.eye(P, dtype=f), tri, np.concatenate([rev, start], axis=1), row, upto, token


def kernel(**inputs):
    import concourse.bacc as bacc
    from concourse.bass_utils import run_bass_kernel_spmd

    a = {name: np.asarray(v) for name, v in inputs.items()}
    wq, wkv = a["L0_attn_W_q_comp"], a["L0_attn_W_kv_comp"]
    wqT, wkT, wvT = wq.T, wkv[:C].T, wkv[C:].T
    swap = lambda w: np.concatenate([w[:, C // 2:], w[:, :C // 2]], axis=1)
    ident, tri, route, tile, upto, token = shape_tables()
    arrays = {
        "x": a["L0_attn_x"].reshape(N, D), "w_kv": a["L0_attn_W_to_kv"], "w_compT": a["L0_attn_W_compress"].T,
        "gamma": a["L0_attn_ln_gamma"][:, None], "beta": a["L0_attn_ln_beta"][:, None],
        "w_qk": np.concatenate([wqT, wkT], axis=1), "w_qk_swap": np.concatenate([swap(wqT), swap(wkT)], axis=1),
        "w_vT": wvT, "w_c2l": a["L0_attn_W_comp2lat"], "w_outT": a["L0_attn_W_out_res"].T, "b_out": a["L0_attn_b_out_res"],
        "routerT": a["L0_ffn_router_w"].T, "gate_w": a["L0_ffn_gate_w"], "up_w": a["L0_ffn_up_w"],
        "down_w": a["L0_ffn_down_w"], "sh_gate": a["L0_ffn_shared_gate_w"], "sh_up": a["L0_ffn_shared_up_w"],
        "sh_down": a["L0_ffn_shared_down_w"], "rope": rope_tables(), "ident_in": ident, "tri_in": tri,
        "route_in": route, "tile_in": tile, "upto_in": upto, "token_in": token,
    }
    arrays = {name: np.ascontiguousarray(v) for name, v in arrays.items()}
    nc = bacc.Bacc("TRN2", target_bir_lowering=False, num_devices=1)
    args = {name: nc.dram_tensor(name, v.shape, mybir.dt.from_np(v.dtype), kind="ExternalInput").ap()
            for name, v in arrays.items()}
    out = nc.dram_tensor("out", (B, T, D), F32, kind="ExternalOutput").ap()
    build(nc, **args, out=out)
    r = run_bass_kernel_spmd(nc, [arrays], core_ids=[0])
    return r.results[0]["out"]
```

```python
from contextlib import ExitStack

import numpy as np
import concourse.bass as bass
from concourse import mybir

F32 = mybir.dt.float32
F32R = mybir.dt.float32r
BF16 = mybir.dt.bfloat16
I32 = mybir.dt.int32
ALU = mybir.AluOpType
ACT = mybir.ActivationFunctionType
AX = mybir.AxisListType

P = 128
B, T, D = 2, 4096, 512
N = B * T
E, FE, FS = 16, 256, 512
C = 64
LAT = 128
GT = 4
GROUP = GT * P
NG = N // GROUP
KD = D // P
FC = FS // P
RT = P
AHEAD = 4
NRT = 2 * N // RT + E
REGION = 2 * N
LIST = E * REGION + RT
LN_EPS = 1e-5
QB = T // GROUP
BIG = 3.0e38
NEG = -1.0e30
EW = KD * 2 * FE + FE // P * D
EH = EW // 2
CA = C + 1


def value(ap):
    return ap.bitcast(F32)


def parts(pe, dst, pairs, first=True, last=True):
    terms = [t for (sh, sl), (mh, ml) in pairs for t in ((sh, mh), (sh, ml), (sl, mh))]
    for i, (w, m) in enumerate(terms):
        mm = pe.matmul(dst, w, m, start=(first and i == 0), stop=(last and i == len(terms) - 1))
    return mm


def after(eng, sem, value):
    if isinstance(value, int) and value <= 0:
        return
    eng.wait_ge(sem, value)


def hold(eng, gate):
    eng.sem_inc(gate, 1)


def build(nc, x, w_kv, w_compT, gamma, beta, w_qk, w_qk_swap, w_vT, w_c2l, w_outT, b_out, routerT,
          gate_w, up_w, down_w, sh_gate, sh_up, sh_down, rope, ident_in, tri_in, route_in, upto_in, token_in, tile_p_in, out):
    q_d = nc.dram_tensor("q_scratch", (C, N), F32, kind="Internal").ap()
    k_d = nc.dram_tensor("k_scratch", (C, N), F32, kind="Internal").ap()
    v_d = nc.dram_tensor("v_scratch", (NG, P, GT * CA), F32, kind="Internal").ap()
    base_d = nc.dram_tensor("base_scratch", (N, D), F32, kind="Internal").ap()
    ew_d = nc.dram_tensor("expert_parts", (E, P, 2, 2, EH), F32, kind="Internal").ap()
    xn_d = nc.dram_tensor("xn_scratch", (N, D), F32, kind="Internal").ap()
    list_d = nc.dram_tensor("token_list", (LIST, 1), I32, kind="Internal").ap()
    rows_out = nc.dram_tensor("rows_out", (NRT * RT, D), F32, kind="Internal").ap()

    with ExitStack() as ctx:
        keep = lambda name, shape, dt: ctx.enter_context(nc.sbuf_tensor(name, shape, dt))
        ident = keep("ident", [P, P], F32)
        slots_all = keep("slots_all", [P, NG * GT, 2], I32)
        gap_all = keep("gap_all", [P, NG * GT], F32)
        table = keep("table", [1, 2, NRT], I32)
        upto_tiles = keep("upto_tiles", [1, E], I32)
        ids_all = keep("ids_all", [P, NRT], I32)
        prepare(nc, x, w_kv, w_compT, gamma, beta, w_qk, w_qk_swap, w_vT, b_out, routerT, sh_gate, sh_up,
                sh_down, rope, ident_in, tri_in, route_in, upto_in, token_in, tile_p_in, q_d, k_d, v_d, base_d, xn_d, list_d,
                ident, slots_all, gap_all, table, upto_tiles, ids_all, ew_d, gate_w, up_w, down_w)
        routed(nc, ew_d, xn_d, rows_out, ident, table, upto_tiles, ids_all)
        attend(nc, w_kv, w_c2l, w_outT, tri_in, q_d, k_d, v_d, base_d, rows_out, out, ident, slots_all, gap_all)


def prepare(nc, x, w_kv, w_compT, gamma, beta, w_qk, w_qk_swap, w_vT, b_out, routerT, sh_gate, sh_up,
            sh_down, rope, ident_in, tri_in, route_in, upto_in, token_in, tile_p_in, q_d, k_d, v_d, base_d, xn_d, list_d,
            ident, slots_all, gap_all, table, upto_tiles, ids_all, ew_d, gate_w, up_w, down_w):
    ctx = ExitStack()
    with ctx:
        sb = lambda name, shape, dt=F32: ctx.enter_context(nc.sbuf_tensor(name, shape, dt))
        ps = lambda name: ctx.enter_context(nc.psum_tensor(name, [P, 512], F32))
        sem = lambda name: ctx.enter_context(nc.semaphore(name))

        wgp, wup, wdp = [[sb(f"{w}_{c}", [P, KD, FS], F32R) for c in "hl"] for w in ("wg", "wu", "wd")]
        wcr = sb("wcr", [P, KD, C + E])
        wcrp = [sb(f"wcr_{c}", [P, KD, C + E], F32R) for c in "hl"]
        wcT = sb("wcT", [P, C])
        wqk = sb("wqk", [C, 2 * C]); wqks = sb("wqks", [C, 2 * C]); wv = sb("wv", [C, C])
        gam = sb("gam", [C, 1]); bet = sb("bet", [C, 1]); bias = sb("bias", [P, D])
        tri = sb("tri", [P, 2, P]); before = sb("before", [P, P], BF16); ones = sb("ones", [P, P], BF16)
        rt = sb("rt", [P, 5, E])
        upto = sb("upto", [P, E, E])
        halfs = sb("halfs", [P, GT])
        zeros = sb("zeros", [P, LIST // P // 3], I32)
        token = sb("token", [P, NG * GT], I32)
        tok = [sb(f"tok_{i}", [P, GT], I32) for i in range(2)]
        x4 = [sb(f"x4_{i}", [P, GT, D]) for i in range(2)]
        xn4 = sb("xn4", [P, GT, D])
        xb4 = [sb(f"xb4_{i}", [P, GT, D]) for i in range(2)]
        xT = [[sb(f"xT_{i}{c}", [P, KD, GROUP], F32R) for c in "hl"] for i in range(2)]
        cs = [sb(f"cs_{i}", [P, 2, GROUP]) for i in range(2)]
        h = [sb(f"h_{c}", [P, FC, GROUP], F32R) for c in "hl"]
        ht = sb("ht", [P, GROUP])
        ew = sb("ew", [P, EH]); ewp = [sb(f"ew_{c}", [P, EH], F32R) for c in "hl"]
        sg = [sb(f"sg_{i}", [P, GROUP]) for i in range(2)]
        stx = sb("stx", [P, GT, 6]); mvx = sb("mvx", [P, GT, 2]); rsx = sb("rsx", [P, GT])
        stc = sb("stc", [P, GT, 6]); mvc = sb("mvc", [P, GT, 2]); rsc = sb("rsc", [P, GT])
        lc = sb("lc", [P, GT, C + E]); cn = sb("cn", [P, GT, C])
        top = sb("top", [P, 2, GT]); pick = sb("pick", [P, 2, GT])
        eq = sb("eq", [P, GT, E]); oh = sb("oh", [P, 2, GT, E]); rest = sb("rest", [P, GT, E])
        mask = sb("mask", [P, GT, E], BF16)
        pb = sb("pb", [P, GT, E]); pk = sb("pk", [P, 2, GT, E]); slotf = sb("slotf", [P, GT, 2])
        slot = [sb(f"slot_{i}", [P, GT, 2], I32) for i in range(2)]
        carry = sb("carry", [P, E])
        chT = sb("chT", [C, GROUP]); t1 = sb("t1", [P, GROUP]); t2 = sb("t2", [P, GROUP])
        qks = [sb(f"qks_{i}", [P, GROUP]) for i in range(2)]
        vs = [sb(f"vs_{i}", [P, GT, CA]) for i in range(2)]
        cnt = sb("cnt", [P, 6, E]); cnti = sb("cnti", [P, 2, E], I32)
        NS = NG * GT * 2
        se = sb("se", [P, NS]); sp_ = sb("sp_", [P, NS]); sei = sb("sei", [P, NS], I32)
        small = sb("small", [1, NRT])
        HT = NRT // 2
        half = sb("half", [P, 2, E]); spot = sb("spot", [P, 4, 2]); spoti = sb("spoti", [P, 2], I32)
        listed = sb("listed", [P, 2, P], I32); listf = sb("listf", [P, 2, P])
        tile_p = sb("tile_p", [P, 2])

        tb = [ps("tb0"), ps("tb1")]
        lb, nb = ps("lb"), ps("nb")
        gb = [ps(f"gb{i}") for i in range(4)]

        consts, x_in = sem("consts"), [sem("x_in0"), sem("x_in1")]
        setup, wc_done, wc_ev = sem("setup"), sem("wc_done"), sem("wc_ev")
        chain, pool_chain = sem("chain"), sem("pool_chain")
        mvx_done, rsx_done, xn_done, xb_done = sem("mvx_done"), sem("rsx_done"), sem("xn_done"), sem("xb_done")
        mvc_done, rsc_done, cn_done = sem("mvc_done"), sem("rsc_done"), sem("cn_done")
        t_done, t_ev, l_done, mask_done = sem("t_done"), sem("t_ev"), sem("l_done"), sem("mask_done")
        cT_done, ch_done, pos_done, pos_ev = sem("cT_done"), sem("ch_done"), sem("pos_done"), sem("pos_ev")
        qkv_done, qk_done, v_done, slot_done = sem("qkv_done"), sem("qk_done"), sem("v_done"), sem("slot_done")
        f_done, sg_done, h_done = sem("f_done"), sem("sg_done"), sem("h_done")
        d_done, d_ev = sem("d_done"), sem("d_ev")
        scattered = [sem("scattered0"), sem("scattered1")]
        st_qkv = [sem("st_qkv0"), sem("st_qkv1")]
        st_base = [sem("st_base0"), sem("st_base1")]
        rope_done = sem("rope_done")
        sp_gate = sem("sp_gate")
        dve_gate, pe_gate, pool_gate = sem("dve_gate"), sem("pe_gate"), sem("pool_gate")
        st_xn, hi_done, split_done, ht_done, hh_done = sem("st_xn"), sem("hi_done"), sem("split_done"), sem("ht_done"), sem("hh_done")
        ew_in, ew_hi, ew_lo, ew_st = sem("ew_in"), sem("ew_hi"), sem("ew_lo"), sem("ew_st")
        te_done = sem("te_done")
        idx_done, listed_in, lf_done, li_done = sem("idx_done"), sem("listed_in"), sem("lf_done"), sem("li_done")
        cleared, t_hi = sem("cleared"), sem("t_hi")

        loads = [(ident[:, :], ident_in), (ht[:, :], w_kv), (wcT[:, :], w_compT),
                 (wcr[:, :, C:C + E], routerT.rearrange("(k p) e -> p k e", p=P)),
                 (tri[:, :, :], tri_in.rearrange("a p c -> p a c")), (rt[:, :, :], route_in),
                 (wqk[:, :], w_qk), (wqks[:, :], w_qk_swap), (wv[:, :], w_vT), (gam[:, :], gamma), (bet[:, :], beta),
                 (bias[:, :], b_out.partition_broadcast(P)),
                 (xb4[0][:, :, :], sh_gate.rearrange("(k p) f -> p k f", p=P)),
                 (xb4[1][:, :, :], sh_up.rearrange("(k p) f -> p k f", p=P)),
                 (xn4[:, :, :], sh_down.rearrange("(k p) f -> p k f", p=P)),
                 (tile_p[:, :], tile_p_in),
                 (upto[:, :, :], upto_in), (token[:, :], token_in)]
        CONSTS = 16 * len(loads)
        x_g = x.rearrange("(g j p) d -> g p j d", j=GT, p=P)
        base_g = base_d.rearrange("(g j p) d -> g p j d", j=GT, p=P)
        xn_g = xn_d.rearrange("(g j p) d -> g p j d", j=GT, p=P)
        rope_g = rope

        def pick_g(ap, n):
            return ap[n] if isinstance(n, int) else ap[bass.ds(n, 1)].rearrange("o p j d -> p (o j) d")

        def pick_e(ap, n):
            return ap[n] if isinstance(n, int) else ap[bass.ds(n, 1)].rearrange("o a b -> (o a) b")

        def run(eng, first, step):
            first()
            step(None, 0, 0)
            step(0, 1, 1)
            step(1, 2, 0)
            with eng.Fori(1, NG // 2 - 1) as i:
                step(2 * i, 2 * i + 1, 1)
                step(2 * i + 1, 2 * i + 2, 0)
            step(NG - 2, NG - 1, 1)
            step(NG - 1, None, 0)

        block = ctx.enter_context(nc.Block())

        def times(n, q):
            return 8 * (n - q)

        @block.sync
        def _(sp):
            def load(n, q):
                after(sp, xn_done, n - 1)
                after(sp, xb_done, n - 1)
                after(sp, qk_done, n - 1)
                hold(sp, sp_gate)
                sp.dma_start(x4[q][:, :, :], pick_g(x_g, n)).then_inc(x_in[q], 16)
                sp.dma_start(cs[q][:, :, :], pick_g(rope_g, n)).then_inc(x_in[q], 16)

            def first():
                load(0, 0)
                for dst, src in loads:
                    sp.dma_start(dst, src).then_inc(consts, 16)
                sp.wait_ge(setup, 1)
                for part in range(3):
                    sp.dma_start(list_d.rearrange("(a p c) o -> a p (c o)", a=3, p=P)[part], zeros[:, :]).then_inc(cleared, 16)
                store_xn(0)
                load_ew(0, 0)

            def load_ew(n, c):
                sp.wait_ge(split_done, 1)
                after(sp, ew_lo, 2 * n + c)
                hold(sp, sp_gate)
                ew_k = ew[:, 0:2 * 2 * FE].rearrange("p (k a f) -> p k a f", a=2, f=FE)
                for a, w in enumerate((gate_w, up_w)):
                    src = pick_e(w, n)[2 * c * P:(2 * c + 2) * P, :].rearrange("(k p) f -> p k f", p=P)
                    sp.dma_start(ew_k[:, :, a, :], src).then_inc(ew_in, 16)
                sp.dma_start(ew[:, 4 * FE:EH], pick_e(down_w, n)[c * P:(c + 1) * P, :]).then_inc(ew_in, 16)

            def store_ew(n, c):
                sp.wait_ge(ew_lo, 2 * n + c + 1)
                hold(sp, sp_gate)
                dst = ew_d[n] if isinstance(n, int) else ew_d[bass.ds(n, 1)].rearrange("o p a c f -> (o p) a c f")
                for a in range(2):
                    sp.dma_start(dst[:, a, c, :], value(ewp[a][:, :])).then_inc(ew_st, 16)

            def store_xn(n):
                sp.wait_ge(xn_done, n + 1)
                hold(sp, sp_gate)
                sp.dma_start(pick_g(xn_g, n), xn4[:, :, :]).then_inc(st_xn, 16)

            def step(s, n, q):
                if n is not None:
                    more = not (isinstance(n, int) and n == NG - 1)
                    if more:
                        load(n + 1, 1 - q)
                    store_ew(n, 0)
                    load_ew(n, 1)
                    store_qkv(n, q)
                    store_ew(n, 1)
                    if more:
                        load_ew(n + 1, 0)
                        store_xn(n + 1)
                if s is not None:
                    sp.wait_ge(d_ev, 4 * s + 4)
                    hold(sp, sp_gate)
                    sp.dma_start(pick_g(base_g, s), xb4[1 - q][:, :, :]).then_inc(st_base[1 - q], 16)

            def store_qkv(n, q):
                sp.wait_ge(qk_done, n + 1)
                sp.wait_ge(v_done, n + 1)
                hold(sp, sp_gate)
                cols = slice(n * GROUP, (n + 1) * GROUP) if isinstance(n, int) else bass.ds(n * GROUP, GROUP)
                sp.dma_start(q_d[:, cols], qks[q][0:C, :]).then_inc(st_qkv[q], 16)
                sp.dma_start(k_d[:, cols], qks[q][C:2 * C, :]).then_inc(st_qkv[q], 16)
                vdst = v_d[n] if isinstance(n, int) else v_d[bass.ds(n, 1)].rearrange("o p c -> (o p) c")
                sp.dma_start(vdst, vs[q][:, :, :].rearrange("p j c -> p (j c)")).then_inc(st_qkv[q], 16)

            run(sp, first, step)
            for q in range(2):
                sp.wait_ge(st_qkv[q], 48 * NG // 2)
                sp.wait_ge(st_base[q], 16 * NG // 2)
            sp.wait_ge(st_xn, 16 * NG)
            sp.wait_ge(ew_st, 64 * NG)

        @block.tensor
        def _(pe):
            def shared_gu(s, q, f):
                t = 4 * s + f
                if f >= 2:
                    pe.wait_ge(ht_done, t - 1)
                else:
                    after(pe, d_ev, 4 * s - 2 + 2 * f)
                if f == 0:
                    pe.wait_ge(t_ev, 4 * s + 4)
                g, u = gb[2 * (f % 2)], gb[2 * (f % 2) + 1]
                for dst, w in ((g, wgp), (u, wup)):
                    mm = parts(pe, dst[:, :], [([a[:, k, f * P:(f + 1) * P] for a in w], [a[:, k, :] for a in xT[q]])
                                               for k in range(KD)])
                mm.then_inc(f_done, 1)

            def shared_down(s, j):
                if j == 0:
                    pe.wait_ge(h_done, 4 * s + 4)
                mm = parts(pe, gb[j][:, :], [([a[:, k, j * P:(j + 1) * P] for a in h], [a[:, k, :] for a in wdp])
                                             for k in range(FC)])
                mm.then_inc(d_done, 1)

            def turn(n, q):
                pe.wait_ge(xn_done, n + 1)
                after(pe, qk_done, n)
                for j in range(GT):
                    after(pe, t_ev, 4 * n + j - 1)
                    for k in range(KD):
                        mm = pe.transpose(tb[j % 2][:, k * P:(k + 1) * P], xn4[:, j, k * P:(k + 1) * P], ident[:, :])
                    mm.then_inc(t_done, 1)

            def logits(n, q):
                pe.wait_ge(t_ev, 4 * n + 4)
                after(pe, v_done, n)
                for j in range(GT):
                    mm = parts(pe, lb[:, j * (C + E):(j + 1) * (C + E)],
                               [([a[:, k, j * P:(j + 1) * P] for a in xT[q]], [a[:, k, :] for a in wcrp]) for k in range(KD)])
                mm.then_inc(l_done, 1)

            def turn_c(n):
                pe.wait_ge(cn_done, n + 1)
                hold(pe, pe_gate)
                for j in range(GT):
                    mm = pe.transpose(nb[0:C, j * P:(j + 1) * P], cn[:, j, :], ident[:, :])
                mm.then_inc(cT_done, 1)

            def positions(n):
                pe.wait_ge(mask_done, n + 1)
                for j in range(GT):
                    for i in range(j + 1):
                        pe.matmul(lb[:, j * E:(j + 1) * E], (before if i == j else ones)[:, :], mask[:, i, :],
                                  start=(i == 0), stop=(i == j))
                for i in range(GT):
                    mm = pe.matmul(lb[:, GT * E:(GT + 1) * E], ones[:, :], mask[:, i, :], start=(i == 0), stop=(i == GT - 1))
                mm.then_inc(pos_done, 1)

            def qkv(n):
                pe.wait_ge(ch_done, n + 1)
                pe.matmul(nb[:, :], wqk[:, :], chT[:, :], start=True, stop=True)
                pe.matmul(tb[0][:, :], wqks[:, :], chT[:, :], start=True, stop=True)
                pe.wait_ge(pos_ev, n + 1)
                for j in range(GT):
                    mm = pe.matmul(lb[:, j * C:(j + 1) * C], chT[:, j * P:(j + 1) * P], wv[:, :], start=True, stop=True)
                mm.then_inc(qkv_done, 1)

            def first():
                pe.wait_ge(consts, CONSTS)
                for k in range(KD):
                    mm = pe.matmul(nb[:, k * C:(k + 1) * C], ht[:, k * P:(k + 1) * P], wcT[:, :], start=True, stop=True)
                mm.then_inc(wc_done, 1)
                pe.wait_ge(split_done, 1)

            def step(s, n, q):
                if s is not None:
                    shared_gu(s, 1 - q, 0)
                if n is not None:
                    turn(n, q)
                if s is not None:
                    shared_gu(s, 1 - q, 1)
                if n is not None:
                    logits(n, q)
                if s is not None:
                    shared_gu(s, 1 - q, 2)
                if n is not None:
                    turn_c(n)
                    positions(n)
                if s is not None:
                    shared_gu(s, 1 - q, 3)
                if n is not None:
                    qkv(n)
                if s is not None:
                    for j in range(GT):
                        shared_down(s, j)

            run(pe, first, step)
            pe.wait_ge(idx_done, 1)
            for c in range(2):
                mm = pe.transpose(lb[0:1, c * HT:(c + 1) * HT], spot[0:HT, 0, c:c + 1], ident[0:HT, 0:HT])
            mm.then_inc(te_done, 1)
            pe.wait_ge(lf_done, 1)
            for c in range(2):
                mm = pe.transpose(nb[:, c * HT:(c + 1) * HT], listf[0:HT, c, :], ident[0:HT, 0:HT])
            mm.then_inc(li_done, 1)

        @block.scalar
        def _(act):
            def silu(s, f):
                t = 4 * s + f
                act.wait_ge(f_done, t + 1)
                after(act, ht_done, t - 1)
                act.activation(sg[f % 2][:, :], gb[2 * (f % 2)][:, :], ACT.Silu).then_inc(sg_done, 1)

            def hidden_high(s, f):
                act.wait_ge(ht_done, 4 * s + f + 1)
                if f == 0:
                    after(act, d_done, 4 * s)
                act.copy(h[0][:, f, :], ht[:, :]).then_inc(hh_done, 1)

            def expert_high(n, c):
                act.wait_ge(ew_in, 96 * n + 48 * c + 48)
                after(act, ew_st, 64 * n + 32 * c)
                act.copy(ewp[0][:, :], ew[:, :]).then_inc(ew_hi, 1)

            def first():
                act.wait_ge(consts, CONSTS)
                for (dst, _), src in ((wgp, xb4[0]), (wup, xb4[1]), (wdp, xn4)):
                    act.copy(dst[:, :, :], src[:, :, :]).then_inc(hi_done, 1)

            def step(s, n, q):
                if s is not None:
                    silu(s, 0)
                if n is not None:
                    for j in range(GT):
                        act.wait_ge(t_done, 4 * n + j + 1)
                        act.copy(xT[q][0][:, :, j * P:(j + 1) * P],
                                 tb[j % 2][:, :].rearrange("p (k t) -> p k t", k=KD)).then_inc(t_hi, 1)
                if s is not None:
                    hidden_high(s, 0)
                if n is not None:
                    expert_high(n, 0)
                if s is not None:
                    for f in range(1, FC):
                        silu(s, f)
                        hidden_high(s, f)
                if n is not None:
                    expert_high(n, 1)

            run(act, first, step)

        @block.vector
        def _(dve):
            LINKS = 18

            def linked(n, k):
                dve.wait_ge(chain, n * LINKS + k)

            def norm(n, q):
                dve.wait_ge(x_in[q], times(n, q) * 2 + 32)
                for j in range(GT):
                    i = dve.bn_stats(stx[:, j, :], x4[q][:, j, :])
                i.then_inc(chain, 1)
                linked(n, 1)
                hold(dve, dve_gate)
                for j in range(GT):
                    i = dve.bn_aggr(mvx[:, j, :], stx[:, j, :])
                i.then_inc(mvx_done, 1)
                after(dve, st_xn, 16 * n)
                after(dve, t_done, 4 * n)
                dve.wait_ge(rsx_done, n + 1)
                for j in range(GT):
                    i = dve.tensor_scalar(xn4[:, j, :], x4[q][:, j, :], mvx[:, j, 0:1], rsx[:, j:j + 1],
                                          ALU.subtract, ALU.mult)
                i.then_inc(xn_done, 1)

            def compressed(n):
                dve.wait_ge(l_done, n + 1)
                dve.tensor_copy(lc[:, :, :], lb[:, 0:GT * (C + E)].rearrange("p (j c) -> p j c", j=GT)).then_inc(chain, 1)
                linked(n, 2)
                for j in range(GT):
                    i = dve.bn_stats(stc[:, j, :], lc[:, j, 0:C])
                i.then_inc(chain, 1)
                linked(n, 3)
                hold(dve, dve_gate)
                for j in range(GT):
                    i = dve.bn_aggr(mvc[:, j, :], stc[:, j, :])
                i.then_inc(mvc_done, 1)

            def choose(n):
                rev = rt[:, 0:GT, :]
                lg = lc[:, :, C:C + E]
                wide = lambda ap: ap.unsqueeze(2).broadcast_to([P, GT, E])
                for c in range(2):
                    src = lg if c == 0 else rest[:, :, :]
                    o = 3 + 6 * c
                    dve.tensor_reduce(top[:, c, :], src, AX.X, ALU.max).then_inc(chain, 1)
                    linked(n, o + 1)
                    dve.tensor_tensor(eq[:, :, :], src, wide(top[:, c, :]), ALU.is_equal).then_inc(chain, 1)
                    linked(n, o + 2)
                    dve.tensor_tensor(pb[:, :, :], eq[:, :, :], rev, ALU.mult).then_inc(chain, 1)
                    linked(n, o + 3)
                    dve.tensor_reduce(pick[:, c, :], pb[:, :, :], AX.X, ALU.max).then_inc(chain, 1)
                    linked(n, o + 4)
                    dve.tensor_tensor(oh[:, c, :, :], rev, wide(pick[:, c, :]), ALU.is_equal).then_inc(chain, 1)
                    linked(n, o + 5)
                    if c == 0:
                        dve.scalar_tensor_tensor(out=rest[:, :, :], in0=oh[:, 0, :, :], scalar=-BIG, in1=lg,
                                                 op0=ALU.mult, op1=ALU.add).then_inc(chain, 1)
                        linked(n, 9)

            def mask_and_gap(n):
                after(dve, pos_done, n)
                dve.tensor_tensor(mask[:, :, :], oh[:, 0, :, :], oh[:, 1, :, :], ALU.add).then_inc(mask_done, 1)
                at = slice(n * GT, (n + 1) * GT) if isinstance(n, int) else bass.ds(n * GT, GT)
                dve.tensor_tensor(gap_all[:, at], top[:, 1, :], top[:, 0, :], ALU.subtract).then_inc(chain, 1)

            def normed(n):
                dve.wait_ge(rsc_done, n + 1)
                for j in range(GT):
                    i = dve.tensor_scalar(cn[:, j, :], lc[:, j, 0:C], mvc[:, j, 0:1], rsc[:, j:j + 1],
                                          ALU.subtract, ALU.mult)
                i.then_inc(cn_done, 1)

            def scaled(n):
                dve.wait_ge(cT_done, n + 1)
                dve.tensor_scalar(chT[:, :], nb[0:C, :], gam[:, 0:1], bet[:, 0:1], ALU.mult, ALU.add).then_inc(ch_done, 1)

            def slots(n, q):
                dve.wait_ge(pos_done, n + 1)
                dve.tensor_tensor(pb[:, :, :], lb[:, 0:GT * E].rearrange("p (j e) -> p j e", e=E),
                                  carry[:, :].unsqueeze(1).broadcast_to([P, GT, E]), ALU.add).then_inc(chain, 1)
                linked(n, 16)
                dve.tensor_tensor(carry[:, :], lb[:, GT * E:(GT + 1) * E], carry[:, :], ALU.add).then_inc(pos_ev, 1)
                for c in range(2):
                    i = dve.tensor_tensor(pk[:, c, :, :], oh[:, c, :, :], pb[:, :, :], ALU.mult)
                i.then_inc(chain, 1)
                linked(n, 17)
                for c in range(2):
                    i = dve.tensor_reduce(slotf[:, :, c], pk[:, c, :, :], AX.X, ALU.add)
                i.then_inc(chain, 1)
                linked(n, 18)
                after(dve, scattered[q], times(n, q) * 8)
                at = slice(n * GT, (n + 1) * GT) if isinstance(n, int) else bass.ds(n * GT, GT)
                dve.tensor_copy(tok[q][:, :], token[:, at])
                dve.tensor_copy(slot[q][:, :, :], slotf[:, :, :]).then_inc(slot_done, 1)
                dve.tensor_copy(slots_all[:, at, :], slotf[:, :, :])

            def roped(n, q):
                dve.wait_ge(qkv_done, n + 1)
                dve.tensor_tensor(t1[:, :], nb[:, :], cs[q][:, 0, :], ALU.mult)
                dve.tensor_tensor(t2[:, :], tb[0][:, :], cs[q][:, 1, :], ALU.mult).then_inc(rope_done, 1)
                after(dve, st_qkv[q], times(n, q) * 3)
                dve.tensor_copy(vs[q][:, :, 0:C], lb[:, 0:GT * C].rearrange("p (j c) -> p j c", j=GT)).then_inc(v_done, 1)
                dve.wait_ge(rope_done, n + 1)
                dve.tensor_tensor(qks[q][:, :], t1[:, :], t2[:, :], ALU.add).then_inc(qk_done, 1)

            def hidden(s, f):
                t = 4 * s + f
                dve.wait_ge(sg_done, t + 1)
                after(dve, h_done, t)
                dve.tensor_tensor(ht[:, :], gb[2 * (f % 2) + 1][:, :], sg[f % 2][:, :], ALU.mult).then_inc(ht_done, 1)

            def hidden_low(s, f):
                dve.wait_ge(hh_done, 4 * s + f + 1)
                dve.tensor_tensor(h[1][:, f, :], ht[:, :], value(h[0][:, f, :]), ALU.subtract).then_inc(h_done, 1)

            def turned_low(n, q):
                for j in range(GT):
                    dve.wait_ge(t_hi, 4 * n + j + 1)
                    cols = slice(j * P, (j + 1) * P)
                    dve.tensor_tensor(xT[q][1][:, :, cols], tb[j % 2][:, :].rearrange("p (k t) -> p k t", k=KD),
                                      value(xT[q][0][:, :, cols]), ALU.subtract).then_inc(t_ev, 1)

            def expert_low(n, c):
                dve.wait_ge(ew_hi, 2 * n + c + 1)
                dve.tensor_tensor(ewp[1][:, :], ew[:, :], value(ewp[0][:, :]), ALU.subtract).then_inc(ew_lo, 1)

            def added(s, q, j):
                if j == 0:
                    dve.wait_ge(xb_done, s + 1)
                dve.wait_ge(d_done, 4 * s + j + 1)
                dve.tensor_tensor(xb4[q][:, j, :], gb[j][:, :], xb4[q][:, j, :], ALU.add).then_inc(d_ev, 1)

            def first():
                dve.wait_ge(consts, CONSTS)
                dve.tensor_copy(before[:, :], tri[:, 0, :])
                dve.tensor_copy(carry[:, :], rt[:, GT, :])
                dve.memset(ones[:, :], 1.0)
                dve.memset(zeros[:, :], 0)
                dve.memset(halfs[:, :], -0.5)
                dve.memset(vs[0][:, :, C:CA], 1.0)
                dve.memset(vs[1][:, :, C:CA], 1.0).then_inc(setup, 1)
                dve.wait_ge(wc_done, 1)
                dve.tensor_copy(wcr[:, :, 0:C], nb[:, 0:KD * C].rearrange("p (k c) -> p k c", k=KD)).then_inc(wc_ev, 1)
                dve.wait_ge(wc_ev, 1)
                dve.tensor_copy(wcrp[0][:, :, :], wcr[:, :, :]).then_inc(wc_ev, 1)
                dve.wait_ge(wc_ev, 2)
                dve.tensor_tensor(wcrp[1][:, :, :], wcr[:, :, :], value(wcrp[0][:, :, :]), ALU.subtract)
                for i, ((high, low), src) in enumerate(((wgp, xb4[0]), (wup, xb4[1]), (wdp, xn4))):
                    dve.wait_ge(hi_done, i + 1)
                    m = dve.tensor_tensor(low[:, :, :], src[:, :, :], value(high[:, :, :]), ALU.subtract)
                m.then_inc(split_done, 1)
                dve.wait_ge(split_done, 1)
                norm(0, 0)

            def step(s, n, q):
                if s is not None:
                    hidden(s, 0)
                if n is not None:
                    turned_low(n, q)
                if s is not None:
                    hidden_low(s, 0)
                    hidden(s, 1)
                if n is not None:
                    expert_low(n, 0)
                if s is not None:
                    hidden_low(s, 1)
                if n is not None:
                    compressed(n)
                    choose(n)
                    mask_and_gap(n)
                    normed(n)
                if s is not None:
                    hidden(s, 2)
                if n is not None:
                    scaled(n)
                if s is not None:
                    hidden_low(s, 2)
                if n is not None:
                    slots(n, q)
                if s is not None:
                    hidden(s, 3)
                    hidden_low(s, 3)
                if n is not None:
                    roped(n, q)
                if s is not None:
                    added(s, 1 - q, 0)
                    added(s, 1 - q, 1)
                if n is not None:
                    expert_low(n, 1)
                    if not (isinstance(n, int) and n == NG - 1):
                        norm(n + 1, 1 - q)
                if s is not None:
                    added(s, 1 - q, 2)
                    added(s, 1 - q, 3)

            run(dve, first, step)

            links = [NG * LINKS]

            def link(i):
                links[0] += 1
                i.then_inc(chain, 1)
                dve.wait_ge(chain, links[0])

            dve.wait_ge(pos_ev, NG)
            link(dve.tensor_tensor(cnt[:, 0, :], carry[:, :], rt[:, GT, :], ALU.subtract))
            link(dve.tensor_scalar(cnt[:, 1, :], cnt[:, 0, :], float(RT - 1), None, ALU.add))
            link(dve.tensor_copy(cnti[:, 0, :], cnt[:, 1, :]))
            link(dve.tensor_scalar(cnti[:, 1, :], cnti[:, 0, :], RT.bit_length() - 1, None, ALU.logical_shift_right))
            link(dve.tensor_copy(cnt[:, 2, :], cnti[:, 1, :]))
            tiles_b = lambda p, n: cnt[0:p, 2, :].unsqueeze(1).broadcast_to([p, n, E])
            tri_b = x4[1][:, :, :].rearrange("p a b -> p (a b)")[:, 0:E * E].rearrange("p (a b) -> p a b", b=E)
            link(dve.tensor_tensor(tri_b, upto[:, :, :], tiles_b(P, E), ALU.mult))
            link(dve.tensor_reduce(cnt[:, 3, :], tri_b, AX.X, ALU.add))
            link(dve.tensor_tensor(cnt[:, 4, :], cnt[:, 3, :], cnt[:, 2, :], ALU.subtract))
            link(dve.tensor_scalar(cnt[:, 5, :], cnt[:, 4, :], float(RT), None, ALU.mult))

            slots = slots_all[:, :, :].rearrange("p t c -> p (t c)")
            link(dve.tensor_scalar(sei[:, :], slots, REGION.bit_length() - 1, None, ALU.logical_shift_right))
            link(dve.tensor_copy(se[:, :], sei[:, :]))
            link(dve.scalar_tensor_tensor(out=sp_[:, :], in0=se[:, :], scalar=-float(REGION), in1=slots,
                                          op0=ALU.mult, op1=ALU.add))
            hot = x4[0][:, :, :].rearrange("p a b -> p (a b)").rearrange("p (s e) -> p s e", e=E)
            rev_b = rt[:, 0, :].unsqueeze(1).broadcast_to([P, NS, E])
            link(dve.tensor_scalar(se[:, :], se[:, :], -1.0, float(E), ALU.mult, ALU.add))
            link(dve.tensor_tensor(hot, se[:, :].unsqueeze(2).broadcast_to([P, NS, E]), rev_b, ALU.is_equal))
            link(dve.tensor_tensor(hot, hot, cnt[:, 5, :].unsqueeze(1).broadcast_to([P, NS, E]), ALU.mult))
            link(dve.tensor_reduce(se[:, :], hot, AX.X, ALU.add))
            link(dve.tensor_tensor(slots, se[:, :], sp_[:, :], ALU.add))

            wide = lambda ap: ap.unsqueeze(1).broadcast_to([P, 2, E])
            link(dve.tensor_tensor(half[:, :, :], tile_p[:, :].unsqueeze(2).broadcast_to([P, 2, E]), wide(cnt[:, 3, :]), ALU.is_ge))
            link(dve.tensor_reduce(spot[:, 0, :], half[:, :, :], AX.X, ALU.add))
            link(dve.tensor_tensor(half[:, :, :], half[:, :, :], wide(cnt[:, 2, :]), ALU.mult))
            link(dve.tensor_reduce(spot[:, 1, :], half[:, :, :], AX.X, ALU.add))
            link(dve.tensor_tensor(spot[:, 2, :], tile_p[:, :], spot[:, 1, :], ALU.subtract))
            link(dve.scalar_tensor_tensor(out=spot[:, 3, :], in0=spot[:, 0, :], scalar=float(REGION // RT),
                                          in1=spot[:, 2, :], op0=ALU.mult, op1=ALU.add))
            link(dve.tensor_scalar(spot[:, 1, :], spot[:, 3, :], float(E * REGION // RT), None, ALU.min))
            dve.tensor_copy(spoti[:, :], spot[:, 1, :]).then_inc(idx_done, 1)

            dve.wait_ge(te_done, 1)
            link(dve.tensor_scalar(small[:, :], lb[0:1, 0:NRT], float(E - 1), 1.0, ALU.min, ALU.add))
            link(dve.tensor_copy(table[:, 0, :], small[:, :]))
            link(dve.tensor_scalar(table[:, 1, :], table[:, 0, :], 1, None, ALU.bitwise_and))
            link(dve.tensor_scalar(cnt[:, 4, :], cnt[:, 3, :], 1.0, None, ALU.add))
            link(dve.tensor_copy(upto_tiles[:, :], cnt[0:1, 4, :]))

            dve.wait_ge(listed_in, 32)
            dve.tensor_copy(listf[0:HT, :, :], listed[0:HT, :, :]).then_inc(lf_done, 1)
            dve.wait_ge(li_done, 1)
            link(dve.tensor_copy(ids_all[:, :], nb[:, 0:NRT]))

        @block.gpsimd
        def _(pool):
            def root(n, per, mv, rs, waited, done):
                pool.wait_ge(waited, n + 1)
                hold(pool, pool_gate)
                pool.tensor_scalar(rs[:, :], mv[:, :, 1], LN_EPS, None, ALU.add).then_inc(pool_chain, 1)
                pool.wait_ge(pool_chain, 2 * n + 1 + per)
                pool.tensor_tensor(rs[:, :], rs[:, :], halfs[:, :], ALU.pow).then_inc(done, 1)

            def norm(n, q):
                root(n, 0, mvx, rsx, mvx_done, rsx_done)
                after(pool, st_base[q], times(n, q))
                for j in range(GT):
                    i = pool.tensor_tensor(xb4[q][:, j, :], x4[q][:, j, :], bias[:, :], ALU.add)
                i.then_inc(xb_done, 1)

            def first():
                pool.wait_ge(split_done, 1)
                norm(0, 0)

            def step(s, n, q):
                if n is None:
                    return
                root(n, 1, mvc, rsc, mvc_done, rsc_done)
                pool.wait_ge(slot_done, n + 1)
                pool.wait_ge(cleared, 48)
                hold(pool, pool_gate)
                for j in range(GT):
                    for c in range(2):
                        pool.indirect_dma_start(list_d[:, :], bass.IndirectOffsetOnAxis(ap=slot[q][:, j, c:c + 1], axis=0),
                                                tok[q][:, j:j + 1], None).then_inc(scattered[q], 16)
                if not (isinstance(n, int) and n == NG - 1):
                    norm(n + 1, 1 - q)

            run(pool, first, step)
            for q in range(2):
                pool.wait_ge(scattered[q], 128 * NG // 2)
            pool.wait_ge(idx_done, 1)
            for c in range(2):
                pool.indirect_dma_start(listed[0:HT, c, :], None, list_d.rearrange("(r c) o -> r (c o)", c=P),
                                        bass.IndirectOffsetOnAxis(ap=spoti[0:HT, c:c + 1], axis=0)).then_inc(listed_in, 16)
            pool.wait_ge(listed_in, 32)


def routed(nc, ew_d, xn_d, rows_out, ident, table, upto_tiles, ids_all):
    with ExitStack() as ctx:
        sb = lambda name, shape, dt=F32: ctx.enter_context(nc.sbuf_tensor(name, shape, dt))
        ps = lambda name: ctx.enter_context(nc.psum_tensor(name, [P, 512], F32))
        sem = lambda name: ctx.enter_context(nc.semaphore(name))
        pair = lambda name: [sem(name + "0"), sem(name + "1")]
        FK = FE // P

        w = sb("w", [P, 2, 2, 2, EH], F32R)
        ids = [sb(f"ids_{i}", [P, 1], I32) for i in range(AHEAD)]
        rows = [sb(f"rows_{i}", [P, D]) for i in range(AHEAD)]
        rT = [[sb(f"rT_{i}{c}", [P, KD, RT], F32R) for c in "hl"] for i in range(2)]
        hT = [[sb(f"hT_{i}{c}", [P, FK, RT], F32R) for c in "hl"] for i in range(2)]
        h = [sb(f"eh_{i}", [P, FE]) for i in range(2)]
        sg = [sb(f"esg_{i}", [P, FE]) for i in range(2)]
        res = [sb(f"res_{i}", [P, D]) for i in range(2)]
        tb, gu, hb, db = [[ps(f"e{n}{i}") for i in range(2)] for n in ("tb", "gu", "hb", "db")]

        w_in, w_ready = pair("w_in"), sem("w_ready")
        ids_done, rows_in, stored = sem("ids_done"), [sem(f"rows_in{i}") for i in range(AHEAD)], pair("rstored")
        t_done, t_hi, t_lo = sem("et_done"), sem("et_hi"), sem("et_lo")
        gu_done, sg_done, h_done = sem("egu_done"), sem("esg_done"), sem("eh_done")
        hb_done, hT_hi, hT_lo = sem("ehb_done"), sem("ehT_hi"), sem("ehT_lo")
        d_done, d_ev = sem("ed_done"), sem("ed_ev")
        pool_gate, sp_gate = sem("epool_gate"), sem("esp_gate")

        def run(eng, step):
            for r in range(AHEAD):
                step(r, r)
            with eng.Fori(1, NRT // AHEAD - 1) as i:
                for r in range(AHEAD):
                    step(AHEAD * i + r, r)
            for r in range(AHEAD):
                step(NRT - AHEAD + r, r)

        def uses(t, r, of=2):
            return 16 // of * (t - r % of)

        known = lambda t, f: isinstance(t, int) and f(t)

        block = ctx.enter_context(nc.Block())

        @block.sync
        def _(sp):
            def load(e, q, at):
                if at is not None:
                    done = sp.value_load(upto_tiles[0:1, at], min_val=1, max_val=NRT + 1)
                    sp.wait_ge(d_ev, done)
                    hold(sp, sp_gate)
                src = ew_d[e] if isinstance(e, int) else ew_d[bass.ds(e, 1)].rearrange("o p a c f -> (o p) a c f")
                for a in range(2):
                    for c in range(2):
                        sp.dma_start(value(w[:, 1 - q, a, c, :]), src[:, a, c, :]).then_inc(w_in[q], 16)
                sp.wait_ge(w_in[q], 32 * (e - q) + 64)
                sp.sem_inc(w_ready, 1)

            load(0, 0, None)
            load(1, 1, None)
            with sp.Fori(1, E // 2) as i:
                load(2 * i, 0, bass.ds(2 * i - 2, 1))
                load(2 * i + 1, 1, bass.ds(2 * i - 1, 1))

        @block.tensor
        def _(pe):
            def turn(t, r):
                pe.wait_ge(rows_in[r], uses(t, r, AHEAD) + 16)
                after(pe, t_lo, t - 1)
                for k in range(KD):
                    mm = pe.transpose(tb[r % 2][:, k * P:(k + 1) * P], rows[r][:, k * P:(k + 1) * P], ident[:, :])
                mm.then_inc(t_done, 1)

            this_buffer, last_buffer = pe.alloc_register("this_buffer"), pe.alloc_register("last_buffer")

            def find_buffer(t):
                at = slice(t, t + 1) if isinstance(t, int) else bass.ds(t, 1)
                pe.reg_mov(this_buffer, pe.value_load(table[0:1, 1, at], min_val=0, max_val=1))

            def weights(b, a, c, lo):
                return w[:, bass.ds(b, 1), a, c, lo:lo + D].rearrange("p o f -> p (o f)")

            def gate_up(t, q):
                b = pe.snap(this_buffer, min_val=0, max_val=1)
                pe.wait_ge(t_lo, t + 1)
                after(pe, h_done, t - 1)
                mm = parts(pe, gu[q][:, :], [([a[:, k, :] for a in rT[q]],
                                              [weights(b, a, k // 2, k % 2 * 2 * FE) for a in range(2)]) for k in range(KD)])
                mm.then_inc(gu_done, 1)

            def down(t, q):
                b = pe.snap(last_buffer, min_val=0, max_val=1)
                pe.wait_ge(hT_lo, t + 1)
                if not known(t, lambda t: t < 2):
                    pe.wait_ge(d_ev, t)
                mm = parts(pe, db[q][:, :], [([a[:, k, :] for a in hT[q]],
                                              [weights(b, a, k, 4 * FE) for a in range(2)]) for k in range(FK)])
                mm.then_inc(d_done, 1)

            def turn_hidden(t, q):
                pe.wait_ge(h_done, t + 1)
                after(pe, hT_lo, t - 1)
                for k in range(FK):
                    mm = pe.transpose(hb[q][:, k * P:(k + 1) * P], h[q][:, k * P:(k + 1) * P], ident[:, :])
                mm.then_inc(hb_done, 1)

            def step(t, r):
                q = r % 2
                gate_up(t, q)
                if not known(t, lambda t: t == 0):
                    down(t - 1, 1 - q)
                pe.reg_mov(last_buffer, this_buffer)
                if not known(t, lambda t: t == NRT - 1):
                    find_buffer(t + 1)
                if not known(t, lambda t: t >= NRT - 2):
                    turn(t + 2, (r + 2) % AHEAD)
                turn_hidden(t, q)

            find_buffer(0)
            turn(0, 0)
            turn(1, 1)
            run(pe, step)
            down(NRT - 1, 1)

        @block.scalar
        def _(act):
            def turned(t, q):
                act.wait_ge(t_done, t + 1)
                after(act, gu_done, t - 1)
                act.copy(rT[q][0][:, :, :], tb[q][:, :].rearrange("p (k t) -> p k t", k=KD)).then_inc(t_hi, 1)

            def silu(t, q):
                act.wait_ge(gu_done, t + 1)
                after(act, h_done, t - 1)
                act.activation(sg[q][:, :], gu[q][:, 0:FE], ACT.Silu).then_inc(sg_done, 1)

            def hidden_turned(t, q):
                act.wait_ge(hb_done, t + 1)
                after(act, d_done, t - 1)
                act.copy(hT[q][0][:, :, :], hb[q][:, 0:FE].rearrange("p (k t) -> p k t", k=FK)).then_inc(hT_hi, 1)

            def downed(t, q):
                act.wait_ge(d_done, t + 1)
                after(act, stored[q], uses(t, q))
                act.copy(res[q][:, :], db[q][:, :]).then_inc(d_ev, 1)

            def store(t, q):
                act.wait_ge(d_ev, t + 2)
                dst = rows_out[t * RT:(t + 1) * RT, :] if isinstance(t, int) else rows_out[bass.ds(t * RT, RT), :]
                act.dma_start(dst, res[q][:, :]).then_inc(stored[q], 16)

            def step(t, r):
                q = r % 2
                silu(t, q)
                if not known(t, lambda t: t < 2):
                    store(t - 2, q)
                if not known(t, lambda t: t >= NRT - 2):
                    turned(t + 2, q)
                if not known(t, lambda t: t == 0):
                    downed(t - 1, 1 - q)
                hidden_turned(t, q)

            act.sem_inc(d_ev, 1)
            turned(0, 0)
            turned(1, 1)
            run(act, step)
            store(NRT - 2, 0)
            downed(NRT - 1, 1)
            store(NRT - 1, 1)
            for q in range(2):
                act.wait_ge(stored[q], 16 * NRT // 2)

        @block.vector
        def _(dve):
            def turned(t, q):
                dve.wait_ge(t_hi, t + 1)
                dve.tensor_tensor(rT[q][1][:, :, :], tb[q][:, :].rearrange("p (k t) -> p k t", k=KD),
                                  value(rT[q][0][:, :, :]), ALU.subtract).then_inc(t_lo, 1)

            def hidden(t, q):
                dve.wait_ge(sg_done, t + 1)
                after(dve, hb_done, t - 1)
                dve.tensor_tensor(h[q][:, :], gu[q][:, FE:2 * FE], sg[q][:, :], ALU.mult).then_inc(h_done, 1)

            def hidden_turned(t, q):
                dve.wait_ge(hT_hi, t + 1)
                dve.tensor_tensor(hT[q][1][:, :, :], hb[q][:, 0:FE].rearrange("p (k t) -> p k t", k=FK),
                                  value(hT[q][0][:, :, :]), ALU.subtract).then_inc(hT_lo, 1)

            def step(t, r):
                q = r % 2
                hidden(t, q)
                if not known(t, lambda t: t >= NRT - 2):
                    turned(t + 2, q)
                hidden_turned(t, q)

            turned(0, 0)
            turned(1, 1)
            run(dve, step)

        @block.gpsimd
        def _(pool):
            def gather(t, r):
                after(pool, rows_in[r], uses(t, r, AHEAD))
                after(pool, t_done, t - AHEAD + 1)
                at = slice(t, t + 1) if isinstance(t, int) else bass.ds(t, 1)
                pool.wait_ge(w_ready, pool.value_load(table[0:1, 0, at], min_val=1, max_val=E))
                hold(pool, pool_gate)
                pool.tensor_copy(ids[r][:, :], ids_all[:, at]).then_inc(ids_done, 1)
                pool.wait_ge(ids_done, t + 1)
                hold(pool, pool_gate)
                pool.indirect_dma_start(rows[r][:, :], None, xn_d[:, :],
                                        bass.IndirectOffsetOnAxis(ap=ids[r][:, :], axis=0)).then_inc(rows_in[r], 16)

            run(pool, gather)


def attend(nc, w_kv, w_c2l, w_outT, tri_in, q_d, k_d, v_d, base_d, rows_out, out, ident, slots_all, gap_all):
    with ExitStack() as ctx:
        sb = lambda name, shape, dt=F32: ctx.enter_context(nc.sbuf_tensor(name, shape, dt))
        ps = lambda name: ctx.enter_context(nc.psum_tensor(name, [P, 512], F32))
        sem = lambda name: ctx.enter_context(nc.semaphore(name))
        pair = lambda name: [sem(name + "0"), sem(name + "1")]
        KB = T // P
        NP, NSC = 4, 3
        SCALE = C ** -0.5

        qa, ka = [[sb(f"{n}_{i}", [P, GROUP]) for i in range(2)] for n in ("qa", "ka")]
        qh = [sb(f"qh_{i}", [P, GROUP], F32R) for i in range(2)]
        qlm = [sb(f"qlm_{i}", [CA, GROUP], F32R) for i in range(2)]
        khl = sb("khl", [P, N], F32R); kh1 = sb("kh1", [CA, N], F32R)
        va = sb("va", [P, NG, GT, CA])
        ones = sb("ones3", [1, T])
        mo = sb("mo", [C, D]); wz = sb("wz", [LAT, D]); wo = sb("wo", [LAT, D]); wc = sb("wc", [LAT, C])
        tri = sb("tri3", [P, 2, P]); future = sb("future", [P, P], BF16); identb = sb("identb", [P, P], BF16)
        w_all = sb("w_all", [P, 2, NG * GT]); den = sb("den", [P, NG * GT])
        mx = sb("mx", [P, GT, QB]); mcol = sb("mcol", [P, GT, CA]); last = sb("last", [CA, 1])
        pr = [sb(f"pr_{i}", [P, GROUP]) for i in range(NP)]
        oT = sb("oT", [CA, GROUP]); lr = sb("lr", [P, GT])
        base = [sb(f"base_{i}", [P, GT, D]) for i in range(2)]
        got = [sb(f"got_{i}", [P, 2, GT, D]) for i in range(2)]

        mb = [ps("mb0"), ps("mb1")]
        sc = [ps(f"sc{i}") for i in range(NSC)]
        ob, pj, nb = ps("ob"), ps("pj"), ps("anb")

        const_in, qkv_in, a_ready, highs, lows = sem("const_in"), pair("qkv_in"), sem("a_ready"), sem("highs"), sem("lows")
        sum_w, mo_done, mo_ev, w_exp, chain = sem("sum_w"), sem("mo_done"), sem("mo_ev"), sem("w_exp"), sem("a_chain")
        m_done, m_red, mc_done, mt_done, mrow = sem("m_done"), sem("m_red"), sem("mc_done"), sem("mt_done"), sem("mrow")
        s_done, e_done, sel_done, pv_done = sem("s_done"), sem("e_done"), sem("sel_done"), sem("pv_done")
        o_ev, l_done, l_ev, p_done, p_ev = sem("o_ev"), sem("al_done"), sem("l_ev"), sem("p_done"), sem("p_ev")
        blk_done, base_in, got_in, out_st = sem("blk_done"), pair("base_in"), pair("got_in"), pair("out_st")

        base_g = base_d.rearrange("(g j p) d -> g p j d", j=GT, p=P)
        out_g = out.rearrange("b t d -> (b t) d").rearrange("(g j p) d -> g p j d", j=GT, p=P)
        CONSTS = 16 * 4

        units = [GT * (n % QB + 1) for n in range(NG)]
        first_unit = [sum(units[:n]) for n in range(NG + 1)]

        def steps(n):
            ahead = units[n + 1] if n + 1 < NG else 0
            for kb in range(units[n]):
                lo = kb
                hi = kb + 1 if kb + 1 < units[n] else ahead
                yield kb, range(min(lo, ahead), min(hi, ahead))

        block = ctx.enter_context(nc.Block())

        @block.sync
        def _(sp):
            for dst, src in ((wz[:, :], w_kv), (wo[:, :], w_outT), (wc[:, :], w_c2l),
                             (tri[:, :, :], tri_in.rearrange("a p c -> p a c"))):
                sp.dma_start(dst, src).then_inc(const_in, 16)

            def load_base(n):
                after(sp, out_st[n % 2], 16 * (n // 2))
                sp.dma_start(base[n % 2][:, :, :], base_g[n]).then_inc(base_in[n % 2], 16)

            def load_block(n):
                q, at = n % 2, slice(n * GROUP, (n + 1) * GROUP)
                after(sp, lows, n - 1)
                for half in (slice(0, C), slice(C, P)):
                    sp.dma_start(qa[q][half, :], q_d[:, at]).then_inc(qkv_in[q], 16)
                    sp.dma_start(ka[q][half, :], k_d[:, at]).then_inc(qkv_in[q], 16)
                sp.dma_start(va[:, n, :, :].rearrange("p j c -> p (j c)"), v_d[n]).then_inc(qkv_in[q], 16)

            load_block(0)
            for n in range(NG):
                if n + 1 < NG:
                    load_block(n + 1)
                load_base(n)
                if n:
                    sp.wait_ge(blk_done, n)
                    sp.dma_start(out_g[n - 1], base[(n - 1) % 2][:, :, :]).then_inc(out_st[(n - 1) % 2], 16)
            sp.wait_ge(blk_done, NG)
            sp.dma_start(out_g[NG - 1], base[(NG - 1) % 2][:, :, :]).then_inc(out_st[(NG - 1) % 2], 16)
            for q in range(2):
                sp.wait_ge(out_st[q], 16 * NG // 2)

        @block.tensor
        def _(pe):
            def max_scores(n, v):
                m, (j, c) = n % QB, divmod(v, n % QB + 1)
                g = first_unit[n] + v
                if v == 0:
                    pe.wait_ge(lows, n + 1)
                after(pe, m_red, g - 1)
                w = GROUP if c < m else P * (j + 1)
                key = n // QB * T + c * GROUP
                mm = pe.matmul(mb[g % 2][:, 0:w], qh[n % 2][0:C, j * P:(j + 1) * P], khl[0:C, key:key + w],
                               start=True, stop=(c < m))
                if c == m:
                    mm = pe.matmul(mb[g % 2][:, w - P:w], identb[:, :], future[:, :], start=False, stop=True)
                mm.then_inc(m_done, 1)

            def turn_max(n):
                pe.wait_ge(mc_done, n + 1)
                after(pe, l_ev, n - 1)
                for j in range(GT):
                    mm = pe.matmul(nb[0:CA, j * P:(j + 1) * P], mcol[:, j, :], ident[:, :], start=True, stop=True)
                mm.then_inc(mt_done, 1)

            def scores(n, kb):
                u, m = first_unit[n] + kb, n % QB
                off = max(0, kb - GT * m) * P
                if kb == 0:
                    pe.wait_ge(mrow, n + 1)
                after(pe, e_done, u - NSC + 1)
                key = n // QB * T + kb * P
                pe.matmul(sc[u % NSC][:, off:GROUP], khl[:, key:key + P], qh[n % 2][:, off:GROUP], start=True, stop=False)
                pe.matmul(sc[u % NSC][:, off:GROUP], kh1[:, key:key + P], qlm[n % 2][:, off:GROUP],
                          start=False, stop=True).then_inc(s_done, 1)

            def outputs(n, kb):
                u, m = first_unit[n] + kb, n % QB
                d = kb - GT * m
                off = max(0, d) * P
                pe.wait_ge(e_done, u + 1)
                if d >= 0:
                    pe.wait_ge(sel_done, GT * n + d + 1)
                if kb == 0:
                    after(pe, o_ev, n)
                pe.matmul(ob[0:CA, off:GROUP], va[:, n // QB * QB + kb // GT, kb % GT, :], pr[u % NP][:, off:GROUP],
                          start=(kb == 0), stop=(kb == units[n] - 1)).then_inc(pv_done, 1)

            def project(n, j):
                if j == 0:
                    pe.wait_ge(o_ev, n + 1)
                    pe.wait_ge(mrow, min(n + 2, NG))
                    for i in range(GT):
                        mm = pe.matmul(nb[:, i:i + 1], oT[:, i * P:(i + 1) * P], last[:, :], start=True, stop=True)
                    mm.then_inc(l_done, 1)
                after(pe, p_ev, GT * n + j)
                pe.matmul(pj[:, :], oT[0:C, j * P:(j + 1) * P], mo[:, :], start=True, stop=True).then_inc(p_done, 1)

            pe.wait_ge(sum_w, 1)
            pe.matmul(pj[0:C, :], wc[:, :], wz[:, :], start=True, stop=True).then_inc(mo_done, 1)
            pe.wait_ge(mo_ev, 1)
            pe.wait_ge(a_ready, 2)
            for v in range(units[0]):
                max_scores(0, v)
            turn_max(0)
            for n in range(NG):
                for kb, ahead in steps(n):
                    scores(n, kb)
                    for v in ahead:
                        max_scores(n + 1, v)
                    if kb >= 2:
                        outputs(n, kb - 2)
                    if n and kb < GT:
                        project(n - 1, kb)
                outputs(n, units[n] - 2)
                outputs(n, units[n] - 1)
                if n + 1 < NG:
                    turn_max(n + 1)
            for j in range(GT):
                project(NG - 1, j)

        @block.scalar
        def _(act):
            def highs_of(n):
                q, at = n % 2, slice(n * GROUP, (n + 1) * GROUP)
                act.wait_ge(qkv_in[q], 80 * (n // 2) + 80)
                if n >= 2:
                    act.wait_ge(pv_done, first_unit[n - 1])
                act.copy(khl[:, at], ka[q][:, :])
                act.copy(kh1[0:C, at], ka[q][0:C, :])
                act.copy(qh[q][:, :], qa[q][:, :]).then_inc(highs, 1)

            act.activation(w_all[:, 1, :], gap_all[:, :], ACT.Exp).then_inc(w_exp, 1)
            act.wait_ge(mo_done, 1)
            act.copy(mo[:, :], pj[0:C, :]).then_inc(mo_ev, 1)
            highs_of(0)
            for n in range(NG):
                m = n % QB
                for kb in range(units[n]):
                    if kb == 0 and n + 1 < NG:
                        highs_of(n + 1)
                    u = first_unit[n] + kb
                    off = max(0, kb - GT * m) * P
                    act.wait_ge(s_done, u + 1)
                    after(act, pv_done, u - NP + 1)
                    act.activation(pr[u % NP][:, off:GROUP], sc[u % NSC][:, off:GROUP], ACT.Exp,
                                   scale=SCALE).then_inc(e_done, 1)
                act.wait_ge(pv_done, first_unit[n + 1])
                after(act, p_done, GT * n)
                act.copy(oT[:, :], ob[0:CA, :]).then_inc(o_ev, 1)

        @block.vector
        def _(dve):
            links = [0]

            def link(i):
                links[0] += 1
                i.then_inc(chain, 1)
                dve.wait_ge(chain, links[0])

            def lows_of(n):
                q, at = n % 2, slice(n * GROUP, (n + 1) * GROUP)
                dve.wait_ge(highs, n + 1)
                dve.tensor_tensor(khl[C:P, at], ka[q][C:P, :], value(khl[C:P, at]), ALU.subtract)
                dve.tensor_tensor(qlm[q][0:C, :], qa[q][0:C, :], value(qh[q][0:C, :]), ALU.subtract).then_inc(lows, 1)

            def reduce_max(n, v):
                m, (j, c) = n % QB, divmod(v, n % QB + 1)
                g = first_unit[n] + v
                w = GROUP if c < m else P * (j + 1)
                dve.wait_ge(m_done, g + 1)
                dve.tensor_reduce(mx[:, j, c:c + 1], mb[g % 2][:, 0:w], AX.X, ALU.max).then_inc(m_red, 1)

            def negated_max(n):
                m = n % QB
                dve.wait_ge(m_red, first_unit[n + 1])
                after(dve, mt_done, n)
                dve.tensor_reduce(mcol[:, :, C], mx[:, :, 0:m + 1], AX.X, ALU.max, negate=True).then_inc(mc_done, 1)
                dve.wait_ge(mt_done, n + 1)
                dve.tensor_copy(qlm[n % 2][C:CA, :], nb[C:CA, :]).then_inc(mrow, 1)

            def combine(n, j):
                q, t = n % 2, GT * n + j
                if j == 0:
                    dve.wait_ge(l_done, n + 1)
                    link(dve.reciprocal(lr[:, :], nb[:, 0:GT]))
                    dve.wait_ge(base_in[q], 16 * (n // 2) + 16)
                    dve.wait_ge(got_in[q], 128 * (n // 2) + 128)
                    dve.sem_inc(l_ev, 1)
                dve.wait_ge(p_done, t + 1)
                row = base[q][:, j, :]
                dve.scalar_tensor_tensor(out=row, in0=pj[:, :], scalar=lr[:, j:j + 1], in1=row,
                                         op0=ALU.mult, op1=ALU.add).then_inc(p_ev, 1)
                dve.wait_ge(p_ev, t + 1)
                link(dve.scalar_tensor_tensor(out=row, in0=got[q][:, 0, j, :], scalar=w_all[:, 0, t:t + 1], in1=row,
                                              op0=ALU.mult, op1=ALU.add))
                i = dve.scalar_tensor_tensor(out=row, in0=got[q][:, 1, j, :], scalar=w_all[:, 1, t:t + 1], in1=row,
                                             op0=ALU.mult, op1=ALU.add)
                if j == GT - 1:
                    i.then_inc(blk_done, 1)

            dve.wait_ge(const_in, CONSTS)
            dve.tensor_tensor(wz[:, :], wz[:, :], wo[:, :], ALU.add).then_inc(sum_w, 1)
            dve.tensor_copy(future[:, :], tri[:, 1, :])
            dve.tensor_copy(identb[:, :], ident[:, :])
            dve.memset(mcol[:, :, :], 0.0)
            dve.memset(last[0:C, :], 0.0)
            dve.memset(last[C:CA, :], 1.0)
            dve.memset(ones[:, :], 1.0).then_inc(a_ready, 1)
            dve.wait_ge(a_ready, 1)
            for b in range(B):
                i = dve.tensor_copy(kh1[C:CA, b * T:(b + 1) * T], ones[:, :])
            i.then_inc(a_ready, 1)
            dve.wait_ge(w_exp, 1)
            link(dve.tensor_scalar(den[:, :], w_all[:, 1, :], 1.0, None, ALU.add))
            link(dve.reciprocal(w_all[:, 0, :], den[:, :]))
            link(dve.tensor_tensor(w_all[:, 1, :], w_all[:, 1, :], w_all[:, 0, :], ALU.mult))
            lows_of(0)
            for v in range(units[0]):
                reduce_max(0, v)
            negated_max(0)
            for n in range(NG):
                if n + 1 < NG:
                    lows_of(n + 1)
                for kb, ahead in steps(n):
                    for v in ahead:
                        reduce_max(n + 1, v)
                    if n and kb < GT:
                        combine(n - 1, kb)
                if n + 1 < NG:
                    negated_max(n + 1)
            for j in range(GT):
                combine(NG - 1, j)

        @block.gpsimd
        def _(pool):
            def gather(n):
                q = n % 2
                after(pool, blk_done, n - 1)
                for j in range(GT):
                    for c in range(2):
                        pool.indirect_dma_start(got[q][:, c, j, :], None, rows_out[:, :],
                                                bass.IndirectOffsetOnAxis(ap=slots_all[:, GT * n + j, c:c + 1], axis=0)
                                                ).then_inc(got_in[q], 16)

            gather(0)
            for n in range(NG):
                for d in range(GT):
                    u = first_unit[n] + GT * (n % QB) + d
                    part = pr[u % NP][:, d * P:(d + 1) * P]
                    pool.wait_ge(e_done, u + 1)
                    pool.affine_select(out=part, in_=part, pattern=[[1, P]], compare_op=ALU.is_ge, fill=0.0,
                                       base=0, channel_multiplier=-1).then_inc(sel_done, 1)
                if n + 1 < NG:
                    gather(n + 1)


def rope_tables():
    f = np.float32
    inv = f(1.0) / np.power(f(10000.0), np.arange(0, C, 2, dtype=f) / f(C)).astype(f)
    angle = np.arange(T, dtype=f)[:, None] * inv[None, :]
    cos, sin = np.cos(angle).astype(f), np.sin(angle).astype(f)
    cos = np.concatenate([cos, cos], axis=1).T
    sin = np.concatenate([-sin, sin], axis=1).T
    one = np.stack([np.concatenate([cos, cos]), np.concatenate([sin, sin])], axis=1)
    seq = one.reshape(2 * C, 2, QB, GROUP).transpose(2, 0, 1, 3)
    return np.ascontiguousarray(np.concatenate([seq] * B))


def shape_tables():
    f = np.float32
    i = np.arange(P)
    tri = np.stack([(i[:, None] < i[None, :]).astype(f), np.where(i[None, :] > i[:, None], f(NEG), f(0)).astype(f)])
    rev = np.tile((E - np.arange(E)).astype(f), (P, GT, 1))
    start = np.tile((np.arange(E) * REGION).astype(f), (P, 1, 1))
    upto = (np.arange(E)[None, :] <= np.arange(E)[:, None]).astype(f)
    upto = np.tile(upto, (P, 1, 1))
    token = np.arange(N, dtype=np.int32).reshape(NG * GT, P).T
    tile_p = (np.arange(P)[:, None] + np.array([0, NRT // 2])[None, :]).astype(f)
    return np.eye(P, dtype=f), tri, np.concatenate([rev, start], axis=1), upto, token, tile_p


def kernel(**inputs):
    import concourse.bacc as bacc
    from concourse.bass_utils import run_bass_kernel_spmd

    a = {name: np.asarray(v) for name, v in inputs.items()}
    wq, wkv = a["L0_attn_W_q_comp"], a["L0_attn_W_kv_comp"]
    wqT, wkT, wvT = wq.T, wkv[:C].T, wkv[C:].T
    swap = lambda w: np.concatenate([w[:, C // 2:], w[:, :C // 2]], axis=1)
    ident, tri, route, upto, token, tile_p = shape_tables()
    arrays = {
        "x": a["L0_attn_x"].reshape(N, D), "w_kv": a["L0_attn_W_to_kv"], "w_compT": a["L0_attn_W_compress"].T,
        "gamma": a["L0_attn_ln_gamma"][:, None], "beta": a["L0_attn_ln_beta"][:, None],
        "w_qk": np.concatenate([wqT, wkT], axis=1), "w_qk_swap": np.concatenate([swap(wqT), swap(wkT)], axis=1),
        "w_vT": wvT, "w_c2l": a["L0_attn_W_comp2lat"], "w_outT": a["L0_attn_W_out_res"].T, "b_out": a["L0_attn_b_out_res"],
        "routerT": a["L0_ffn_router_w"].T, "gate_w": a["L0_ffn_gate_w"], "up_w": a["L0_ffn_up_w"],
        "down_w": a["L0_ffn_down_w"], "sh_gate": a["L0_ffn_shared_gate_w"], "sh_up": a["L0_ffn_shared_up_w"],
        "sh_down": a["L0_ffn_shared_down_w"], "rope": rope_tables(), "ident_in": ident, "tri_in": tri,
        "route_in": route, "upto_in": upto, "token_in": token, "tile_p_in": tile_p,
    }
    arrays = {name: np.ascontiguousarray(v) for name, v in arrays.items()}
    nc = bacc.Bacc("TRN2", target_bir_lowering=False, num_devices=1)
    args = {name: nc.dram_tensor(name, v.shape, mybir.dt.from_np(v.dtype), kind="ExternalInput").ap()
            for name, v in arrays.items()}
    out = nc.dram_tensor("out", (B, T, D), F32, kind="ExternalOutput").ap()
    build(nc, **args, out=out)
    r = run_bass_kernel_spmd(nc, [arrays], core_ids=[0])
    return r.results[0]["out"]
```

```python
from contextlib import ExitStack

import numpy as np
import concourse.bass as bass
from concourse import mybir

F32 = mybir.dt.float32
F32R = mybir.dt.float32r
BF16 = mybir.dt.bfloat16
I32 = mybir.dt.int32
ALU = mybir.AluOpType
ACT = mybir.ActivationFunctionType
AX = mybir.AxisListType

P = 128
B, T, D = 2, 4096, 512
N = B * T
E, FE, FS = 16, 256, 512
C = 64
LAT = 128
GT = 4
GROUP = GT * P
NG = N // GROUP
KD = D // P
FC = FS // P
RT = P
AHEAD = 4
NRT = 2 * N // RT + E
REGION = 2 * N
LIST = E * REGION + RT
LN_EPS = 1e-5
QB = T // GROUP
BIG = 3.0e38
NEG = -1.0e30
EW = KD * 2 * FE + FE // P * D
EH = EW // 2
CA = C + 1


def value(ap):
    return ap.bitcast(F32)


def parts(pe, dst, pairs, first=True, last=True):
    terms = [t for (sh, sl), (mh, ml) in pairs for t in ((sh, mh), (sh, ml), (sl, mh))]
    for i, (w, m) in enumerate(terms):
        mm = pe.matmul(dst, w, m, start=(first and i == 0), stop=(last and i == len(terms) - 1))
    return mm


def after(eng, sem, value):
    if isinstance(value, int) and value <= 0:
        return
    eng.wait_ge(sem, value)


def hold(eng, gate):
    eng.sem_inc(gate, 1)


def build(nc, x, w_kv, w_compT, gamma, beta, w_qk, w_qk_swap, w_vT, w_c2l, w_outT, b_out, routerT,
          gate_w, up_w, down_w, sh_gate, sh_up, sh_down, rope, ident_in, tri_in, route_in, upto_in, token_in, tile_p_in, out):
    q_d = nc.dram_tensor("q_scratch", (C, N), F32, kind="Internal").ap()
    k_d = nc.dram_tensor("k_scratch", (C, N), F32, kind="Internal").ap()
    v_d = nc.dram_tensor("v_scratch", (NG, P, GT * CA), F32, kind="Internal").ap()
    base_d = nc.dram_tensor("base_scratch", (N, D), F32, kind="Internal").ap()
    ew_d = nc.dram_tensor("expert_parts", (E, P, 2, 2, EH), F32, kind="Internal").ap()
    xn_d = nc.dram_tensor("xn_scratch", (N, D), F32, kind="Internal").ap()
    list_d = nc.dram_tensor("token_list", (LIST, 1), I32, kind="Internal").ap()
    rows_out = nc.dram_tensor("rows_out", (NRT * RT, D), F32, kind="Internal").ap()

    with ExitStack() as ctx:
        keep = lambda name, shape, dt: ctx.enter_context(nc.sbuf_tensor(name, shape, dt))
        ident = keep("ident", [P, P], F32)
        slots_all = keep("slots_all", [P, NG * GT, 2], I32)
        gap_all = keep("gap_all", [P, NG * GT], F32)
        table = keep("table", [1, 2, NRT], I32)
        upto_tiles = keep("upto_tiles", [1, E], I32)
        ids_all = keep("ids_all", [P, NRT], I32)
        prepare(nc, x, w_kv, w_compT, gamma, beta, w_qk, w_qk_swap, w_vT, b_out, routerT, sh_gate, sh_up,
                sh_down, rope, ident_in, tri_in, route_in, upto_in, token_in, tile_p_in, q_d, k_d, v_d, base_d, xn_d, list_d,
                ident, slots_all, gap_all, table, upto_tiles, ids_all, ew_d, gate_w, up_w, down_w)
        routed(nc, ew_d, xn_d, rows_out, ident, table, upto_tiles, ids_all)
        attend(nc, w_kv, w_c2l, w_outT, tri_in, q_d, k_d, v_d, base_d, rows_out, out, ident, slots_all, gap_all)


def prepare(nc, x, w_kv, w_compT, gamma, beta, w_qk, w_qk_swap, w_vT, b_out, routerT, sh_gate, sh_up,
            sh_down, rope, ident_in, tri_in, route_in, upto_in, token_in, tile_p_in, q_d, k_d, v_d, base_d, xn_d, list_d,
            ident, slots_all, gap_all, table, upto_tiles, ids_all, ew_d, gate_w, up_w, down_w):
    ctx = ExitStack()
    with ctx:
        sb = lambda name, shape, dt=F32: ctx.enter_context(nc.sbuf_tensor(name, shape, dt))
        ps = lambda name: ctx.enter_context(nc.psum_tensor(name, [P, 512], F32))
        sem = lambda name: ctx.enter_context(nc.semaphore(name))

        wgp, wup, wdp = [[sb(f"{w}_{c}", [P, KD, FS], F32R) for c in "hl"] for w in ("wg", "wu", "wd")]
        wcr = sb("wcr", [P, KD, C + E])
        wcrp = [sb(f"wcr_{c}", [P, KD, C + E], F32R) for c in "hl"]
        wcT = sb("wcT", [P, C])
        wqk = sb("wqk", [C, 2 * C]); wqks = sb("wqks", [C, 2 * C]); wv = sb("wv", [C, C])
        gam = sb("gam", [C, 1]); bet = sb("bet", [C, 1]); bias = sb("bias", [P, D])
        tri = sb("tri", [P, 2, P]); before = sb("before", [P, P], BF16); ones = sb("ones", [P, P], BF16)
        rt = sb("rt", [P, 5, E])
        upto = sb("upto", [P, E, E])
        halfs = sb("halfs", [P, GT])
        zeros = sb("zeros", [P, LIST // P // 3], I32)
        token = sb("token", [P, NG * GT], I32)
        tok = [sb(f"tok_{i}", [P, GT], I32) for i in range(2)]
        x4 = [sb(f"x4_{i}", [P, GT, D]) for i in range(2)]
        xn4 = sb("xn4", [P, GT, D])
        xb4 = [sb(f"xb4_{i}", [P, GT, D]) for i in range(2)]
        xT = [[sb(f"xT_{i}{c}", [P, KD, GROUP], F32R) for c in "hl"] for i in range(2)]
        cs = [sb(f"cs_{i}", [P, 2, GROUP]) for i in range(2)]
        h = [sb(f"h_{c}", [P, FC, GROUP], F32R) for c in "hl"]
        ht = sb("ht", [P, GROUP])
        ew = sb("ew", [P, EH]); ewp = [sb(f"ew_{c}", [P, EH], F32R) for c in "hl"]
        sg = [sb(f"sg_{i}", [P, GROUP]) for i in range(2)]
        stx = sb("stx", [P, GT, 6]); mvx = sb("mvx", [P, GT, 2]); rsx = sb("rsx", [P, GT])
        stc = sb("stc", [P, GT, 6]); mvc = sb("mvc", [P, GT, 2]); rsc = sb("rsc", [P, GT])
        lc = sb("lc", [P, GT, C + E]); cn = sb("cn", [P, GT, C])
        top = sb("top", [P, 2, GT]); pick = sb("pick", [P, 2, GT])
        eq = sb("eq", [P, GT, E]); oh = sb("oh", [P, 2, GT, E]); rest = sb("rest", [P, GT, E])
        mask = sb("mask", [P, GT, E], BF16)
        pb = sb("pb", [P, GT, E]); pk = sb("pk", [P, 2, GT, E]); slotf = sb("slotf", [P, GT, 2])
        slot = [sb(f"slot_{i}", [P, GT, 2], I32) for i in range(2)]
        carry = sb("carry", [P, E])
        chT = sb("chT", [C, GROUP]); t1 = sb("t1", [P, GROUP]); t2 = sb("t2", [P, GROUP])
        qks = [sb(f"qks_{i}", [P, GROUP]) for i in range(2)]
        vs = [sb(f"vs_{i}", [P, GT, CA]) for i in range(2)]
        cnt = sb("cnt", [P, 6, E]); cnti = sb("cnti", [P, 2, E], I32)
        NS = NG * GT * 2
        se = sb("se", [P, NS]); sp_ = sb("sp_", [P, NS]); sei = sb("sei", [P, NS], I32)
        small = sb("small", [1, NRT])
        HT = NRT // 2
        half = sb("half", [P, 2, E]); spot = sb("spot", [P, 4, 2]); spoti = sb("spoti", [P, 2], I32)
        listed = sb("listed", [P, 2, P], I32); listf = sb("listf", [P, 2, P])
        tile_p = sb("tile_p", [P, 2])

        tb = [ps("tb0"), ps("tb1")]
        lb, nb = ps("lb"), ps("nb")
        gb = [ps(f"gb{i}") for i in range(4)]

        consts, x_in = sem("consts"), [sem("x_in0"), sem("x_in1")]
        setup, wc_done, wc_ev = sem("setup"), sem("wc_done"), sem("wc_ev")
        chain, pool_chain = sem("chain"), sem("pool_chain")
        mvx_done, rsx_done, xn_done, xb_done = sem("mvx_done"), sem("rsx_done"), sem("xn_done"), sem("xb_done")
        mvc_done, rsc_done, cn_done = sem("mvc_done"), sem("rsc_done"), sem("cn_done")
        t_done, t_ev, l_done, mask_done = sem("t_done"), sem("t_ev"), sem("l_done"), sem("mask_done")
        cT_done, ch_done, pos_done, pos_ev = sem("cT_done"), sem("ch_done"), sem("pos_done"), sem("pos_ev")
        qkv_done, qk_done, v_done, slot_done = sem("qkv_done"), sem("qk_done"), sem("v_done"), sem("slot_done")
        f_done, sg_done, h_done = sem("f_done"), sem("sg_done"), sem("h_done")
        d_done, d_ev = sem("d_done"), sem("d_ev")
        scattered = [sem("scattered0"), sem("scattered1")]
        st_qkv = [sem("st_qkv0"), sem("st_qkv1")]
        st_base = [sem("st_base0"), sem("st_base1")]
        rope_done = sem("rope_done")
        sp_gate = sem("sp_gate")
        dve_gate, pe_gate, pool_gate = sem("dve_gate"), sem("pe_gate"), sem("pool_gate")
        st_xn, hi_done, split_done, ht_done, hh_done = sem("st_xn"), sem("hi_done"), sem("split_done"), sem("ht_done"), sem("hh_done")
        ew_in, ew_hi, ew_lo, ew_st = sem("ew_in"), sem("ew_hi"), sem("ew_lo"), sem("ew_st")
        te_done, weights_in = sem("te_done"), sem("weights_in")
        idx_done, listed_in, lf_done, li_done = sem("idx_done"), sem("listed_in"), sem("lf_done"), sem("li_done")
        cleared, t_hi = sem("cleared"), sem("t_hi")

        loads = [(ident[:, :], ident_in), (ht[:, :], w_kv), (wcT[:, :], w_compT),
                 (wcr[:, :, C:C + E], routerT.rearrange("(k p) e -> p k e", p=P)),
                 (tri[:, :, :], tri_in.rearrange("a p c -> p a c")), (rt[:, :, :], route_in),
                 (wqk[:, :], w_qk), (wqks[:, :], w_qk_swap), (wv[:, :], w_vT), (gam[:, :], gamma), (bet[:, :], beta),
                 (bias[:, :], b_out.partition_broadcast(P)),
                 (tile_p[:, :], tile_p_in),
                 (upto[:, :, :], upto_in), (token[:, :], token_in)]
        CONSTS = 16 * len(loads)
        staged = (x4[1][:, :, :], xb4[1][:, :, :], xb4[0][:, :, :])
        x_g = x.rearrange("(g j p) d -> g p j d", j=GT, p=P)
        base_g = base_d.rearrange("(g j p) d -> g p j d", j=GT, p=P)
        xn_g = xn_d.rearrange("(g j p) d -> g p j d", j=GT, p=P)
        rope_g = rope

        def pick_g(ap, n):
            return ap[n] if isinstance(n, int) else ap[bass.ds(n, 1)].rearrange("o p j d -> p (o j) d")

        def pick_e(ap, n):
            return ap[n] if isinstance(n, int) else ap[bass.ds(n, 1)].rearrange("o a b -> (o a) b")

        def run(eng, first, step):
            first()
            step(None, 0, 0)
            step(0, 1, 1)
            step(1, 2, 0)
            with eng.Fori(1, NG // 2 - 1) as i:
                step(2 * i, 2 * i + 1, 1)
                step(2 * i + 1, 2 * i + 2, 0)
            step(NG - 2, NG - 1, 1)
            step(NG - 1, None, 0)

        block = ctx.enter_context(nc.Block())

        def known(n, number):
            return isinstance(n, int) and n == number

        def times(n, q):
            return 8 * (n - q)

        @block.sync
        def _(sp):
            def load(n, q):
                if known(n, 1):
                    sp.wait_ge(split_done, 1)
                after(sp, xn_done, n - 1)
                after(sp, xb_done, n - 1)
                after(sp, qk_done, n - 1)
                hold(sp, sp_gate)
                sp.dma_start(x4[q][:, :, :], pick_g(x_g, n)).then_inc(x_in[q], 16)
                sp.dma_start(cs[q][:, :, :], pick_g(rope_g, n)).then_inc(x_in[q], 16)

            def first():
                load(0, 0)
                for dst, src in loads:
                    sp.dma_start(dst, src).then_inc(consts, 16)
                for dst, src in zip(staged, (sh_gate, sh_up, sh_down)):
                    sp.dma_start(dst, src.rearrange("(k p) f -> p k f", p=P)).then_inc(weights_in, 16)
                sp.wait_ge(setup, 1)
                for part in range(3):
                    sp.dma_start(list_d.rearrange("(a p c) o -> a p (c o)", a=3, p=P)[part], zeros[:, :]).then_inc(cleared, 16)
                store_xn(0)
                load_ew(0, 0)

            def load_ew(n, c):
                after(sp, ew_lo, 2 * n + c)
                hold(sp, sp_gate)
                ew_k = ew[:, 0:2 * 2 * FE].rearrange("p (k a f) -> p k a f", a=2, f=FE)
                for a, w in enumerate((gate_w, up_w)):
                    src = pick_e(w, n)[2 * c * P:(2 * c + 2) * P, :].rearrange("(k p) f -> p k f", p=P)
                    sp.dma_start(ew_k[:, :, a, :], src).then_inc(ew_in, 16)
                sp.dma_start(ew[:, 4 * FE:EH], pick_e(down_w, n)[c * P:(c + 1) * P, :]).then_inc(ew_in, 16)

            def store_ew(n, c):
                sp.wait_ge(ew_lo, 2 * n + c + 1)
                hold(sp, sp_gate)
                dst = ew_d[n] if isinstance(n, int) else ew_d[bass.ds(n, 1)].rearrange("o p a c f -> (o p) a c f")
                for a in range(2):
                    sp.dma_start(dst[:, a, c, :], value(ewp[a][:, :])).then_inc(ew_st, 16)

            def store_xn(n):
                sp.wait_ge(xn_done, n + 1)
                hold(sp, sp_gate)
                sp.dma_start(pick_g(xn_g, n), xn4[:, :, :]).then_inc(st_xn, 16)

            def step(s, n, q):
                if n is not None:
                    more = not (isinstance(n, int) and n == NG - 1)
                    if more:
                        load(n + 1, 1 - q)
                    store_ew(n, 0)
                    load_ew(n, 1)
                    store_qkv(n, q)
                    store_ew(n, 1)
                    if more:
                        load_ew(n + 1, 0)
                        store_xn(n + 1)
                if s is not None:
                    sp.wait_ge(d_ev, 4 * s + 4)
                    hold(sp, sp_gate)
                    sp.dma_start(pick_g(base_g, s), xb4[1 - q][:, :, :]).then_inc(st_base[1 - q], 16)

            def store_qkv(n, q):
                sp.wait_ge(qk_done, n + 1)
                sp.wait_ge(v_done, n + 1)
                hold(sp, sp_gate)
                cols = slice(n * GROUP, (n + 1) * GROUP) if isinstance(n, int) else bass.ds(n * GROUP, GROUP)
                sp.dma_start(q_d[:, cols], qks[q][0:C, :]).then_inc(st_qkv[q], 16)
                sp.dma_start(k_d[:, cols], qks[q][C:2 * C, :]).then_inc(st_qkv[q], 16)
                vdst = v_d[n] if isinstance(n, int) else v_d[bass.ds(n, 1)].rearrange("o p c -> (o p) c")
                sp.dma_start(vdst, vs[q][:, :, :].rearrange("p j c -> p (j c)")).then_inc(st_qkv[q], 16)

            run(sp, first, step)
            for q in range(2):
                sp.wait_ge(st_qkv[q], 48 * NG // 2)
                sp.wait_ge(st_base[q], 16 * NG // 2)
            sp.wait_ge(st_xn, 16 * NG)
            sp.wait_ge(ew_st, 64 * NG)

        @block.tensor
        def _(pe):
            def shared_gu(s, q, f):
                t = 4 * s + f
                if f >= 2:
                    pe.wait_ge(ht_done, t - 1)
                else:
                    after(pe, d_ev, 4 * s - 2 + 2 * f)
                if f == 0:
                    pe.wait_ge(t_ev, 4 * s + 4)
                    if known(s, 0):
                        pe.wait_ge(split_done, 3)
                g, u = gb[2 * (f % 2)], gb[2 * (f % 2) + 1]
                for dst, w in ((g, wgp), (u, wup)):
                    mm = parts(pe, dst[:, :], [([a[:, k, f * P:(f + 1) * P] for a in w], [a[:, k, :] for a in xT[q]])
                                               for k in range(KD)])
                mm.then_inc(f_done, 1)

            def shared_down(s, j):
                if j == 0:
                    pe.wait_ge(h_done, 4 * s + 4)
                mm = parts(pe, gb[j][:, :], [([a[:, k, j * P:(j + 1) * P] for a in h], [a[:, k, :] for a in wdp])
                                             for k in range(FC)])
                mm.then_inc(d_done, 1)

            def turn(n, q):
                pe.wait_ge(xn_done, n + 1)
                after(pe, qk_done, n)
                for j in range(GT):
                    after(pe, t_ev, 4 * n + j - 1)
                    for k in range(KD):
                        mm = pe.transpose(tb[j % 2][:, k * P:(k + 1) * P], xn4[:, j, k * P:(k + 1) * P], ident[:, :])
                    mm.then_inc(t_done, 1)

            def logits(n, q):
                pe.wait_ge(t_ev, 4 * n + 4)
                after(pe, v_done, n)
                if known(n, 0):
                    pe.wait_ge(wc_ev, 3)
                for j in range(GT):
                    mm = parts(pe, lb[:, j * (C + E):(j + 1) * (C + E)],
                               [([a[:, k, j * P:(j + 1) * P] for a in xT[q]], [a[:, k, :] for a in wcrp]) for k in range(KD)])
                mm.then_inc(l_done, 1)

            def turn_c(n):
                pe.wait_ge(cn_done, n + 1)
                hold(pe, pe_gate)
                for j in range(GT):
                    mm = pe.transpose(nb[0:C, j * P:(j + 1) * P], cn[:, j, :], ident[:, :])
                mm.then_inc(cT_done, 1)

            def positions(n):
                pe.wait_ge(mask_done, n + 1)
                for j in range(GT):
                    for i in range(j + 1):
                        pe.matmul(lb[:, j * E:(j + 1) * E], (before if i == j else ones)[:, :], mask[:, i, :],
                                  start=(i == 0), stop=(i == j))
                for i in range(GT):
                    mm = pe.matmul(lb[:, GT * E:(GT + 1) * E], ones[:, :], mask[:, i, :], start=(i == 0), stop=(i == GT - 1))
                mm.then_inc(pos_done, 1)

            def qkv(n):
                pe.wait_ge(ch_done, n + 1)
                pe.matmul(nb[:, :], wqk[:, :], chT[:, :], start=True, stop=True)
                pe.matmul(tb[0][:, :], wqks[:, :], chT[:, :], start=True, stop=True)
                pe.wait_ge(pos_ev, n + 1)
                for j in range(GT):
                    mm = pe.matmul(lb[:, j * C:(j + 1) * C], chT[:, j * P:(j + 1) * P], wv[:, :], start=True, stop=True)
                mm.then_inc(qkv_done, 1)

            def turn_tiles():
                pe.wait_ge(idx_done, 1)
                for c in range(2):
                    mm = pe.transpose(lb[0:1, c * HT:(c + 1) * HT], spot[0:HT, 0, c:c + 1], ident[0:HT, 0:HT])
                mm.then_inc(te_done, 1)

            def turn_numbers():
                pe.wait_ge(lf_done, 1)
                for c in range(2):
                    mm = pe.transpose(nb[:, c * HT:(c + 1) * HT], listf[0:HT, c, :], ident[0:HT, 0:HT])
                mm.then_inc(li_done, 1)

            def first():
                pe.wait_ge(consts, CONSTS)
                for k in range(KD):
                    mm = pe.matmul(nb[:, k * C:(k + 1) * C], ht[:, k * P:(k + 1) * P], wcT[:, :], start=True, stop=True)
                mm.then_inc(wc_done, 1)

            def step(s, n, q):
                if s is not None:
                    shared_gu(s, 1 - q, 0)
                if n is not None:
                    turn(n, q)
                if s is not None:
                    shared_gu(s, 1 - q, 1)
                if n is not None:
                    logits(n, q)
                if s is not None:
                    shared_gu(s, 1 - q, 2)
                if n is None:
                    turn_tiles()
                if n is not None:
                    turn_c(n)
                    positions(n)
                if s is not None:
                    shared_gu(s, 1 - q, 3)
                if n is None:
                    turn_numbers()
                if n is not None:
                    qkv(n)
                if s is not None:
                    for j in range(GT):
                        shared_down(s, j)

            run(pe, first, step)

        @block.scalar
        def _(act):
            def silu(s, f):
                t = 4 * s + f
                act.wait_ge(f_done, t + 1)
                after(act, ht_done, t - 1)
                act.activation(sg[f % 2][:, :], gb[2 * (f % 2)][:, :], ACT.Silu).then_inc(sg_done, 1)

            def hidden_high(s, f):
                act.wait_ge(ht_done, 4 * s + f + 1)
                if f == 0:
                    after(act, d_done, 4 * s)
                act.copy(h[0][:, f, :], ht[:, :]).then_inc(hh_done, 1)

            def expert_high(n, c):
                act.wait_ge(ew_in, 96 * n + 48 * c + 48)
                after(act, ew_st, 64 * n + 32 * c)
                act.copy(ewp[0][:, :], ew[:, :]).then_inc(ew_hi, 1)

            def first():
                pass

            def weights_high():
                act.wait_ge(weights_in, 48)
                for (dst, _), src in zip((wgp, wup, wdp), staged):
                    act.copy(dst[:, :, :], src).then_inc(hi_done, 1)

            def step(s, n, q):
                if s is not None:
                    silu(s, 0)
                if n is not None:
                    for j in range(GT):
                        act.wait_ge(t_done, 4 * n + j + 1)
                        act.copy(xT[q][0][:, :, j * P:(j + 1) * P],
                                 tb[j % 2][:, :].rearrange("p (k t) -> p k t", k=KD)).then_inc(t_hi, 1)
                if s is not None:
                    hidden_high(s, 0)
                if n is not None:
                    if known(n, 0):
                        weights_high()
                    expert_high(n, 0)
                if s is not None:
                    for f in range(1, FC):
                        silu(s, f)
                        hidden_high(s, f)
                if n is not None:
                    expert_high(n, 1)

            run(act, first, step)

        @block.vector
        def _(dve):
            LINKS = 18

            def linked(n, k):
                dve.wait_ge(chain, n * LINKS + k)

            def norm(n, q):
                dve.wait_ge(x_in[q], times(n, q) * 2 + 32)
                for j in range(GT):
                    i = dve.bn_stats(stx[:, j, :], x4[q][:, j, :])
                i.then_inc(chain, 1)
                linked(n, 1)
                hold(dve, dve_gate)
                for j in range(GT):
                    i = dve.bn_aggr(mvx[:, j, :], stx[:, j, :])
                i.then_inc(mvx_done, 1)
                after(dve, st_xn, 16 * n)
                after(dve, t_done, 4 * n)
                dve.wait_ge(rsx_done, n + 1)
                for j in range(GT):
                    i = dve.tensor_scalar(xn4[:, j, :], x4[q][:, j, :], mvx[:, j, 0:1], rsx[:, j:j + 1],
                                          ALU.subtract, ALU.mult)
                i.then_inc(xn_done, 1)

            def compressed(n):
                dve.wait_ge(l_done, n + 1)
                dve.tensor_copy(lc[:, :, :], lb[:, 0:GT * (C + E)].rearrange("p (j c) -> p j c", j=GT)).then_inc(chain, 1)
                linked(n, 2)
                for j in range(GT):
                    i = dve.bn_stats(stc[:, j, :], lc[:, j, 0:C])
                i.then_inc(chain, 1)
                linked(n, 3)
                hold(dve, dve_gate)
                for j in range(GT):
                    i = dve.bn_aggr(mvc[:, j, :], stc[:, j, :])
                i.then_inc(mvc_done, 1)

            def choose(n):
                rev = rt[:, 0:GT, :]
                lg = lc[:, :, C:C + E]
                wide = lambda ap: ap.unsqueeze(2).broadcast_to([P, GT, E])
                for c in range(2):
                    src = lg if c == 0 else rest[:, :, :]
                    o = 3 + 6 * c
                    dve.tensor_reduce(top[:, c, :], src, AX.X, ALU.max).then_inc(chain, 1)
                    linked(n, o + 1)
                    dve.tensor_tensor(eq[:, :, :], src, wide(top[:, c, :]), ALU.is_equal).then_inc(chain, 1)
                    linked(n, o + 2)
                    dve.tensor_tensor(pb[:, :, :], eq[:, :, :], rev, ALU.mult).then_inc(chain, 1)
                    linked(n, o + 3)
                    dve.tensor_reduce(pick[:, c, :], pb[:, :, :], AX.X, ALU.max).then_inc(chain, 1)
                    linked(n, o + 4)
                    dve.tensor_tensor(oh[:, c, :, :], rev, wide(pick[:, c, :]), ALU.is_equal).then_inc(chain, 1)
                    linked(n, o + 5)
                    if c == 0:
                        dve.scalar_tensor_tensor(out=rest[:, :, :], in0=oh[:, 0, :, :], scalar=-BIG, in1=lg,
                                                 op0=ALU.mult, op1=ALU.add).then_inc(chain, 1)
                        linked(n, 9)

            def mask_and_gap(n):
                after(dve, pos_done, n)
                dve.tensor_tensor(mask[:, :, :], oh[:, 0, :, :], oh[:, 1, :, :], ALU.add).then_inc(mask_done, 1)
                at = slice(n * GT, (n + 1) * GT) if isinstance(n, int) else bass.ds(n * GT, GT)
                dve.tensor_tensor(gap_all[:, at], top[:, 1, :], top[:, 0, :], ALU.subtract).then_inc(chain, 1)

            def normed(n):
                dve.wait_ge(rsc_done, n + 1)
                for j in range(GT):
                    i = dve.tensor_scalar(cn[:, j, :], lc[:, j, 0:C], mvc[:, j, 0:1], rsc[:, j:j + 1],
                                          ALU.subtract, ALU.mult)
                i.then_inc(cn_done, 1)

            def scaled(n):
                dve.wait_ge(cT_done, n + 1)
                dve.tensor_scalar(chT[:, :], nb[0:C, :], gam[:, 0:1], bet[:, 0:1], ALU.mult, ALU.add).then_inc(ch_done, 1)

            def slots(n, q):
                dve.wait_ge(pos_done, n + 1)
                dve.tensor_tensor(pb[:, :, :], lb[:, 0:GT * E].rearrange("p (j e) -> p j e", e=E),
                                  carry[:, :].unsqueeze(1).broadcast_to([P, GT, E]), ALU.add).then_inc(chain, 1)
                linked(n, 16)
                dve.tensor_tensor(carry[:, :], lb[:, GT * E:(GT + 1) * E], carry[:, :], ALU.add).then_inc(pos_ev, 1)
                for c in range(2):
                    i = dve.tensor_tensor(pk[:, c, :, :], oh[:, c, :, :], pb[:, :, :], ALU.mult)
                i.then_inc(chain, 1)
                linked(n, 17)
                for c in range(2):
                    i = dve.tensor_reduce(slotf[:, :, c], pk[:, c, :, :], AX.X, ALU.add)
                i.then_inc(chain, 1)
                linked(n, 18)
                after(dve, scattered[q], times(n, q) * 8)
                at = slice(n * GT, (n + 1) * GT) if isinstance(n, int) else bass.ds(n * GT, GT)
                dve.tensor_copy(tok[q][:, :], token[:, at])
                dve.tensor_copy(slot[q][:, :, :], slotf[:, :, :]).then_inc(slot_done, 1)
                dve.tensor_copy(slots_all[:, at, :], slotf[:, :, :])

            def roped(n, q):
                dve.wait_ge(qkv_done, n + 1)
                dve.tensor_tensor(t1[:, :], nb[:, :], cs[q][:, 0, :], ALU.mult)
                dve.tensor_tensor(t2[:, :], tb[0][:, :], cs[q][:, 1, :], ALU.mult).then_inc(rope_done, 1)
                after(dve, st_qkv[q], times(n, q) * 3)
                dve.tensor_copy(vs[q][:, :, 0:C], lb[:, 0:GT * C].rearrange("p (j c) -> p j c", j=GT)).then_inc(v_done, 1)
                dve.wait_ge(rope_done, n + 1)
                dve.tensor_tensor(qks[q][:, :], t1[:, :], t2[:, :], ALU.add).then_inc(qk_done, 1)

            def hidden(s, f):
                t = 4 * s + f
                dve.wait_ge(sg_done, t + 1)
                after(dve, h_done, t)
                dve.tensor_tensor(ht[:, :], gb[2 * (f % 2) + 1][:, :], sg[f % 2][:, :], ALU.mult).then_inc(ht_done, 1)

            def hidden_low(s, f):
                dve.wait_ge(hh_done, 4 * s + f + 1)
                dve.tensor_tensor(h[1][:, f, :], ht[:, :], value(h[0][:, f, :]), ALU.subtract).then_inc(h_done, 1)

            def turned_low(n, q):
                for j in range(GT):
                    dve.wait_ge(t_hi, 4 * n + j + 1)
                    cols = slice(j * P, (j + 1) * P)
                    dve.tensor_tensor(xT[q][1][:, :, cols], tb[j % 2][:, :].rearrange("p (k t) -> p k t", k=KD),
                                      value(xT[q][0][:, :, cols]), ALU.subtract).then_inc(t_ev, 1)

            def expert_low(n, c):
                dve.wait_ge(ew_hi, 2 * n + c + 1)
                dve.tensor_tensor(ewp[1][:, :], ew[:, :], value(ewp[0][:, :]), ALU.subtract).then_inc(ew_lo, 1)

            def added(s, q, j):
                if j == 0:
                    dve.wait_ge(xb_done, s + 1)
                dve.wait_ge(d_done, 4 * s + j + 1)
                dve.tensor_tensor(xb4[q][:, j, :], gb[j][:, :], xb4[q][:, j, :], ALU.add).then_inc(d_ev, 1)

            def first():
                dve.memset(ones[:, :], 1.0)
                dve.memset(zeros[:, :], 0)
                dve.memset(halfs[:, :], -0.5)
                dve.memset(vs[0][:, :, C:CA], 1.0)
                dve.memset(vs[1][:, :, C:CA], 1.0).then_inc(setup, 1)
                norm(0, 0)
                dve.wait_ge(consts, CONSTS)
                dve.tensor_copy(before[:, :], tri[:, 0, :])
                dve.tensor_copy(carry[:, :], rt[:, GT, :])
                dve.wait_ge(wc_done, 1)
                dve.tensor_copy(wcr[:, :, 0:C], nb[:, 0:KD * C].rearrange("p (k c) -> p k c", k=KD)).then_inc(wc_ev, 1)
                dve.wait_ge(wc_ev, 1)
                dve.tensor_copy(wcrp[0][:, :, :], wcr[:, :, :]).then_inc(wc_ev, 1)
                dve.wait_ge(wc_ev, 2)
                dve.tensor_tensor(wcrp[1][:, :, :], wcr[:, :, :], value(wcrp[0][:, :, :]), ALU.subtract).then_inc(wc_ev, 1)
                dve.wait_ge(wc_ev, 3)

            def weights_low():
                for i, ((high, low), src) in enumerate(zip((wgp, wup, wdp), staged)):
                    dve.wait_ge(hi_done, i + 1)
                    dve.tensor_tensor(low[:, :, :], src, value(high[:, :, :]), ALU.subtract).then_inc(split_done, 1)
                dve.wait_ge(split_done, 3)

            links = [NG * LINKS]

            def link(i):
                links[0] += 1
                i.then_inc(chain, 1)
                dve.wait_ge(chain, links[0])

            def count_tiles():
                dve.wait_ge(xb_done, NG)
                dve.wait_ge(pos_ev, NG)
                link(dve.tensor_tensor(cnt[:, 0, :], carry[:, :], rt[:, GT, :], ALU.subtract))
                link(dve.tensor_scalar(cnt[:, 1, :], cnt[:, 0, :], float(RT - 1), None, ALU.add))
                link(dve.tensor_copy(cnti[:, 0, :], cnt[:, 1, :]))
                link(dve.tensor_scalar(cnti[:, 1, :], cnti[:, 0, :], RT.bit_length() - 1, None, ALU.logical_shift_right))
                link(dve.tensor_copy(cnt[:, 2, :], cnti[:, 1, :]))
                tiles_b = lambda p, n: cnt[0:p, 2, :].unsqueeze(1).broadcast_to([p, n, E])
                tri_b = x4[1][:, :, :].rearrange("p a b -> p (a b)")[:, 0:E * E].rearrange("p (a b) -> p a b", b=E)
                link(dve.tensor_tensor(tri_b, upto[:, :, :], tiles_b(P, E), ALU.mult))
                link(dve.tensor_reduce(cnt[:, 3, :], tri_b, AX.X, ALU.add))
                link(dve.tensor_tensor(cnt[:, 4, :], cnt[:, 3, :], cnt[:, 2, :], ALU.subtract))
                link(dve.tensor_scalar(cnt[:, 5, :], cnt[:, 4, :], float(RT), None, ALU.mult))

            def find_rows():
                slots = slots_all[:, :, :].rearrange("p t c -> p (t c)")
                link(dve.tensor_scalar(sei[:, :], slots, REGION.bit_length() - 1, None, ALU.logical_shift_right))
                link(dve.tensor_copy(se[:, :], sei[:, :]))
                link(dve.scalar_tensor_tensor(out=sp_[:, :], in0=se[:, :], scalar=-float(REGION), in1=slots,
                                              op0=ALU.mult, op1=ALU.add))
                hot = x4[0][:, :, :].rearrange("p a b -> p (a b)").rearrange("p (s e) -> p s e", e=E)
                rev_b = rt[:, 0, :].unsqueeze(1).broadcast_to([P, NS, E])
                link(dve.tensor_scalar(se[:, :], se[:, :], -1.0, float(E), ALU.mult, ALU.add))
                link(dve.tensor_tensor(hot, se[:, :].unsqueeze(2).broadcast_to([P, NS, E]), rev_b, ALU.is_equal))
                link(dve.tensor_tensor(hot, hot, cnt[:, 5, :].unsqueeze(1).broadcast_to([P, NS, E]), ALU.mult))
                link(dve.tensor_reduce(se[:, :], hot, AX.X, ALU.add))
                link(dve.tensor_tensor(slots, se[:, :], sp_[:, :], ALU.add))

            def find_spots():
                wide = lambda ap: ap.unsqueeze(1).broadcast_to([P, 2, E])
                link(dve.tensor_tensor(half[:, :, :], tile_p[:, :].unsqueeze(2).broadcast_to([P, 2, E]), wide(cnt[:, 3, :]), ALU.is_ge))
                link(dve.tensor_reduce(spot[:, 0, :], half[:, :, :], AX.X, ALU.add))
                link(dve.tensor_tensor(half[:, :, :], half[:, :, :], wide(cnt[:, 2, :]), ALU.mult))
                link(dve.tensor_reduce(spot[:, 1, :], half[:, :, :], AX.X, ALU.add))
                link(dve.tensor_tensor(spot[:, 2, :], tile_p[:, :], spot[:, 1, :], ALU.subtract))
                link(dve.scalar_tensor_tensor(out=spot[:, 3, :], in0=spot[:, 0, :], scalar=float(REGION // RT),
                                              in1=spot[:, 2, :], op0=ALU.mult, op1=ALU.add))
                link(dve.tensor_scalar(spot[:, 1, :], spot[:, 3, :], float(E * REGION // RT), None, ALU.min))
                dve.tensor_copy(spoti[:, :], spot[:, 1, :]).then_inc(idx_done, 1)

            def table_of_tiles():
                dve.wait_ge(te_done, 1)
                link(dve.tensor_scalar(small[:, :], lb[0:1, 0:NRT], float(E - 1), 1.0, ALU.min, ALU.add))
                link(dve.tensor_copy(table[:, 0, :], small[:, :]))
                link(dve.tensor_scalar(table[:, 1, :], table[:, 0, :], 1, None, ALU.bitwise_and))
                link(dve.tensor_scalar(cnt[:, 4, :], cnt[:, 3, :], 1.0, None, ALU.add))
                link(dve.tensor_copy(upto_tiles[:, :], cnt[0:1, 4, :]))
                dve.wait_ge(listed_in, 32)
                dve.tensor_copy(listf[0:HT, :, :], listed[0:HT, :, :]).then_inc(lf_done, 1)

            def numbers_of_tiles():
                dve.wait_ge(li_done, 1)
                link(dve.tensor_copy(ids_all[:, :], nb[:, 0:NRT]))

            def step(s, n, q):
                if s is not None:
                    hidden(s, 0)
                if n is not None:
                    turned_low(n, q)
                if known(n, 0):
                    weights_low()
                if s is not None:
                    hidden_low(s, 0)
                if n is None:
                    count_tiles()
                    find_spots()
                if n is not None and not known(n, 0):
                    expert_low(n, 0)
                if s is not None:
                    hidden(s, 1)
                    hidden_low(s, 1)
                if n is not None:
                    compressed(n)
                    choose(n)
                    mask_and_gap(n)
                    normed(n)
                if s is not None:
                    hidden(s, 2)
                if n is not None:
                    scaled(n)
                if s is not None:
                    hidden_low(s, 2)
                if n is None:
                    table_of_tiles()
                if n is not None:
                    slots(n, q)
                if s is not None:
                    hidden(s, 3)
                    hidden_low(s, 3)
                if n is None:
                    numbers_of_tiles()
                    find_rows()
                if n is not None:
                    roped(n, q)
                if s is not None:
                    added(s, 1 - q, 0)
                    added(s, 1 - q, 1)
                if known(n, 0):
                    expert_low(0, 0)
                    norm(1, 1)
                    expert_low(0, 1)
                elif n is not None:
                    expert_low(n, 1)
                    if not known(n, NG - 1):
                        norm(n + 1, 1 - q)
                if s is not None:
                    added(s, 1 - q, 2)
                    added(s, 1 - q, 3)

            run(dve, first, step)

        @block.gpsimd
        def _(pool):
            def root(n, per, mv, rs, waited, done):
                pool.wait_ge(waited, n + 1)
                hold(pool, pool_gate)
                pool.tensor_scalar(rs[:, :], mv[:, :, 1], LN_EPS, None, ALU.add).then_inc(pool_chain, 1)
                pool.wait_ge(pool_chain, 2 * n + 1 + per)
                pool.tensor_tensor(rs[:, :], rs[:, :], halfs[:, :], ALU.pow).then_inc(done, 1)

            def biased(n, q):
                after(pool, st_base[q], times(n, q))
                for j in range(GT):
                    i = pool.tensor_tensor(xb4[q][:, j, :], x4[q][:, j, :], bias[:, :], ALU.add)
                i.then_inc(xb_done, 1)

            def first():
                pool.wait_ge(setup, 1)
                root(0, 0, mvx, rsx, mvx_done, rsx_done)

            def step(s, n, q):
                if n is None:
                    return
                root(n, 1, mvc, rsc, mvc_done, rsc_done)
                pool.wait_ge(slot_done, n + 1)
                pool.wait_ge(cleared, 48)
                hold(pool, pool_gate)
                for j in range(GT):
                    for c in range(2):
                        pool.indirect_dma_start(list_d[:, :], bass.IndirectOffsetOnAxis(ap=slot[q][:, j, c:c + 1], axis=0),
                                                tok[q][:, j:j + 1], None).then_inc(scattered[q], 16)
                if known(n, 0):
                    pool.wait_ge(consts, CONSTS)
                    pool.wait_ge(split_done, 3)
                    biased(0, 0)
                if not known(n, NG - 1):
                    root(n + 1, 0, mvx, rsx, mvx_done, rsx_done)
                    biased(n + 1, 1 - q)

            run(pool, first, step)
            for q in range(2):
                pool.wait_ge(scattered[q], 128 * NG // 2)
            pool.wait_ge(idx_done, 1)
            for c in range(2):
                pool.indirect_dma_start(listed[0:HT, c, :], None, list_d.rearrange("(r c) o -> r (c o)", c=P),
                                        bass.IndirectOffsetOnAxis(ap=spoti[0:HT, c:c + 1], axis=0)).then_inc(listed_in, 16)
            pool.wait_ge(listed_in, 32)


def routed(nc, ew_d, xn_d, rows_out, ident, table, upto_tiles, ids_all):
    with ExitStack() as ctx:
        sb = lambda name, shape, dt=F32: ctx.enter_context(nc.sbuf_tensor(name, shape, dt))
        ps = lambda name: ctx.enter_context(nc.psum_tensor(name, [P, 512], F32))
        sem = lambda name: ctx.enter_context(nc.semaphore(name))
        pair = lambda name: [sem(name + "0"), sem(name + "1")]
        FK = FE // P

        w = sb("w", [P, 2, 2, 2, EH], F32R)
        ids = [sb(f"ids_{i}", [P, 1], I32) for i in range(AHEAD)]
        rows = [sb(f"rows_{i}", [P, D]) for i in range(AHEAD)]
        rT = [[sb(f"rT_{i}{c}", [P, KD, RT], F32R) for c in "hl"] for i in range(2)]
        hT = [[sb(f"hT_{i}{c}", [P, FK, RT], F32R) for c in "hl"] for i in range(2)]
        h = [sb(f"eh_{i}", [P, FE]) for i in range(2)]
        sg = [sb(f"esg_{i}", [P, FE]) for i in range(2)]
        res = [sb(f"res_{i}", [P, D]) for i in range(2)]
        tb, gu, hb, db = [[ps(f"e{n}{i}") for i in range(2)] for n in ("tb", "gu", "hb", "db")]

        w_in, w_ready = pair("w_in"), sem("w_ready")
        ids_done, rows_in, stored = sem("ids_done"), [sem(f"rows_in{i}") for i in range(AHEAD)], pair("rstored")
        t_done, t_hi, t_lo = sem("et_done"), sem("et_hi"), sem("et_lo")
        gu_done, sg_done, h_done = sem("egu_done"), sem("esg_done"), sem("eh_done")
        hb_done, hT_hi, hT_lo = sem("ehb_done"), sem("ehT_hi"), sem("ehT_lo")
        d_done, d_ev = sem("ed_done"), sem("ed_ev")
        pool_gate, sp_gate = sem("epool_gate"), sem("esp_gate")

        def run(eng, step):
            for r in range(AHEAD):
                step(r, r)
            with eng.Fori(1, NRT // AHEAD - 1) as i:
                for r in range(AHEAD):
                    step(AHEAD * i + r, r)
            for r in range(AHEAD):
                step(NRT - AHEAD + r, r)

        def uses(t, r, of=2):
            return 16 // of * (t - r % of)

        known = lambda t, f: isinstance(t, int) and f(t)

        def wait_weights(eng, t):
            at = slice(t, t + 1) if isinstance(t, int) else bass.ds(t, 1)
            eng.wait_ge(w_ready, eng.value_load(table[0:1, 0, at], min_val=1, max_val=E))

        block = ctx.enter_context(nc.Block())

        @block.sync
        def _(sp):
            def load(e, q, at):
                if at is not None:
                    done = sp.value_load(upto_tiles[0:1, at], min_val=1, max_val=NRT + 1)
                    sp.wait_ge(d_ev, done)
                    hold(sp, sp_gate)
                src = ew_d[e] if isinstance(e, int) else ew_d[bass.ds(e, 1)].rearrange("o p a c f -> (o p) a c f")
                for a in range(2):
                    for c in range(2):
                        sp.dma_start(value(w[:, 1 - q, a, c, :]), src[:, a, c, :]).then_inc(w_in[q], 16)
                sp.wait_ge(w_in[q], 32 * (e - q) + 64)
                sp.sem_inc(w_ready, 1)

            load(0, 0, None)
            load(1, 1, None)
            with sp.Fori(1, E // 2) as i:
                load(2 * i, 0, bass.ds(2 * i - 2, 1))
                load(2 * i + 1, 1, bass.ds(2 * i - 1, 1))

        @block.tensor
        def _(pe):
            def turn(t, r):
                pe.wait_ge(rows_in[r], uses(t, r, AHEAD) + 16)
                after(pe, t_lo, t - 1)
                for k in range(KD):
                    mm = pe.transpose(tb[r % 2][:, k * P:(k + 1) * P], rows[r][:, k * P:(k + 1) * P], ident[:, :])
                mm.then_inc(t_done, 1)

            this_buffer, last_buffer = pe.alloc_register("this_buffer"), pe.alloc_register("last_buffer")

            def find_buffer(t):
                at = slice(t, t + 1) if isinstance(t, int) else bass.ds(t, 1)
                pe.reg_mov(this_buffer, pe.value_load(table[0:1, 1, at], min_val=0, max_val=1))

            def weights(b, a, c, lo):
                return w[:, bass.ds(b, 1), a, c, lo:lo + D].rearrange("p o f -> p (o f)")

            def gate_up(t, q):
                b = pe.snap(this_buffer, min_val=0, max_val=1)
                if known(t, lambda t: t < AHEAD):
                    wait_weights(pe, t)
                pe.wait_ge(t_lo, t + 1)
                after(pe, h_done, t - 1)
                mm = parts(pe, gu[q][:, :], [([a[:, k, :] for a in rT[q]],
                                              [weights(b, a, k // 2, k % 2 * 2 * FE) for a in range(2)]) for k in range(KD)])
                mm.then_inc(gu_done, 1)

            def down(t, q):
                b = pe.snap(last_buffer, min_val=0, max_val=1)
                pe.wait_ge(hT_lo, t + 1)
                if not known(t, lambda t: t < 2):
                    pe.wait_ge(d_ev, t)
                mm = parts(pe, db[q][:, :], [([a[:, k, :] for a in hT[q]],
                                              [weights(b, a, k, 4 * FE) for a in range(2)]) for k in range(FK)])
                mm.then_inc(d_done, 1)

            def turn_hidden(t, q):
                pe.wait_ge(h_done, t + 1)
                after(pe, hT_lo, t - 1)
                for k in range(FK):
                    mm = pe.transpose(hb[q][:, k * P:(k + 1) * P], h[q][:, k * P:(k + 1) * P], ident[:, :])
                mm.then_inc(hb_done, 1)

            def step(t, r):
                q = r % 2
                gate_up(t, q)
                if not known(t, lambda t: t == 0):
                    down(t - 1, 1 - q)
                pe.reg_mov(last_buffer, this_buffer)
                if not known(t, lambda t: t == NRT - 1):
                    find_buffer(t + 1)
                if not known(t, lambda t: t >= NRT - 2):
                    turn(t + 2, (r + 2) % AHEAD)
                turn_hidden(t, q)

            find_buffer(0)
            turn(0, 0)
            turn(1, 1)
            run(pe, step)
            down(NRT - 1, 1)

        @block.scalar
        def _(act):
            def turned(t, q):
                act.wait_ge(t_done, t + 1)
                after(act, gu_done, t - 1)
                act.copy(rT[q][0][:, :, :], tb[q][:, :].rearrange("p (k t) -> p k t", k=KD)).then_inc(t_hi, 1)

            def silu(t, q):
                act.wait_ge(gu_done, t + 1)
                after(act, h_done, t - 1)
                act.activation(sg[q][:, :], gu[q][:, 0:FE], ACT.Silu).then_inc(sg_done, 1)

            def hidden_turned(t, q):
                act.wait_ge(hb_done, t + 1)
                after(act, d_done, t - 1)
                act.copy(hT[q][0][:, :, :], hb[q][:, 0:FE].rearrange("p (k t) -> p k t", k=FK)).then_inc(hT_hi, 1)

            def downed(t, q):
                act.wait_ge(d_done, t + 1)
                after(act, stored[q], uses(t, q))
                act.copy(res[q][:, :], db[q][:, :]).then_inc(d_ev, 1)

            def store(t, q):
                act.wait_ge(d_ev, t + 2)
                dst = rows_out[t * RT:(t + 1) * RT, :] if isinstance(t, int) else rows_out[bass.ds(t * RT, RT), :]
                act.dma_start(dst, res[q][:, :]).then_inc(stored[q], 16)

            def step(t, r):
                q = r % 2
                silu(t, q)
                if not known(t, lambda t: t < 2):
                    store(t - 2, q)
                if not known(t, lambda t: t >= NRT - 2):
                    turned(t + 2, q)
                if not known(t, lambda t: t == 0):
                    downed(t - 1, 1 - q)
                hidden_turned(t, q)

            act.sem_inc(d_ev, 1)
            turned(0, 0)
            turned(1, 1)
            run(act, step)
            store(NRT - 2, 0)
            downed(NRT - 1, 1)
            store(NRT - 1, 1)
            for q in range(2):
                act.wait_ge(stored[q], 16 * NRT // 2)

        @block.vector
        def _(dve):
            def turned(t, q):
                dve.wait_ge(t_hi, t + 1)
                dve.tensor_tensor(rT[q][1][:, :, :], tb[q][:, :].rearrange("p (k t) -> p k t", k=KD),
                                  value(rT[q][0][:, :, :]), ALU.subtract).then_inc(t_lo, 1)

            def hidden(t, q):
                dve.wait_ge(sg_done, t + 1)
                after(dve, hb_done, t - 1)
                dve.tensor_tensor(h[q][:, :], gu[q][:, FE:2 * FE], sg[q][:, :], ALU.mult).then_inc(h_done, 1)

            def hidden_turned(t, q):
                dve.wait_ge(hT_hi, t + 1)
                dve.tensor_tensor(hT[q][1][:, :, :], hb[q][:, 0:FE].rearrange("p (k t) -> p k t", k=FK),
                                  value(hT[q][0][:, :, :]), ALU.subtract).then_inc(hT_lo, 1)

            def step(t, r):
                q = r % 2
                hidden(t, q)
                if not known(t, lambda t: t >= NRT - 2):
                    turned(t + 2, q)
                hidden_turned(t, q)

            turned(0, 0)
            turned(1, 1)
            run(dve, step)

        @block.gpsimd
        def _(pool):
            def gather(t, r):
                after(pool, rows_in[r], uses(t, r, AHEAD))
                after(pool, t_done, t - AHEAD + 1)
                at = slice(t, t + 1) if isinstance(t, int) else bass.ds(t, 1)
                if not known(t, lambda t: t < AHEAD):
                    wait_weights(pool, t)
                hold(pool, pool_gate)
                pool.tensor_copy(ids[r][:, :], ids_all[:, at]).then_inc(ids_done, 1)
                pool.wait_ge(ids_done, t + 1)
                hold(pool, pool_gate)
                pool.indirect_dma_start(rows[r][:, :], None, xn_d[:, :],
                                        bass.IndirectOffsetOnAxis(ap=ids[r][:, :], axis=0)).then_inc(rows_in[r], 16)

            run(pool, gather)


def attend(nc, w_kv, w_c2l, w_outT, tri_in, q_d, k_d, v_d, base_d, rows_out, out, ident, slots_all, gap_all):
    with ExitStack() as ctx:
        sb = lambda name, shape, dt=F32: ctx.enter_context(nc.sbuf_tensor(name, shape, dt))
        ps = lambda name: ctx.enter_context(nc.psum_tensor(name, [P, 512], F32))
        sem = lambda name: ctx.enter_context(nc.semaphore(name))
        pair = lambda name: [sem(name + "0"), sem(name + "1")]
        KB = T // P
        NE, NP, NSC = 3, 5, 3
        LAG = 3
        SCALE = C ** -0.5

        qa, ka = [[sb(f"{n}_{i}", [P, GROUP]) for i in range(2)] for n in ("qa", "ka")]
        qh = [sb(f"qh_{i}", [P, GROUP], F32R) for i in range(2)]
        qlm = [sb(f"qlm_{i}", [CA, GROUP], F32R) for i in range(2)]
        khl = sb("khl", [P, N], F32R); kh1 = sb("kh1", [CA, N], F32R)
        va = [sb(f"va_{i}", [P, GT, CA]) for i in range(2)]
        vap = [sb(f"va_{c}", [P, NG, GT, CA], F32R) for c in "hl"]
        ones = sb("ones3", [1, GROUP])
        wc = sb("wc", [LAT, C])
        tri = sb("tri3", [P, 2, P]); future = sb("future", [P, P], BF16); identb = sb("identb", [P, P], BF16)
        w_all = sb("w_all", [P, 2, NG * GT]); den = sb("den", [P, NG * GT])
        mx = sb("mx", [P, GT, QB]); mcol = sb("mcol", [P, GT, CA]); last = sb("last", [CA, 2], F32R)
        ex = [sb(f"ex_{i}", [P, GROUP]) for i in range(NE)]
        prp = [[sb(f"pr_{i}{c}", [P, GROUP], F32R) for c in "hl"] for i in range(NP)]
        oT = [sb(f"oT_{c}", [CA, GROUP], F32R) for c in "hl"]; mop = [sb(f"mo_{c}", [C, D], F32R) for c in "hl"]
        last_f = sb("last_f", [CA, 2]); lr = sb("lr", [P, 2 * GT])
        base = [sb(f"base_{i}", [P, GT, D]) for i in range(2)]
        got = [sb(f"got_{i}", [P, 2, GT, D]) for i in range(2)]
        wz, wo, mo = got[1][:, 0, 0, :], got[1][:, 0, 1, :], got[1][0:C, 0, 2, :]

        mb = [ps("mb0"), ps("mb1")]
        sc = [ps(f"sc{i}") for i in range(NSC)]
        ob, pj, nb = ps("ob"), ps("pj"), ps("anb")

        const_in, qkv_in, a_ready, highs, lows = sem("const_in"), pair("qkv_in"), sem("a_ready"), sem("highs"), sem("lows")
        sum_w, mo_done, mo_ev, w_exp, chain = sem("sum_w"), sem("mo_done"), sem("mo_ev"), sem("w_exp"), sem("a_chain")
        m_done, m_red, mc_done, mt_done, mrow = sem("m_done"), sem("m_red"), sem("mc_done"), sem("mt_done"), sem("mrow")
        s_done, e_done, sel_done, pv_done = sem("s_done"), sem("e_done"), sem("sel_done"), sem("pv_done")
        dve_low, pool_low, o_hi = sem("dve_low"), sem("pool_low"), sem("o_hi")
        o_ev, l_done, l_ev, p_done, p_ev = sem("o_ev"), sem("al_done"), sem("l_ev"), sem("p_done"), sem("p_ev")
        w1_ev, w2_ev, base_in, got_in, out_st = sem("w1_ev"), sem("w2_ev"), pair("base_in"), pair("got_in"), pair("out_st")

        base_g = base_d.rearrange("(g j p) d -> g p j d", j=GT, p=P)
        out_g = out.rearrange("b t d -> (b t) d").rearrange("(g j p) d -> g p j d", j=GT, p=P)
        CONSTS = 16 * 4

        units = [GT * (n % QB + 1) for n in range(NG)]
        first_unit = [sum(units[:n]) for n in range(NG + 1)]

        by_pool = [kb % 2 == 1 and GT < kb and kb < u - GT for u in units for kb in range(u)]
        pool_before = [sum(by_pool[:u]) for u in range(len(by_pool))]

        def low_there(eng, u):
            if u < 0:
                return
            if by_pool[u]:
                eng.wait_ge(pool_low, pool_before[u] + 1)
            else:
                eng.wait_ge(dve_low, u - pool_before[u] + 1)

        def make_low(eng, n, kb):
            u, d = first_unit[n] + kb, kb - GT * (n % QB)
            off = max(0, d) * P
            eng.wait_ge(e_done, u + 1)
            if d >= 0:
                eng.wait_ge(sel_done, GT * n + d + 1)
            after(eng, pv_done, u - NP + 1)
            eng.tensor_tensor(prp[u % NP][1][:, off:GROUP], ex[u % NE][:, off:GROUP],
                              value(prp[u % NP][0][:, off:GROUP]), ALU.subtract
                              ).then_inc(pool_low if by_pool[u] else dve_low, 1)

        start = [1 if u == GT else 3 if u == 2 * GT else 5 for u in units]

        def steps(n):
            ahead = units[n + 1] if n + 1 < NG else 0
            over = units[n] - 2 - start[n]
            for kb in range(units[n]):
                behind = [(j, term) for j in range(GT) for term in range(3)
                          if n and kb == min(1 + j * (n % QB + 1) + term, units[n] - 1)]
                yield kb, range(*(min(ahead, max(0, -(-ahead * k // over))) for k in (kb - start[n], kb - start[n] + 1))), behind

        block = ctx.enter_context(nc.Block())

        @block.sync
        def _(sp):
            def load_base(n):
                after(sp, out_st[n % 2], 16 * (n // 2))
                sp.dma_start(base[n % 2][:, :, :], base_g[n]).then_inc(base_in[n % 2], 16)

            def load_block(n):
                q, at = n % 2, slice(n * GROUP, (n + 1) * GROUP)
                after(sp, lows, n - 1)
                for half in (slice(0, C), slice(C, P)):
                    sp.dma_start(qa[q][half, :], q_d[:, at]).then_inc(qkv_in[q], 16)
                    sp.dma_start(ka[q][half, :], k_d[:, at]).then_inc(qkv_in[q], 16)
                sp.dma_start(va[q][:, :, :].rearrange("p j c -> p (j c)"), v_d[n]).then_inc(qkv_in[q], 16)

            load_block(0)
            for dst, src in ((tri[:, :, :], tri_in.rearrange("a p c -> p a c")), (wz, w_kv), (wo, w_outT), (wc[:, :], w_c2l)):
                sp.dma_start(dst, src).then_inc(const_in, 16)
            load_block(1)
            for n in range(NG):
                load_base(n)
                if n + 2 < NG:
                    load_block(n + 2)
                if n:
                    sp.wait_ge(w2_ev, GT * n)
                    sp.dma_start(out_g[n - 1], base[(n - 1) % 2][:, :, :]).then_inc(out_st[(n - 1) % 2], 16)
            sp.wait_ge(w2_ev, GT * NG)
            sp.dma_start(out_g[NG - 1], base[(NG - 1) % 2][:, :, :]).then_inc(out_st[(NG - 1) % 2], 16)
            for q in range(2):
                sp.wait_ge(out_st[q], 16 * NG // 2)

        @block.tensor
        def _(pe):
            def max_scores(n, v):
                m, (j, c) = n % QB, divmod(v, n % QB + 1)
                g = first_unit[n] + v
                if v == 0:
                    pe.wait_ge(lows, n + 1)
                after(pe, m_red, g - 1)
                w = GROUP if c < m else P * (j + 1)
                key = n // QB * T + c * GROUP
                mm = pe.matmul(mb[g % 2][:, 0:w], qh[n % 2][0:C, j * P:(j + 1) * P], khl[0:C, key:key + w],
                               start=True, stop=(c < m))
                if c == m:
                    mm = pe.matmul(mb[g % 2][:, w - P:w], identb[:, :], future[:, :], start=False, stop=True)
                mm.then_inc(m_done, 1)

            def turn_max(n):
                pe.wait_ge(mc_done, n + 1)
                after(pe, l_ev, n - 1)
                for j in range(GT):
                    mm = pe.matmul(nb[0:CA, j * P:(j + 1) * P], mcol[:, j, :], ident[:, :], start=True, stop=True)
                mm.then_inc(mt_done, 1)

            def scores(n, kb):
                u, m = first_unit[n] + kb, n % QB
                off = max(0, kb - GT * m) * P
                if kb == 0:
                    pe.wait_ge(mrow, n + 1)
                after(pe, e_done, u - NSC + 1)
                key = n // QB * T + kb * P
                pe.matmul(sc[u % NSC][:, off:GROUP], khl[:, key:key + P], qh[n % 2][:, off:GROUP], start=True, stop=False)
                pe.matmul(sc[u % NSC][:, off:GROUP], kh1[:, key:key + P], qlm[n % 2][:, off:GROUP],
                          start=False, stop=True).then_inc(s_done, 1)

            def outputs(n, kb):
                u, m = first_unit[n] + kb, n % QB
                d = kb - GT * m
                off = max(0, d) * P
                low_there(pe, u)
                if kb == 0:
                    after(pe, o_ev, n)
                parts(pe, ob[0:CA, off:GROUP], [([a[:, n // QB * QB + kb // GT, kb % GT, :] for a in vap],
                                                 [a[:, off:GROUP] for a in prp[u % NP]])],
                      first=(kb == 0), last=(kb == units[n] - 1)).then_inc(pv_done, 1)

            def project(n, j):
                if n == 0 and j == 0:
                    pe.wait_ge(mo_ev, 2)
                if j == 0:
                    pe.wait_ge(o_ev, n + 1)
                    pe.wait_ge(mrow, min(n + 2, NG))
                    for i in range(GT):
                        for c in range(2):
                            mm = pe.matmul(nb[:, 2 * i:2 * i + 2], oT[c][:, i * P:(i + 1) * P], last[:, :],
                                           start=(c == 0), stop=(c == 1))
                    mm.then_inc(l_done, 1)
                after(pe, p_ev, GT * n + j)
                parts(pe, pj[:, :], [([a[0:C, j * P:(j + 1) * P] for a in oT], [a[:, :] for a in mop])]).then_inc(p_done, 1)

            pe.wait_ge(a_ready, 2)
            for v in range(units[0]):
                max_scores(0, v)
            turn_max(0)
            pe.wait_ge(sum_w, 1)
            pe.matmul(pj[0:C, :], wc[:, :], wz, start=True, stop=True).then_inc(mo_done, 1)
            for n in range(NG):
                for kb, ahead, behind in steps(n):
                    scores(n, kb)
                    for v in ahead:
                        max_scores(n + 1, v)
                    if kb >= LAG:
                        outputs(n, kb - LAG)
                    for j, term in behind:
                        if term == 0:
                            project(n - 1, j)
                for kb in range(units[n] - LAG, units[n]):
                    if kb == units[n] - LAG + 1 and n + 1 < NG:
                        turn_max(n + 1)
                    outputs(n, kb)
            for j in range(GT):
                project(NG - 1, j)

        @block.scalar
        def _(act):
            def highs_of(n, which):
                q, at = n % 2, slice(n * GROUP, (n + 1) * GROUP)
                if which == 0:
                    act.wait_ge(qkv_in[q], 80 * (n // 2) + 80)
                    if n >= 2:
                        act.wait_ge(pv_done, first_unit[n - 1])
                dst, src = ((khl[:, at], ka[q][:, :]), (kh1[0:C, at], ka[q][0:C, :]),
                            (vap[0][:, n, :, :], va[q][:, :, :]), (qh[q][:, :], qa[q][:, :]))[which]
                if which == 1:
                    act.copy(kh1[C:CA, at], ones[:, :])
                act.copy(dst, src).then_inc(highs, 1)

            def maximum_row(n):
                act.wait_ge(mt_done, n + 1)
                act.copy(qlm[n % 2][C:CA, :], nb[C:CA, :]).then_inc(mrow, 1)

            act.wait_ge(a_ready, 1)
            for which in range(4):
                highs_of(0, which)
            act.activation(w_all[:, 1, :], gap_all[:, :], ACT.Exp).then_inc(w_exp, 1)
            act.wait_ge(mo_done, 1)
            act.copy(mo, pj[0:C, :])
            act.copy(mop[0][:, :], pj[0:C, :]).then_inc(mo_ev, 1)
            maximum_row(0)
            for n in range(NG):
                m = n % QB
                for kb in range(units[n]):
                    for which in range(4):
                        if n + 1 < NG and kb == max(1, start[n] - 1 - (3 - which) * (start[n] - 1) // 4):
                            highs_of(n + 1, which)
                    u = first_unit[n] + kb
                    off = max(0, kb - GT * m) * P
                    act.wait_ge(s_done, u + 1)
                    low_there(act, u - NE)
                    after(act, pv_done, u - NP + 1)
                    for dst in (ex[u % NE], prp[u % NP][0]):
                        i = act.activation(dst[:, off:GROUP], sc[u % NSC][:, off:GROUP], ACT.Exp, scale=SCALE)
                    i.then_inc(e_done, 1)
                if n + 1 < NG:
                    maximum_row(n + 1)
                act.wait_ge(pv_done, first_unit[n + 1])
                after(act, p_done, GT * n)
                act.copy(oT[0][:, :], ob[0:CA, :]).then_inc(o_hi, 1)

        @block.vector
        def _(dve):
            links = [0]

            def link(i):
                links[0] += 1
                i.then_inc(chain, 1)
                dve.wait_ge(chain, links[0])

            def lows_of(n):
                q, at = n % 2, slice(n * GROUP, (n + 1) * GROUP)
                dve.wait_ge(highs, 4 * n + 4)
                dve.tensor_tensor(khl[C:P, at], ka[q][C:P, :], value(khl[C:P, at]), ALU.subtract)
                dve.tensor_tensor(vap[1][:, n, :, :], va[q][:, :, :], value(vap[0][:, n, :, :]), ALU.subtract)
                dve.tensor_tensor(qlm[q][0:C, :], qa[q][0:C, :], value(qh[q][0:C, :]), ALU.subtract).then_inc(lows, 1)

            def reduce_max(n, v):
                m, (j, c) = n % QB, divmod(v, n % QB + 1)
                g = first_unit[n] + v
                w = GROUP if c < m else P * (j + 1)
                dve.wait_ge(m_done, g + 1)
                dve.tensor_reduce(mx[:, j, c:c + 1], mb[g % 2][:, 0:w], AX.X, ALU.max).then_inc(m_red, 1)

            def negated_max(n):
                m = n % QB
                dve.wait_ge(m_red, first_unit[n + 1])
                after(dve, mt_done, n)
                dve.tensor_reduce(mcol[:, :, C], mx[:, :, 0:m + 1], AX.X, ALU.max, negate=True).then_inc(mc_done, 1)

            def probability_low(n, kb):
                if not by_pool[first_unit[n] + kb]:
                    make_low(dve, n, kb)

            def output_low(n):
                dve.wait_ge(o_hi, n + 1)
                dve.tensor_tensor(oT[1][:, :], ob[0:CA, :], value(oT[0][:, :]), ALU.subtract).then_inc(o_ev, 1)

            def combine(n, j, term):
                q, t = n % 2, GT * n + j
                if j == 0 and term == 0:
                    dve.wait_ge(l_done, n + 1)
                    link(dve.reciprocal(lr[:, :], nb[:, 0:2 * GT]))
                    dve.sem_inc(l_ev, 1)
                    dve.wait_ge(base_in[q], 16 * (n // 2) + 16)
                    dve.wait_ge(got_in[q], 128 * (n // 2) + 128)
                row = base[q][:, j, :]
                if term == 0:
                    dve.wait_ge(p_done, t + 1)
                    dve.scalar_tensor_tensor(out=row, in0=pj[:, :], scalar=lr[:, 2 * j:2 * j + 1], in1=row,
                                             op0=ALU.mult, op1=ALU.add).then_inc(p_ev, 1)
                    return
                dve.wait_ge(p_ev if term == 1 else w1_ev, t + 1)
                dve.scalar_tensor_tensor(out=row, in0=got[q][:, term - 1, j, :], scalar=w_all[:, term - 1, t:t + 1],
                                         in1=row, op0=ALU.mult, op1=ALU.add).then_inc(w1_ev if term == 1 else w2_ev, 1)

            dve.memset(mcol[:, :, :], 0.0)
            dve.memset(last_f[0:C, :], 0.0)
            dve.memset(last_f[C:CA, :], 1.0)
            dve.memset(ones[:, :], 1.0).then_inc(a_ready, 1)
            dve.wait_ge(a_ready, 1)
            dve.tensor_copy(last[:, :], last_f[:, :])
            dve.tensor_copy(identb[:, :], ident[:, :])
            lows_of(0)
            dve.wait_ge(const_in, CONSTS)
            dve.tensor_copy(future[:, :], tri[:, 1, :]).then_inc(a_ready, 1)
            dve.tensor_tensor(wz, wz, wo, ALU.add).then_inc(sum_w, 1)
            for v in range(units[0]):
                reduce_max(0, v)
            negated_max(0)
            dve.wait_ge(mo_ev, 1)
            dve.tensor_tensor(mop[1][:, :], mo, value(mop[0][:, :]), ALU.subtract).then_inc(mo_ev, 1)
            dve.wait_ge(w_exp, 1)
            link(dve.tensor_scalar(den[:, :], w_all[:, 1, :], 1.0, None, ALU.add))
            link(dve.reciprocal(w_all[:, 0, :], den[:, :]))
            link(dve.tensor_tensor(w_all[:, 1, :], w_all[:, 1, :], w_all[:, 0, :], ALU.mult))
            for n in range(NG):
                for kb, ahead, behind in steps(n):
                    if kb:
                        probability_low(n, kb - 1)
                    if kb == max(1, start[n] - 1) and n + 1 < NG:
                        lows_of(n + 1)
                    for v in ahead:
                        reduce_max(n + 1, v)
                    if kb == units[n] - 3 and n + 1 < NG:
                        negated_max(n + 1)
                    for j, term in behind:
                        combine(n - 1, j, term)
                probability_low(n, units[n] - 1)
                output_low(n)
            for j in range(GT):
                for term in range(3):
                    combine(NG - 1, j, term)

        @block.gpsimd
        def _(pool):
            def gather(n):
                q = n % 2
                after(pool, w2_ev, GT * (n - 1))
                for j in range(GT):
                    for c in range(2):
                        pool.indirect_dma_start(got[q][:, c, j, :], None, rows_out[:, :],
                                                bass.IndirectOffsetOnAxis(ap=slots_all[:, GT * n + j, c:c + 1], axis=0)
                                                ).then_inc(got_in[q], 16)

            gather(0)
            for n in range(NG):
                for kb in range(units[n]):
                    if by_pool[first_unit[n] + kb]:
                        make_low(pool, n, kb)
                for d in range(GT):
                    u = first_unit[n] + GT * (n % QB) + d
                    pool.wait_ge(e_done, u + 1)
                    for buf in (ex[u % NE], prp[u % NP][0]):
                        part = buf[:, d * P:(d + 1) * P]
                        i = pool.affine_select(out=part, in_=part, pattern=[[1, P]], compare_op=ALU.is_ge, fill=0.0,
                                               base=0, channel_multiplier=-1)
                    i.then_inc(sel_done, 1)
                if n == 0:
                    pool.wait_ge(mo_ev, 2)
                if n + 1 < NG:
                    gather(n + 1)


def rope_tables():
    f = np.float32
    inv = f(1.0) / np.power(f(10000.0), np.arange(0, C, 2, dtype=f) / f(C)).astype(f)
    angle = np.arange(T, dtype=f)[:, None] * inv[None, :]
    cos, sin = np.cos(angle).astype(f), np.sin(angle).astype(f)
    cos = np.concatenate([cos, cos], axis=1).T
    sin = np.concatenate([-sin, sin], axis=1).T
    one = np.stack([np.concatenate([cos, cos]), np.concatenate([sin, sin])], axis=1)
    seq = one.reshape(2 * C, 2, QB, GROUP).transpose(2, 0, 1, 3)
    return np.ascontiguousarray(np.concatenate([seq] * B))


def shape_tables():
    f = np.float32
    i = np.arange(P)
    tri = np.stack([(i[:, None] < i[None, :]).astype(f), np.where(i[None, :] > i[:, None], f(NEG), f(0)).astype(f)])
    rev = np.tile((E - np.arange(E)).astype(f), (P, GT, 1))
    start = np.tile((np.arange(E) * REGION).astype(f), (P, 1, 1))
    upto = (np.arange(E)[None, :] <= np.arange(E)[:, None]).astype(f)
    upto = np.tile(upto, (P, 1, 1))
    token = np.arange(N, dtype=np.int32).reshape(NG * GT, P).T
    tile_p = (np.arange(P)[:, None] + np.array([0, NRT // 2])[None, :]).astype(f)
    return np.eye(P, dtype=f), tri, np.concatenate([rev, start], axis=1), upto, token, tile_p


def kernel(**inputs):
    import concourse.bacc as bacc
    from concourse.bass_utils import run_bass_kernel_spmd

    a = {name: np.asarray(v) for name, v in inputs.items()}
    wq, wkv = a["L0_attn_W_q_comp"], a["L0_attn_W_kv_comp"]
    wqT, wkT, wvT = wq.T, wkv[:C].T, wkv[C:].T
    swap = lambda w: np.concatenate([w[:, C // 2:], w[:, :C // 2]], axis=1)
    ident, tri, route, upto, token, tile_p = shape_tables()
    arrays = {
        "x": a["L0_attn_x"].reshape(N, D), "w_kv": a["L0_attn_W_to_kv"], "w_compT": a["L0_attn_W_compress"].T,
        "gamma": a["L0_attn_ln_gamma"][:, None], "beta": a["L0_attn_ln_beta"][:, None],
        "w_qk": np.concatenate([wqT, wkT], axis=1), "w_qk_swap": np.concatenate([swap(wqT), swap(wkT)], axis=1),
        "w_vT": wvT, "w_c2l": a["L0_attn_W_comp2lat"], "w_outT": a["L0_attn_W_out_res"].T, "b_out": a["L0_attn_b_out_res"],
        "routerT": a["L0_ffn_router_w"].T, "gate_w": a["L0_ffn_gate_w"], "up_w": a["L0_ffn_up_w"],
        "down_w": a["L0_ffn_down_w"], "sh_gate": a["L0_ffn_shared_gate_w"], "sh_up": a["L0_ffn_shared_up_w"],
        "sh_down": a["L0_ffn_shared_down_w"], "rope": rope_tables(), "ident_in": ident, "tri_in": tri,
        "route_in": route, "upto_in": upto, "token_in": token, "tile_p_in": tile_p,
    }
    arrays = {name: np.ascontiguousarray(v) for name, v in arrays.items()}
    nc = bacc.Bacc("TRN2", target_bir_lowering=False, num_devices=1)
    args = {name: nc.dram_tensor(name, v.shape, mybir.dt.from_np(v.dtype), kind="ExternalInput").ap()
            for name, v in arrays.items()}
    out = nc.dram_tensor("out", (B, T, D), F32, kind="ExternalOutput").ap()
    build(nc, **args, out=out)
    r = run_bass_kernel_spmd(nc, [arrays], core_ids=[0])
    return r.results[0]["out"]
```
